# Optimizing a Trainium2 kernel written in Bass

```python
import numpy as np
import jax
import jax.numpy as jnp

def _softmax(x, axis=-1):
    return jax.nn.softmax(x, axis=axis)

def _gelu(x):
    return jax.nn.gelu(x, approximate=True)

def _silu(x):
    return jax.nn.silu(x)

def _sigmoid(x):
    return jax.nn.sigmoid(x)

def _layernorm(x, axis=-1, eps=1e-05):
    m = jnp.mean(x, axis=axis, keepdims=True)
    v = jnp.var(x, axis=axis, keepdims=True)
    return (x - m) / jnp.sqrt(v + eps)

def _scatter_add(tgt, idx, src, axis=0):
    return tgt.at[idx].add(src)

def _segment_sum(src, seg, n):
    return jax.ops.segment_sum(src, seg, n)
kernel_name = 'mk_hybrid_d1_jaxref_r4_f2a63e'

def setup_inputs(seed: int=0):
    np.random.seed(seed)
    _w = jnp.asarray

    def _L0_attn_a_setup():
        import jax, jax.numpy as jnp
        import numpy as np
        DIM = 256
        NH = 16
        HD = DIM // NH
        DROPE = 16
        MAXSEQ = 512
        LAT = 64
        BATCH = 2
        SEQ = 512

        def _rope_freqs(max_seq, head_dim):
            inv = 1.0 / 10000.0 ** (jnp.arange(0, head_dim, 2, dtype=jnp.float32) / head_dim)
            ang = jnp.arange(max_seq, dtype=jnp.float32)[:, None] * inv[None, :]
            return (jnp.cos(ang), jnp.sin(ang))

        def _apply_decoupled_rope(x, cosf, sinf, d_rope):
            b, d1, d2, hd = x.shape
            half = d_rope // 2
            xr = x[..., :d_rope].astype(jnp.float32).reshape(b, d1, d2, half, 2)
            xa, xb = (xr[..., 0], xr[..., 1])
            c = cosf[:d1, :half][None, :, None, :]
            s = sinf[:d1, :half][None, :, None, :]
            rot = jnp.stack([xa * c - xb * s, xa * s + xb * c], axis=-1)
            rot = rot.reshape(b, d1, d2, d_rope)
            return jnp.concatenate([rot, x[..., d_rope:]], axis=-1)
        key = jax.random.key(seed)
        ks = jax.random.split(key, 8)

        def w(k, o, i):
            return jax.random.normal(k, (o, i), jnp.float32) / np.sqrt(i).astype(np.float32)
        return {'x': jax.random.normal(ks[0], (BATCH, SEQ, DIM), jnp.float32), 'wq': w(ks[1], NH * HD, DIM), 'wk_a': w(ks[2], LAT, DIM), 'wk_b': w(ks[3], NH * HD, LAT), 'wv_a': w(ks[4], LAT, DIM), 'wv_b': w(ks[5], NH * HD, LAT), 'wo': w(ks[6], DIM, NH * HD)}
    _L0_attn_a_in = _L0_attn_a_setup()

    def _L0_attn_b_setup():
        import jax, jax.numpy as jnp
        import numpy as np
        D_MODEL = 256
        D_STATE = 16
        D_CONV = 4
        EXPAND = 2
        D_INNER = D_MODEL * EXPAND
        BATCH = 4
        SEQLEN = 1024

        def _selective_scan(xc, delta, A, B, C, D):
            batch, seqlen, d_inner = xc.shape
            d_state = A.shape[1]

            def step(h, inp):
                x_t, dt, B_t, C_t = inp
                A_disc = jnp.exp(dt[:, :, None] * A[None])
                h = A_disc * h + dt[:, :, None] * B_t[:, None, :] * x_t[:, :, None]
                y_t = jnp.einsum('bds,bs->bd', h, C_t) + D[None, :] * x_t
                return (h, y_t)
            h0 = jnp.zeros((batch, d_inner, d_state), xc.dtype)
            xs = (jnp.swapaxes(xc, 0, 1), jnp.swapaxes(delta, 0, 1), jnp.swapaxes(B, 0, 1), jnp.swapaxes(C, 0, 1))
            _, ys = jax.lax.scan(step, h0, xs)
            return jnp.swapaxes(ys, 0, 1)
        key = jax.random.key(seed)
        ks = jax.random.split(key, 10)
        s = 1.0 / np.sqrt(D_MODEL)
        si = 1.0 / np.sqrt(D_INNER)
        return {'x': jax.random.normal(ks[0], (BATCH, SEQLEN, D_MODEL), jnp.float32), 'x_proj_w': jax.random.normal(ks[1], (D_INNER, D_MODEL), jnp.float32) * s, 'dt_proj_w': jax.random.normal(ks[2], (D_INNER, D_MODEL), jnp.float32) * s, 'dt_proj_b': jax.random.normal(ks[3], (D_INNER,), jnp.float32) * 0.1, 'A_log': jax.random.normal(ks[4], (D_INNER, D_STATE), jnp.float32), 'D': jnp.ones((D_INNER,), jnp.float32), 'B_proj_w': jax.random.normal(ks[5], (D_STATE, D_MODEL), jnp.float32) * s, 'C_proj_w': jax.random.normal(ks[6], (D_STATE, D_MODEL), jnp.float32) * s, 'conv_w': jax.random.normal(ks[7], (D_INNER, 1, D_CONV), jnp.float32) * 0.5, 'conv_b': jax.random.normal(ks[8], (D_INNER,), jnp.float32) * 0.1, 'out_proj_w': jax.random.normal(ks[9], (D_MODEL, D_INNER), jnp.float32) * si}
    _L0_attn_b_in = _L0_attn_b_setup()

    def _L0_ffn_setup():
        import jax, jax.numpy as jnp
        import numpy as np
        D_MODEL = 256
        M = 64
        INNER = 16
        key = jax.random.key(seed)
        ks = jax.random.split(key, 9)

        def init(k, shape, fan_in):
            bound = 1.0 / np.sqrt(fan_in)
            return jax.random.uniform(k, shape, jnp.float32, -bound, bound)
        x = jax.random.normal(ks[0], (16, 1024, D_MODEL), dtype=jnp.float32)
        Win = init(ks[1], (D_MODEL, M), D_MODEL)
        bin_ = init(ks[2], (M,), D_MODEL)
        W1 = init(ks[3], (M, INNER), 1)
        b1 = init(ks[4], (M, INNER), 1)
        W2 = init(ks[5], (M, INNER), INNER)
        b2 = init(ks[6], (M,), INNER)
        Wout = init(ks[7], (M, D_MODEL), M)
        bout = init(ks[8], (D_MODEL,), M)
        return {'x': x, 'Win': Win, 'bin_': bin_, 'W1': W1, 'b1': b1, 'W2': W2, 'b2': b2, 'Wout': Wout, 'bout': bout}
    _L0_ffn_in = _L0_ffn_setup()
    _d = {'L0_attn_a_x': _L0_attn_a_in['x'], 'L0_attn_a_wq': _L0_attn_a_in['wq'], 'L0_attn_a_wk_a': _L0_attn_a_in['wk_a'], 'L0_attn_a_wk_b': _L0_attn_a_in['wk_b'], 'L0_attn_a_wv_a': _L0_attn_a_in['wv_a'], 'L0_attn_a_wv_b': _L0_attn_a_in['wv_b'], 'L0_attn_a_wo': _L0_attn_a_in['wo'], 'L0_attn_b_x_proj_w': _L0_attn_b_in['x_proj_w'], 'L0_attn_b_dt_proj_w': _L0_attn_b_in['dt_proj_w'], 'L0_attn_b_dt_proj_b': _L0_attn_b_in['dt_proj_b'], 'L0_attn_b_A_log': _L0_attn_b_in['A_log'], 'L0_attn_b_D': _L0_attn_b_in['D'], 'L0_attn_b_B_proj_w': _L0_attn_b_in['B_proj_w'], 'L0_attn_b_C_proj_w': _L0_attn_b_in['C_proj_w'], 'L0_attn_b_conv_w': _L0_attn_b_in['conv_w'], 'L0_attn_b_conv_b': _L0_attn_b_in['conv_b'], 'L0_attn_b_out_proj_w': _L0_attn_b_in['out_proj_w'], 'L0_ffn_Win': _L0_ffn_in['Win'], 'L0_ffn_bin_': _L0_ffn_in['bin_'], 'L0_ffn_W1': _L0_ffn_in['W1'], 'L0_ffn_b1': _L0_ffn_in['b1'], 'L0_ffn_W2': _L0_ffn_in['W2'], 'L0_ffn_b2': _L0_ffn_in['b2'], 'L0_ffn_Wout': _L0_ffn_in['Wout'], 'L0_ffn_bout': _L0_ffn_in['bout']}
    _x0 = _d['L0_attn_a_x']
    _d['L0_attn_a_x'] = jax.random.normal(jax.random.fold_in(jax.random.key(seed), 1), (8, 1024, 256), dtype=_x0.dtype)
    del _x0
    return _d

def reference(L0_attn_a_x, L0_attn_a_wq, L0_attn_a_wk_a, L0_attn_a_wk_b, L0_attn_a_wv_a, L0_attn_a_wv_b, L0_attn_a_wo, L0_attn_b_x_proj_w, L0_attn_b_dt_proj_w, L0_attn_b_dt_proj_b, L0_attn_b_A_log, L0_attn_b_D, L0_attn_b_B_proj_w, L0_attn_b_C_proj_w, L0_attn_b_conv_w, L0_attn_b_conv_b, L0_attn_b_out_proj_w, L0_ffn_Win, L0_ffn_bin_, L0_ffn_W1, L0_ffn_b1, L0_ffn_W2, L0_ffn_b2, L0_ffn_Wout, L0_ffn_bout):

    def _L0_attn_a_ref(x, wq, wk_a, wk_b, wv_a, wv_b, wo):
        import jax, jax.numpy as jnp
        import numpy as np
        DIM = 256
        NH = 16
        HD = DIM // NH
        DROPE = 16
        MAXSEQ = 512
        LAT = 64
        BATCH = 2
        SEQ = 512

        def _rope_freqs(max_seq, head_dim):
            inv = 1.0 / 10000.0 ** (jnp.arange(0, head_dim, 2, dtype=jnp.float32) / head_dim)
            ang = jnp.arange(max_seq, dtype=jnp.float32)[:, None] * inv[None, :]
            return (jnp.cos(ang), jnp.sin(ang))

        def _apply_decoupled_rope(x, cosf, sinf, d_rope):
            b, d1, d2, hd = x.shape
            half = d_rope // 2
            xr = x[..., :d_rope].astype(jnp.float32).reshape(b, d1, d2, half, 2)
            xa, xb = (xr[..., 0], xr[..., 1])
            c = cosf[:d1, :half][None, :, None, :]
            s = sinf[:d1, :half][None, :, None, :]
            rot = jnp.stack([xa * c - xb * s, xa * s + xb * c], axis=-1)
            rot = rot.reshape(b, d1, d2, d_rope)
            return jnp.concatenate([rot, x[..., d_rope:]], axis=-1)
        b, s, _ = x.shape
        q = (x @ wq.T).reshape(b, s, NH, HD).transpose(0, 2, 1, 3)
        k = (x @ wk_a.T @ wk_b.T).reshape(b, s, NH, HD).transpose(0, 2, 1, 3)
        v = (x @ wv_a.T @ wv_b.T).reshape(b, s, NH, HD).transpose(0, 2, 1, 3)
        cosf, sinf = _rope_freqs(MAXSEQ, HD)
        q = _apply_decoupled_rope(q, cosf, sinf, DROPE)
        k = _apply_decoupled_rope(k, cosf, sinf, DROPE)
        scores = jnp.einsum('bhqd,bhkd->bhqk', q, k) / np.float32(np.sqrt(HD))
        attn = jax.nn.softmax(scores, axis=-1)
        out = jnp.einsum('bhqk,bhkd->bhqd', attn, v)
        out = out.transpose(0, 2, 1, 3).reshape(b, s, NH * HD)
        return out @ wo.T

    def _L0_attn_b_ref(x, x_proj_w, dt_proj_w, dt_proj_b, A_log, D, B_proj_w, C_proj_w, conv_w, conv_b, out_proj_w):
        import jax, jax.numpy as jnp
        import numpy as np
        D_MODEL = 256
        D_STATE = 16
        D_CONV = 4
        EXPAND = 2
        D_INNER = D_MODEL * EXPAND
        BATCH = 4
        SEQLEN = 1024

        def _selective_scan(xc, delta, A, B, C, D):
            batch, seqlen, d_inner = xc.shape
            d_state = A.shape[1]

            def step(h, inp):
                x_t, dt, B_t, C_t = inp
                A_disc = jnp.exp(dt[:, :, None] * A[None])
                h = A_disc * h + dt[:, :, None] * B_t[:, None, :] * x_t[:, :, None]
                y_t = jnp.einsum('bds,bs->bd', h, C_t) + D[None, :] * x_t
                return (h, y_t)
            h0 = jnp.zeros((batch, d_inner, d_state), xc.dtype)
            xs = (jnp.swapaxes(xc, 0, 1), jnp.swapaxes(delta, 0, 1), jnp.swapaxes(B, 0, 1), jnp.swapaxes(C, 0, 1))
            _, ys = jax.lax.scan(step, h0, xs)
            return jnp.swapaxes(ys, 0, 1)
        seqlen = x.shape[1]
        x_inner = x @ x_proj_w.T
        xc = jax.lax.conv_general_dilated(jnp.swapaxes(x_inner, 1, 2), conv_w, window_strides=(1,), padding=[(D_CONV - 1, 0)], dimension_numbers=('NCH', 'OIH', 'NCH'), feature_group_count=D_INNER)
        xc = jnp.swapaxes(xc + conv_b[None, :, None], 1, 2)
        xc = jax.nn.silu(xc)
        B = x @ B_proj_w.T
        C = x @ C_proj_w.T
        delta = jax.nn.softplus(x @ dt_proj_w.T + dt_proj_b)
        A = -jnp.exp(A_log.astype(jnp.float32))
        y = _selective_scan(xc, delta, A, B, C, D)
        return y @ out_proj_w.T

    def _L0_ffn_ref(x, Win, bin_, W1, b1, W2, b2, Wout, bout):
        import jax, jax.numpy as jnp
        import numpy as np
        D_MODEL = 256
        M = 64
        INNER = 16
        s = jnp.einsum('btd,dm->btm', x, Win) + bin_
        h = jax.nn.relu(s[..., None] * W1 + b1)
        g = jnp.einsum('btmh,mh->btm', h, W2) + b2
        out = jnp.einsum('btm,md->btd', g, Wout) + bout
        return out
    x = L0_attn_a_x
    x = x + _L0_attn_a_ref(_layernorm(x, axis=-1), L0_attn_a_wq, L0_attn_a_wk_a, L0_attn_a_wk_b, L0_attn_a_wv_a, L0_attn_a_wv_b, L0_attn_a_wo)
    x = x + _L0_ffn_ref(_layernorm(x, axis=-1), L0_ffn_Win, L0_ffn_bin_, L0_ffn_W1, L0_ffn_b1, L0_ffn_W2, L0_ffn_b2, L0_ffn_Wout, L0_ffn_bout)
    x = x + _L0_attn_b_ref(_layernorm(x, axis=-1), L0_attn_b_x_proj_w, L0_attn_b_dt_proj_w, L0_attn_b_dt_proj_b, L0_attn_b_A_log, L0_attn_b_D, L0_attn_b_B_proj_w, L0_attn_b_C_proj_w, L0_attn_b_conv_w, L0_attn_b_conv_b, L0_attn_b_out_proj_w)
    x = x + _L0_ffn_ref(_layernorm(x, axis=-1), L0_ffn_Win, L0_ffn_bin_, L0_ffn_W1, L0_ffn_b1, L0_ffn_W2, L0_ffn_b2, L0_ffn_Wout, L0_ffn_bout)
    return x

_drawn_inputs = setup_inputs


def setup_inputs(seed=0):
    import zlib

    import numpy as np

    out = dict(_drawn_inputs(seed))
    spreads = {'L0_attn_b_D': (1.0, 0.2)}
    factors = {'L0_ffn_bin_': 7.136}
    for name, (base, spread) in spreads.items():
        noise = np.random.default_rng([zlib.crc32(name.encode()), seed]).standard_normal(out[name].shape)
        drawn = base * np.exp(spread * noise) if base else spread * noise
        out[name] = jnp.asarray(drawn.astype(out[name].dtype))
    for name, factor in factors.items():
        out[name] = (out[name] * factor).astype(out[name].dtype)
    return out
```

```python
import numpy as np
import concourse.bass as bass
from concourse import mybir
from contextlib import ExitStack

F32 = mybir.dt.float32
BF16 = mybir.dt.bfloat16
ALU = mybir.AluOpType
ACT = mybir.ActivationFunctionType
AX = mybir.AxisListType

P = 128
NB, T, D = 8, 1024, 256
NH, HD = 16, 16
LAT = 64
DI, NS, TAPS = 512, 16, 4
M, INNER = 64, 16
EPS = 1e-5

TT = T // P
CB = D // P
DB = DI // P
HALF = 512
PAIR = 2 * HALF
NG, GH = 4, 4
SLOTS = 6
ROWS = SLOTS * HD
VW = 32
Q_PARTS = (0, 0, 0, 1, 1, 2)
K_PARTS = (0, 1, 2, 0, 1, 0)


def each_batch(eng, unroll, body):
    with eng.Fori(0, NB // unroll - 1) as i:
        for u in range(unroll):
            body(i * unroll + u, u, i, False)
    for u in range(unroll):
        body(NB - unroll + u, u, NB // unroll - 1, u == unroll - 1)


class Stage:

    def __init__(self, nc, ctx, name):
        self.nc, self.ctx, self.name = nc, ctx, name
        self.sems = []
        ctx.callback(self.end)

    def end(self):
        self.nc.clear_and_free_semaphores(self.sems)
        self.nc.all_engine_barrier()

    def sb(self, name, shape, dt=F32):
        return self.ctx.enter_context(self.nc.sbuf_tensor(f"{self.name}_{name}", shape, dt))

    def ps(self, name, shape):
        return self.ctx.enter_context(self.nc.psum_tensor(f"{self.name}_{name}", shape, F32))

    def sem(self, name):
        self.sems.append(self.nc.alloc_semaphore(name=f"{self.name}_{name}"))
        return self.sems[-1]


def stand(eng, passed):
    eng.sem_inc(passed, 1)


def make_identity(nc, pool, ident, zeroed, ready):
    nc.gpsimd.memset(ident[:, :], 0.0).then_inc(zeroed, 1)
    pool.wait_ge(zeroed, 1)
    nc.gpsimd.affine_select(out=ident[:, :], in_=ident[:, :], compare_op=ALU.not_equal, fill=1.0,
                            base=0, pattern=[[-1, P]], channel_multiplier=1).then_inc(ready, 1)


class Norm:

    def __init__(self, st):
        self.stats = st.sb("stats", [P, TT, 6])
        self.mv = [st.sb(f"mean_var{u}", [P, TT, 2]) for u in range(2)]
        self.var_eps = st.sb("var_eps", [P, TT])
        self.neg_mean = st.sb("neg_mean", [P, TT])
        self.rstd = st.sb("rstd", [P, TT])
        self.exponent = st.sb("exponent", [P, TT])
        self.xn = [st.sb(f"xn{u}", [P, TT, D]) for u in range(2)]
        self.stats_done = st.sem("stats_done")
        self.mv_ready = st.sem("mean_var_ready")
        self.rstd_steps = st.sem("rstd_steps")
        self.xn_ready = st.sem("xn_ready")
        self.transposed = st.sem("transposed")
        self.exponent_set = st.sem("exponent_set")
        self.pool_passed = st.sem("pool_passed")
        self.dve_passed = st.sem("dve_passed")

    def setup(self, nc, pool):
        pool.sem_inc(self.transposed, 2 * CB)
        pool.sem_inc(self.mv_ready, 1)
        pool.sem_inc(self.xn_ready, 1)
        nc.gpsimd.memset(self.exponent[:, :], -0.5).then_inc(self.exponent_set, 1)

    def vector(self, nc, dve, b, u, x):
        dve.wait_ge(self.mv_ready, b + 1)
        for t in range(TT):
            last = nc.vector.bn_stats(self.stats[:, t, :], x[:, t, :])
        last.then_inc(self.stats_done, 1)
        dve.wait_ge(self.stats_done, b + 1)
        dve.wait_ge(self.transposed, CB * (b + 1))
        stand(dve, self.dve_passed)
        for t in range(TT):
            last = nc.vector.bn_aggr(self.mv[u][:, t, :], self.stats[:, t, :])
        last.then_inc(self.mv_ready, 1)

    def gpsimd(self, nc, pool, b, u, x):
        mv = self.mv[u]
        pool.wait_ge(self.exponent_set, 1)
        pool.wait_ge(self.xn_ready, b + 1)
        pool.wait_ge(self.mv_ready, b + 2)
        stand(pool, self.pool_passed)
        nc.gpsimd.tensor_scalar(self.var_eps[:, :], mv[:, :, 1], 1.0, EPS, ALU.mult, ALU.add)\
            .then_inc(self.rstd_steps, 1)
        nc.gpsimd.tensor_scalar(self.neg_mean[:, :], mv[:, :, 0], -1.0, 0.0, ALU.mult, ALU.add)\
            .then_inc(self.rstd_steps, 1)
        pool.wait_ge(self.rstd_steps, 3 * b + 2)
        nc.gpsimd.tensor_tensor(self.rstd[:, :], self.var_eps[:, :], self.exponent[:, :], ALU.pow)\
            .then_inc(self.rstd_steps, 1)
        pool.wait_ge(self.rstd_steps, 3 * b + 3)
        pool.wait_ge(self.transposed, CB * (b + 1))
        stand(pool, self.pool_passed)
        for t in range(TT):
            last = nc.gpsimd.tensor_scalar(self.xn[u][:, t, :], x[:, t, :], self.neg_mean[:, t:t + 1],
                                           self.rstd[:, t:t + 1], ALU.add, ALU.mult)
        last.then_inc(self.xn_ready, 1)

    def tensor(self, nc, pe, b, u, ident, banks, free):
        pe.wait_ge(self.xn_ready, b + 2)
        for c in range(CB):
            free(c)
            for t in range(TT):
                last = nc.tensor.transpose(banks[c][:, t * P:(t + 1) * P],
                                           self.xn[u][:, t, c * P:(c + 1) * P], ident[:, :])
            last.then_inc(self.transposed, 1)

    def wait_transposed(self, eng, b, c):
        eng.wait_ge(self.transposed, 2 * CB + CB * b + c + 1)


def project_qkv(nc, x, wq, wk_b, wkv_aT, wv_bT, turnT, qk_parts, v_ones):
    T0, T1, LATENT, Q0, Q1, K0, K1, V0, V1 = range(9)
    JOBS, PRODUCTS = 9, 7
    PAIR_OF = {T0: 0, T1: 1, LATENT: 2, Q0: 3, Q1: 0, K0: 1, K1: 2, V0: 3, V1: 1}
    BEFORE = {T0: Q1, T1: V1, LATENT: K1, Q0: V0, Q1: T0, K0: T1, K1: LATENT, V0: Q0, V1: K0}
    QK = (Q0, Q1, K0, K1)

    with ExitStack() as ctx:
        st = Stage(nc, ctx, "qkv")
        xt = [st.sb(f"x{u}", [P, TT, D]) for u in range(2)]
        norm = Norm(st)
        xnT = st.sb("xnT", [P, CB, T])
        latent = st.sb("latent", [P, T])
        parts = [st.sb(f"parts{u}", [P, len(QK), 3, T], BF16) for u in range(2)]
        rest = st.sb("rest", [P, len(QK), T])
        v = [st.sb(f"v{u}", [P, TT, NH, VW]) for u in range(2)]
        ident = st.sb("ident", [P, P])
        wq_n = st.sb("wq", [P, CB, D])
        wkb_n = st.sb("wk_b", [P, CB, LAT])
        turn = st.sb("turn", [P, CB, P])
        wqT = st.sb("wqT", [P, CB, D])
        wkbT = st.sb("wk_bT", [P, D])
        wvbT = st.sb("wv_bT", [P, D])
        wkvaT = st.sb("wkv_aT", [P, CB, P])
        ps = [st.ps(f"p{i}", [P, PAIR]) for i in range(4)]

        weights = st.sem("weights")
        x_loaded = [st.sem(f"x_loaded{u}") for u in range(2)]
        zeroed = st.sem("zeroed")
        ident_ready = st.sem("ident_ready")
        pads_ready = st.sem("pads_ready")
        ones_ready = st.sem("ones_ready")
        turned = st.sem("turned")
        turned_copied = st.sem("turned_copied")
        product = st.sem("product")
        act_read = st.sem("act_read")
        rest_ready = st.sem("rest_ready")
        mid_ready = st.sem("mid_ready")
        parts_ready = st.sem("parts_ready")
        parts_stored = [st.sem(f"parts_stored{u}") for u in range(2)]
        v_stored = [st.sem(f"v_stored{u}") for u in range(2)]
        pool_passed = norm.pool_passed
        block = ctx.enter_context(nc.Block())
        WEIGHTS = 16 * 5

        @block.sync
        def _(sp):
            sp.dma_start(xt[0][:, :, :], x[0].rearrange("(t p) c -> p t c", p=P)).then_inc(x_loaded[0], 16)
            sp.dma_start(wq_n[:, :, :], wq.rearrange("(a p) c -> p a c", p=P)).then_inc(weights, 16)
            sp.dma_start(wkb_n[:, :, :], wk_b.rearrange("(a p) c -> p a c", p=P)).then_inc(weights, 16)
            sp.dma_start(turn[:, :, :], turnT.rearrange("a p c -> p a c")).then_inc(weights, 16)
            sp.dma_start(wkvaT[:, :, :], wkv_aT.rearrange("(a p) c -> p a c", p=P)).then_inc(weights, 16)
            sp.wait_ge(pads_ready, 1)
            sp.dma_start(wvbT[LAT:P, :], wv_bT).then_inc(weights, 16)
            sp.dma_start(xt[1][:, :, :], x[1].rearrange("(t p) c -> p t c", p=P)).then_inc(x_loaded[1], 16)

            def batch(b, u, i, last):
                for k in range(len(QK)):
                    sp.wait_ge(parts_ready, 4 + 4 * b + k + 1)
                    sp.dma_start(qk_parts[b, k // 2, :, (k % 2) * P:(k % 2 + 1) * P, :].rearrange("a p t -> p a t"),
                                 parts[u][:, k, :, :]).then_inc(parts_stored[u], 16)
                sp.wait_ge(act_read, JOBS + JOBS * b + V1 + 1)
                sp.dma_start(v_ones[b], v[u][:, :, :, :].rearrange("p t h w -> p (t h w)")).then_inc(v_stored[u], 16)

            def load(b, u):
                sp.wait_ge(norm.xn_ready, b + 2)
                sp.dma_start(xt[u][:, :, :], x[b + 2].rearrange("(t p) c -> p t c", p=P)).then_inc(x_loaded[u], 16)

            with sp.Fori(0, NB // 2 - 1) as i:
                for u in range(2):
                    batch(2 * i + u, u, i, False)
                    load(2 * i + u, u)
            for u in range(2):
                batch(NB - 2 + u, u, NB // 2 - 1, True)
            for u in range(2):
                sp.wait_ge(parts_stored[u], 64 * (NB // 2 + 1))
                sp.wait_ge(v_stored[u], 16 * (NB // 2 + 1))

        @block.gpsimd
        def _(pool):
            nc.gpsimd.memset(wvbT[:, :], 0.0)
            nc.gpsimd.memset(wkbT[:, :], 0.0).then_inc(pads_ready, 1)
            pool.sem_inc(parts_ready, 4)
            norm.setup(nc, pool)
            make_identity(nc, pool, ident, zeroed, ident_ready)
            pool.wait_ge(x_loaded[0], 16)
            norm.gpsimd(nc, pool, 0, 0, xt[0])

            def batch(b, u, i, last):
                if not last:
                    pool.wait_ge(x_loaded[1 - u], 16 * (i + 1 + u))
                    norm.gpsimd(nc, pool, b + 1, 1 - u, xt[1 - u])
                for k in range(len(QK)):
                    pool.wait_ge(rest_ready, 4 + 4 * b + k + 1)
                    pool.wait_ge(parts_stored[u], 64 * (i + 1))
                    stand(pool, pool_passed)
                    nc.gpsimd.tensor_scalar(parts[u][:, k, 1, :], rest[:, k, :], 1.0, 0.0, ALU.mult, ALU.add)\
                        .then_inc(mid_ready, 1)
                    pool.wait_ge(mid_ready, 4 * b + k + 1)
                    nc.gpsimd.tensor_tensor(parts[u][:, k, 2, :], rest[:, k, :], parts[u][:, k, 1, :], ALU.subtract)\
                        .then_inc(parts_ready, 1)

            each_batch(pool, 2, batch)

        @block.vector
        def _(dve):
            dve.sem_inc(rest_ready, 4)
            for u in range(2):
                last = nc.vector.memset(v[u][:, :, :, HD:VW], 1.0)
            last.then_inc(ones_ready, 1)
            dve.wait_ge(x_loaded[0], 16)
            norm.vector(nc, dve, 0, 0, xt[0])

            def batch(b, u, i, last):
                if not last:
                    dve.wait_ge(x_loaded[1 - u], 16 * (i + 1 + u))
                    norm.vector(nc, dve, b + 1, 1 - u, xt[1 - u])
                for k, job in enumerate(QK):
                    dve.wait_ge(act_read, JOBS + JOBS * b + job + 1)
                    dve.wait_ge(parts_ready, 4 * b + k + 1 + 0)
                    nc.vector.tensor_tensor(rest[:, k, :], ps[PAIR_OF[job]][:, :], parts[u][:, k, 0, :], ALU.subtract)\
                        .then_inc(rest_ready, 1)

            each_batch(dve, 2, batch)

        @block.scalar
        def _(act):
            act.sem_inc(act_read, JOBS)
            for u in range(2):
                act.sem_inc(parts_stored[u], 64)
                act.sem_inc(v_stored[u], 16)
            act.wait_ge(pads_ready, 1)
            for c in range(CB):
                act.wait_ge(turned, c + 1)
                nc.scalar.activation(wqT[:, c, :], ps[c][:, 0:D], ACT.Copy).then_inc(turned_copied, 1)
            act.wait_ge(turned, 3)
            nc.scalar.activation(wkbT[0:LAT, :], ps[2][0:LAT, 0:D], ACT.Copy).then_inc(turned_copied, 1)
            act.wait_ge(ones_ready, 1)

            def batch(b, u, i, last):
                def read(job, out, in_):
                    if job in (T0, T1):
                        norm.wait_transposed(act, b, job - T0)
                    else:
                        act.wait_ge(product, PRODUCTS * b + job - LATENT + 1)
                    nc.scalar.activation(out, in_, ACT.Copy).then_inc(act_read, 1)

                for job in (T0, T1):
                    read(job, xnT[:, job - T0, :], ps[PAIR_OF[job]][:, :])
                read(LATENT, latent[:, :], ps[PAIR_OF[LATENT]][:, :])
                act.wait_ge(parts_stored[u], 64 * (i + 1))
                for k, job in enumerate(QK):
                    read(job, parts[u][:, k, 0, :], ps[PAIR_OF[job]][:, :])
                act.wait_ge(v_stored[u], 16 * (i + 1))
                for n, job in enumerate((V0, V1)):
                    read(job, v[u][:, 4 * n:4 * n + 4, :, 0:HD],
                         ps[PAIR_OF[job]][:, :].rearrange("p (t h d) -> p t h d", t=4, h=NH))

            each_batch(act, 2, batch)

        @block.tensor
        def _(pe):
            pe.wait_ge(weights, WEIGHTS)
            for c in range(CB):
                for f in range(CB):
                    last = nc.tensor.matmul(ps[c][:, f * P:(f + 1) * P], wq_n[:, f, c * P:(c + 1) * P],
                                            turn[:, f, :], start=True, stop=True)
                last.then_inc(turned, 1)
            for f in range(CB):
                last = nc.tensor.matmul(ps[2][0:LAT, f * P:(f + 1) * P], wkb_n[:, f, :], turn[:, f, :],
                                        start=True, stop=True)
            last.then_inc(turned, 1)
            pe.wait_ge(turned_copied, 3)
            pe.wait_ge(ident_ready, 1)

            def batch(b, u, i, last):
                def free(job):
                    old = BEFORE[job]
                    turn_ = b if old < job else b - 1
                    pe.wait_ge(act_read, JOBS + JOBS * turn_ + old + 1)
                    if old in QK:
                        pe.wait_ge(rest_ready, 4 + 4 * turn_ + QK.index(old) + 1)

                norm.tensor(nc, pe, b, u, ident, (ps[PAIR_OF[T0]], ps[PAIR_OF[T1]]), lambda c: free(T0 + c))

                def project(job, weight, source, blocks):
                    free(job)
                    for h in range(2):
                        for c in range(blocks):
                            last_m = nc.tensor.matmul(ps[PAIR_OF[job]][:, h * HALF:(h + 1) * HALF], weight(c),
                                                      source(c, h), start=c == 0, stop=c == blocks - 1)
                    last_m.then_inc(product, 1)

                half = lambda c, h: xnT[:, c, h * HALF:(h + 1) * HALF]
                pe.wait_ge(act_read, JOBS + JOBS * b + T1 + 1)
                project(LATENT, lambda c: wkvaT[:, c, :], half, CB)
                for f in range(CB):
                    project(Q0 + f, lambda c: wqT[:, c, f * P:(f + 1) * P], half, CB)
                pe.wait_ge(act_read, JOBS + JOBS * b + LATENT + 1)
                for f in range(CB):
                    project(K0 + f, lambda c: wkbT[:, f * P:(f + 1) * P],
                            lambda c, h: latent[:, h * HALF:(h + 1) * HALF], 1)
                for n, job in enumerate((V0, V1)):
                    free(job)
                    for t in range(4):
                        last_m = nc.tensor.matmul(ps[PAIR_OF[job]][:, t * D:(t + 1) * D],
                                                  latent[:, (4 * n + t) * P:(4 * n + t + 1) * P], wvbT[:, :],
                                                  start=True, stop=True)
                    last_m.then_inc(product, 1)

            each_batch(pe, 2, batch)


def attention(nc, qk_parts, v_ones, max_scratch, attnT):
    LEAD = 3
    UNITS = GH * TT
    STEPS = 2 * TT
    GROUPS = NB * NG
    FULL = ROWS + 3
    SCALE = float(HD) ** -0.5

    with ExitStack() as ctx:
        st = Stage(nc, ctx, "attn")
        q = [st.sb(f"q{g}", [FULL, GH, T], BF16) for g in range(NG)]
        k = [st.sb(f"k{g}", [FULL, GH, T], BF16) for g in range(NG)]
        v = [st.sb(f"v{g}", [P, TT, GH * VW]) for g in range(NG)]
        probs = [st.sb(f"probs{i}", [P, GH, HALF]) for i in range(2)]
        maxima = [st.sb(f"maxima{i}", [P, UNITS]) for i in range(2)]
        maxT = [st.sb(f"maxT{i}", [P, 32]) for i in range(2)]
        max_rest = st.sb("max_rest", [P, 32])
        max_parts = [st.sb(f"max_parts{i}", [P, 3, 32], BF16) for i in range(2)]
        sums = st.sb("sums", [P, 2, HALF])
        blocks = st.sb("blocks", [P, 32, 32])
        recip = st.sb("recip", [P, 32])
        outT = st.sb("outT", [P, T])
        psT = [st.ps(f"scoresT{i}", [P, HALF]) for i in range(2)]
        psM = [st.ps(f"scores{i}", [P, PAIR]) for i in range(2)]
        psO = [st.ps(f"out{i}", [P, HALF]) for i in range(2)]

        qk_loaded = [st.sem(f"qk_loaded{g}") for g in range(NG)]
        v_loaded = [st.sem(f"v_loaded{g}") for g in range(NG)]
        ones_ready = st.sem("ones_ready")
        scores_ready = st.sem("scores_ready")
        maxima_read = st.sem("maxima_read")
        maxT_ready = st.sem("maxT_ready")
        max_steps = st.sem("max_steps")
        max_stored = st.sem("max_stored")
        max_loaded = [st.sem(f"max_loaded{g}") for g in range(NG)]
        scoresT_ready = st.sem("scoresT_ready")
        exps_done = st.sem("exps_done")
        pv_done = st.sem("pv_done")
        out_copied = st.sem("out_copied")
        sums_read = st.sem("sums_read")
        norm_steps = st.sem("norm_steps")
        out_stored = st.sem("out_stored")
        pool_passed = st.sem("pool_passed")
        dve_passed = st.sem("dve_passed")
        act_passed = st.sem("act_passed")
        block = ctx.enter_context(nc.Block())
        LOADS = 16 * 2 * SLOTS

        @block.sync
        def _(sp):
            def load(b, g):
                for tile, which, slots in ((q, 0, Q_PARTS), (k, 1, K_PARTS)):
                    for s, part in enumerate(slots):
                        heads = qk_parts[b, which, part, g * GH * HD:(g + 1) * GH * HD, :]
                        sp.dma_start(tile[g][s * HD:(s + 1) * HD, :, :],
                                     heads.rearrange("(h d) t -> d h t", d=HD)).then_inc(qk_loaded[g], 16)
                sp.dma_start(v[g][:, :, :], v_ones[b].rearrange("p (t w) -> p t w", t=TT)
                             [:, :, g * GH * VW:(g + 1) * GH * VW]).then_inc(v_loaded[g], 16)

            def max_rows(b, g, n):
                sp.wait_ge(max_steps, 4 * (n + 1))
                sp.dma_start(max_scratch[g], max_parts[g % 2][:, :, :].rearrange("p a r -> p (a r)"))\
                    .then_inc(max_stored, 16)
                sp.wait_ge(max_stored, 16 * (n + 1))
                for a in range(3):
                    sp.dma_start(q[g][ROWS + a:ROWS + a + 1, :, :].rearrange("o h (t q r) -> o (h t) q r", q=4, r=32),
                                 max_scratch[g][:, a * 32:(a + 1) * 32].rearrange("(o q c) r -> o c q r", o=1, q=4))\
                        .then_inc(max_loaded[g], 16)

            for g in range(NG):
                load(0, g)
            max_rows(0, 0, 0)

            def batch(b, u, i, last):
                for g in range(NG):
                    n = NG * b + g
                    if not (last and g == NG - 1):
                        max_rows(b, (g + 1) % NG, n + 1)
                    if not last:
                        sp.wait_ge(pv_done, 2 + STEPS * (n + 1))
                        load(b + 1, g)
                    sp.wait_ge(norm_steps, 4 * (n + 2))
                    for h in range(GH):
                        row = g * GH * HD + h * HD
                        sp.dma_start(attnT[b, row:row + HD, :], outT[h * 32:h * 32 + HD, :]).then_inc(out_stored, 16)

            each_batch(sp, 1, batch)
            sp.wait_ge(out_stored, 64 * (GROUPS + 1))

        @block.gpsimd
        def _(pool):
            for g in range(NG):
                last_m = nc.gpsimd.memset(k[g][ROWS:FULL, :, :], 1.0)
            last_m.then_inc(ones_ready, 1)

            def split(g, n):
                i = g % 2
                pool.wait_ge(maxT_ready, n + 1)
                pool.wait_ge(max_steps, 4 * n)
                stand(pool, pool_passed)
                nc.gpsimd.tensor_scalar(max_parts[i][:, 0, :], maxT[i][:, :], 1.0, 0.0, ALU.mult, ALU.add)\
                    .then_inc(max_steps, 1)
                pool.wait_ge(max_steps, 4 * n + 1)
                nc.gpsimd.tensor_tensor(max_rest[:, :], maxT[i][:, :], max_parts[i][:, 0, :], ALU.subtract)\
                    .then_inc(max_steps, 1)
                pool.wait_ge(max_steps, 4 * n + 2)
                stand(pool, pool_passed)
                nc.gpsimd.tensor_scalar(max_parts[i][:, 1, :], max_rest[:, :], 1.0, 0.0, ALU.mult, ALU.add)\
                    .then_inc(max_steps, 1)
                pool.wait_ge(max_steps, 4 * n + 3)
                nc.gpsimd.tensor_tensor(max_parts[i][:, 2, :], max_rest[:, :], max_parts[i][:, 1, :], ALU.subtract)\
                    .then_inc(max_steps, 1)

            split(0, 0)

            def batch(b, u, i, last):
                for g in range(NG):
                    if not (last and g == NG - 1):
                        split((g + 1) % NG, NG * b + g + 1)

            each_batch(pool, 1, batch)

        @block.vector
        def _(dve):
            dve.sem_inc(maxima_read, 2)
            dve.sem_inc(sums_read, 1)
            dve.sem_inc(norm_steps, 4)

            def unit(b, m):
                g, c = m // UNITS, m % UNITS
                n, i = NG * b + g, g % 2
                dve.wait_ge(scores_ready, UNITS * n + c + 1)
                if c == 0:
                    dve.wait_ge(maxT_ready, n)
                nc.vector.tensor_reduce(maxima[i][:, c:c + 1], psM[c % 2][:, :], AX.X, ALU.max, negate=True)\
                    .then_inc(maxima_read, 1)
                if c == UNITS - 1:
                    dve.wait_ge(maxima_read, 2 + UNITS * (n + 1))
                    nc.vector.transpose(maxT[i][:, :], maxima[i][:, :]).then_inc(maxT_ready, 1)

            def divide(b, g):
                n = NG * b + g
                dve.wait_ge(out_copied, 2 + 2 * (n + 1))
                dve.wait_ge(norm_steps, 4 * (n + 1))
                nc.vector.transpose(blocks[:, :, :].rearrange("p a r -> p (a r)"),
                                    sums[:, :, :].rearrange("p a r -> p (a r)")).then_inc(sums_read, 1)
                dve.wait_ge(sums_read, n + 2)
                nc.vector.reciprocal(recip[:, :], blocks[:, :, HD]).then_inc(norm_steps, 1)
                dve.wait_ge(norm_steps, 4 * (n + 1) + 1)
                nc.vector.tensor_tensor(blocks[:, :, 0:HD], blocks[:, :, 0:HD],
                                        recip[:, :].unsqueeze(2).to_broadcast([P, 32, HD]), ALU.mult)\
                    .then_inc(norm_steps, 1)
                dve.wait_ge(norm_steps, 4 * (n + 1) + 2)
                dve.wait_ge(out_stored, 64 * (n + 1))
                nc.vector.transpose(outT[:, :], blocks[:, :, :].rearrange("p a r -> p (a r)"))\
                    .then_inc(norm_steps, 2)

            for m in range(UNITS + 2 * LEAD):
                unit(0, m)

            def batch(b, u, i, last):
                for s in range(NG * STEPS):
                    for w in range(2):
                        m = UNITS + 2 * LEAD + 2 * s + w
                        if not (last and m >= NG * UNITS):
                            unit(b, m)
                    if s % STEPS == LEAD and s > STEPS:
                        divide(b, s // STEPS - 1)
                divide(b, NG - 1)

            each_batch(dve, 1, batch)

        @block.scalar
        def _(act):
            act.sem_inc(exps_done, 2)
            act.sem_inc(out_copied, 2)
            act.sem_inc(out_stored, 64)

            def copy_out(b, g, half):
                n = NG * b + g
                act.wait_ge(pv_done, 2 + STEPS * n + STEPS - 1 + half)
                act.wait_ge(sums_read, n + 1)
                nc.scalar.activation(sums[:, half, :], psO[half][:, :], ACT.Copy).then_inc(out_copied, 1)

            def batch(b, u, i, last):
                for s in range(NG * STEPS):
                    g = s // STEPS
                    if g > 0 and s % STEPS < 2:
                        copy_out(b, g - 1, s % STEPS)
                    for h in range(GH):
                        act.wait_ge(scoresT_ready, GH * (NG * STEPS * b + s) + h + 1)
                        if h == 0:
                            act.wait_ge(pv_done, NG * STEPS * b + s + 1)
                        nc.scalar.activation(probs[s % 2][:, h, :], psT[h % 2][:, :], ACT.Exp, scale=SCALE)\
                            .then_inc(exps_done, 1)
                for half in range(2):
                    copy_out(b, NG - 1, half)

            each_batch(act, 1, batch)

        @block.tensor
        def _(pe):
            pe.sem_inc(pv_done, 2)
            pe.wait_ge(ones_ready, 1)

            def unit_half(b, m, half):
                g, c = m // UNITS, m % UNITS
                n, g = NG * b + g, g % NG
                h, t = c // TT, c % TT
                if half == 0:
                    if c == 0:
                        pe.wait_ge(qk_loaded[g], LOADS * (b + 1 + m // (NG * UNITS)))
                    pe.wait_ge(maxima_read, UNITS * n + c + 1)
                mm = nc.tensor.matmul(psM[c % 2][:, half * HALF:(half + 1) * HALF],
                                      q[g][0:ROWS, h, t * P:(t + 1) * P],
                                      k[g][0:ROWS, h, half * HALF:(half + 1) * HALF], start=True, stop=True)
                if half == 1:
                    mm.then_inc(scores_ready, 1)

            def values(b, s):
                g, kt, half = s // STEPS, s % STEPS // 2, s % 2
                pe.wait_ge(exps_done, 2 + GH * (NG * STEPS * b + s + 1))
                if kt == 0:
                    pe.wait_ge(out_copied, 2 * (NG * b + g) + half + 1)
                    pe.wait_ge(v_loaded[g], 16 * (b + 1))
                for h in range(GH):
                    mm = nc.tensor.matmul(psO[half][h * VW:(h + 1) * VW, :], v[g][:, kt, h * VW:(h + 1) * VW],
                                          probs[s % 2][:, h, :], start=kt == 0, stop=kt == TT - 1)
                mm.then_inc(pv_done, 1)

            for m in range(UNITS + 2 * LEAD):
                for half in range(2):
                    unit_half(0, m, half)

            def batch(b, u, i, last):
                for s in range(NG * STEPS):
                    g, kt, half = s // STEPS, s % STEPS // 2, s % 2
                    if s % STEPS == 0:
                        pe.wait_ge(max_loaded[g], 48 * (b + 1))
                    for h in range(GH):
                        pe.wait_ge(exps_done, GH * (NG * STEPS * b + s) + h + 1)
                        nc.tensor.matmul(psT[h % 2][:, :], k[g][0:FULL, h, kt * P:(kt + 1) * P],
                                         q[g][0:FULL, h, half * HALF:(half + 1) * HALF], start=True, stop=True)\
                            .then_inc(scoresT_ready, 1)
                        m = UNITS + 2 * LEAD + 2 * s + h // 2
                        if not (last and m >= NG * UNITS):
                            unit_half(b, m, h % 2)
                    if s > 0:
                        values(b, s - 1)
                values(b, NG * STEPS - 1)

            each_batch(pe, 1, batch)


def residual_ffn(nc, name, x_in, branchT, branch_w, win, b_in, w1, b1, w2, b2, wout, bout, x_out):
    KB = branchT.shape[1] // P
    MIX0, MIX1, T0, T1, UNITS, OUT0, OUT1 = range(7)
    PAIR_OF = {MIX0: 0, MIX1: 1, T0: 2, T1: 3, UNITS: 0, OUT0: 1, OUT1: 2}
    RELUS = 4

    with ExitStack() as ctx:
        st = Stage(nc, ctx, name)
        xt = [st.sb(f"x{u}", [P, TT, D]) for u in range(2)]
        branch = [st.sb(f"branch{u}", [P, KB, T]) for u in range(2)]
        norm = Norm(st)
        xnT = st.sb("xnT", [P, CB, T])
        s = [st.sb(f"s{u}", [P, HALF]) for u in range(2)]
        hidden = [st.sb(f"hidden{i}", [P, HALF]) for i in range(RELUS)]
        g = st.sb("g", [P, HALF])
        ident = st.sb("ident", [P, P])
        bw = st.sb("branch_w", [P, KB, D])
        win_sb = st.sb("win", [P, CB, M])
        cols = st.sb("cols", [P, 2, 1])
        w1_sb, b1_sb, w2_sb = (st.sb(n, [P, INNER]) for n in ("w1", "b1", "w2"))
        wout_sb = [st.sb(f"wout{h}", [P, D]) for h in range(2)]
        bout_sb = st.sb("bout", [P, D])
        ps = [st.ps(f"p{i}", [P, PAIR]) for i in range(4)]

        weights = st.sem("weights")
        pads_ready = st.sem("pads_ready")
        zeroed = st.sem("zeroed")
        ident_ready = st.sem("ident_ready")
        x_loaded = [st.sem(f"x_loaded{u}") for u in range(2)]
        branch_loaded = [st.sem(f"branch_loaded{u}") for u in range(2)]
        x_stored = [st.sem(f"x_stored{u}") for u in range(2)]
        mixed = st.sem("mixed")
        added = st.sem("added")
        copied = st.sem("copied")
        units_ready = st.sem("units_ready")
        biased = st.sem("biased")
        relu_ready = st.sem("relu_ready")
        summed = st.sem("summed")
        out_ready = st.sem("out_ready")
        x_ready = st.sem("x_ready")
        block = ctx.enter_context(nc.Block())
        tokens = lambda a: a.rearrange("(t p) c -> p t c", p=P)

        @block.sync
        def _(sp):
            def load(b, u):
                sp.dma_start(xt[u][:, :, :], tokens(x_in[b])).then_inc(x_loaded[u], 16)
                sp.dma_start(branch[u][:, :, :], branchT[b].rearrange("(a p) t -> p a t", p=P))\
                    .then_inc(branch_loaded[u], 16)

            load(0, 0)
            sp.dma_start(bw[:, :, :], branch_w.rearrange("(a p) c -> p a c", p=P)).then_inc(weights, 16)
            sp.dma_start(win_sb[:, :, :], win.rearrange("(a p) c -> p a c", p=P)).then_inc(weights, 16)
            sp.dma_start(bout_sb[:, :], bout.rearrange("(o c) -> o c", o=1).to_broadcast([P, D])).then_inc(weights, 16)
            for h in range(2):
                rows = slice(h * M, (h + 1) * M)
                for tile, w in ((w1_sb, w1), (b1_sb, b1), (w2_sb, w2)):
                    sp.dma_start(tile[rows, :], w).then_inc(weights, 16)
                for n, w in enumerate((b_in, b2)):
                    sp.dma_start(cols[rows, n, :], w.rearrange("(m o) -> m o", o=1)).then_inc(weights, 16)
            sp.wait_ge(pads_ready, 1)
            for h in range(2):
                sp.dma_start(wout_sb[h][h * M:(h + 1) * M, :], wout).then_inc(weights, 16)
            load(1, 1)

            def batch(b, u, i, last):
                sp.wait_ge(x_ready, 8 + 4 * (b + 1))
                sp.dma_start(tokens(x_out[b]), xt[u][:, :, :]).then_inc(x_stored[u], 16)

            def reload(b, u, i):
                sp.wait_ge(x_stored[u], 16 * (i + 1))
                load(b + 2, u)

            with sp.Fori(0, NB // 2 - 1) as i:
                for u in range(2):
                    batch(2 * i + u, u, i, False)
                    reload(2 * i + u, u, i)
            for u in range(2):
                batch(NB - 2 + u, u, NB // 2 - 1, True)
            for u in range(2):
                sp.wait_ge(x_stored[u], 16 * (NB // 2))
        WEIGHTS = 16 * (3 + 10 + 2)

        @block.gpsimd
        def _(pool):
            for h in range(2):
                last_m = nc.gpsimd.memset(wout_sb[h][:, :], 0.0)
            last_m.then_inc(pads_ready, 1)
            norm.setup(nc, pool)
            make_identity(nc, pool, ident, zeroed, ident_ready)
            pool.wait_ge(weights, WEIGHTS)
            norm.gpsimd(nc, pool, 0, 0, xt[0])

            def batch(b, u, i, last):
                if not last:
                    norm.gpsimd(nc, pool, b + 1, 1 - u, xt[1 - u])
                for n in range(4):
                    pool.wait_ge(norm.xn_ready, b + 2)
                    tiles = xt[u][:, 2 * n:2 * n + 2, :]
                    nc.gpsimd.tensor_tensor(tiles, tiles, bout_sb[:, :].unsqueeze(1).to_broadcast([P, 2, D]), ALU.add)\
                        .then_inc(biased, 1)

            each_batch(pool, 2, batch)

        @block.vector
        def _(dve):
            dve.sem_inc(added, 4)
            dve.sem_inc(summed, RELUS)
            dve.sem_inc(x_ready, 8)
            dve.sem_inc(out_ready, 2)

            def front(b, u, i):
                dve.wait_ge(x_loaded[u], 16 * (i + 1))
                for n in range(4):
                    if n % 2 == 0:
                        dve.wait_ge(mixed, 2 * b + n // 2 + 1)
                    tiles = xt[u][:, 2 * n:2 * n + 2, :]
                    nc.vector.tensor_tensor(tiles, tiles, ps[PAIR_OF[MIX0 + n // 2]]
                                            [:, (n % 2) * HALF:(n % 2 + 1) * HALF]
                                            .rearrange("p (t c) -> p t c", t=2), ALU.add).then_inc(added, 1)
                dve.wait_ge(added, 4 + 4 * (b + 1))
                norm.vector(nc, dve, b, u, xt[u])

            dve.wait_ge(weights, WEIGHTS)
            front(0, 0, 0)

            def batch(b, u, i, last):
                if not last:
                    front(b + 1, 1 - u, i + u)
                for j in range(INNER):
                    dve.wait_ge(relu_ready, INNER * b + j + 1)
                    dve.wait_ge(summed, RELUS + INNER * b + j)
                    if j == 0:
                        dve.wait_ge(out_ready, 2 * b + 2)
                        ins = nc.vector.tensor_scalar(g[:, :], hidden[j % RELUS][:, :], w2_sb[:, j:j + 1],
                                                      cols[:, 1, :], ALU.mult, ALU.add)
                    else:
                        ins = nc.vector.scalar_tensor_tensor(g[:, :], hidden[j % RELUS][:, :], w2_sb[:, j:j + 1],
                                                             g[:, :], ALU.mult, ALU.add)
                    ins.then_inc(summed, 1)
                dve.wait_ge(biased, 4 * (b + 1))
                for n in range(4):
                    if n % 2 == 0:
                        dve.wait_ge(out_ready, 2 + 2 * b + n // 2 + 1)
                    tiles = xt[u][:, 2 * n:2 * n + 2, :]
                    nc.vector.tensor_tensor(tiles, tiles, ps[PAIR_OF[OUT0 + n // 2]]
                                            [:, (n % 2) * HALF:(n % 2 + 1) * HALF]
                                            .rearrange("p (t c) -> p t c", t=2), ALU.add).then_inc(x_ready, 1)

            each_batch(dve, 2, batch)

        @block.scalar
        def _(act):
            act.sem_inc(copied, 3)
            act.wait_ge(weights, WEIGHTS)

            def front(b, u):
                for c in range(CB):
                    norm.wait_transposed(act, b, c)
                    nc.scalar.activation(xnT[:, c, :], ps[PAIR_OF[T0 + c]][:, :], ACT.Copy).then_inc(copied, 1)
                act.wait_ge(units_ready, b + 1)
                nc.scalar.activation(s[u][:, :], ps[PAIR_OF[UNITS]][:, 0:HALF], ACT.Identity, bias=cols[:, 0, :])\
                    .then_inc(copied, 1)

            front(0, 0)

            def batch(b, u, i, last):
                act.wait_ge(copied, 3 + 3 * (b + 1))
                for j in range(INNER):
                    act.wait_ge(summed, INNER * b + j + 1)
                    nc.scalar.activation(hidden[j % RELUS][:, :], s[u][:, :], ACT.Relu, bias=b1_sb[:, j:j + 1],
                                         scale=w1_sb[:, j:j + 1]).then_inc(relu_ready, 1)
                    if j == INNER // 2 + 1 and not last:
                        front(b + 1, 1 - u)

            each_batch(act, 2, batch)

        @block.tensor
        def _(pe):
            pe.wait_ge(weights, WEIGHTS)
            pe.wait_ge(ident_ready, 1)

            def tiles(job, n, source, weight, blocks, done):
                for t in range(4):
                    for c in range(blocks):
                        mm = nc.tensor.matmul(ps[PAIR_OF[job]][:, t * D:(t + 1) * D], source(c, 4 * n + t), weight(c),
                                              start=c == 0, stop=c == blocks - 1)
                mm.then_inc(done, 1)

            def front(b, u, i):
                pe.wait_ge(branch_loaded[u], 16 * (i + 1))
                pe.wait_ge(copied, 3 * (b + 1))
                for n in range(2):
                    if n == 1:
                        pe.wait_ge(x_ready, 4 * b + 2)
                    tiles(MIX0 + n, n, lambda c, t: branch[u][:, c, t * P:(t + 1) * P], lambda c: bw[:, c, :], KB, mixed)

                def free(c):
                    if c == 0:
                        pe.wait_ge(x_ready, 4 * b + 4)
                    else:
                        pe.wait_ge(copied, 3 * b + 2)

                norm.tensor(nc, pe, b, u, ident, (ps[PAIR_OF[T0]], ps[PAIR_OF[T1]]), free)
                pe.wait_ge(copied, 3 + 3 * b + 2)
                pe.wait_ge(added, 4 + 4 * b + 2)
                for h in range(2):
                    for c in range(CB):
                        mm = nc.tensor.matmul(ps[PAIR_OF[UNITS]][h * M:(h + 1) * M, 0:HALF], win_sb[:, c, :],
                                              xnT[:, c, h * HALF:(h + 1) * HALF], start=c == 0, stop=c == CB - 1)
                mm.then_inc(units_ready, 1)

            front(0, 0, 0)

            def batch(b, u, i, last):
                if not last:
                    front(b + 1, 1 - u, i + u)
                pe.wait_ge(summed, RELUS + INNER * (b + 1))
                if last:
                    pe.wait_ge(added, 4 + 4 * (b + 1))
                else:
                    pe.wait_ge(added, 4 + 4 * (b + 2))
                for n in range(2):
                    if n == 1:
                        pe.wait_ge(copied, 3 + 3 * b + 3 * (not last) + 1)
                    tiles(OUT0 + n, n, lambda c, t: g[:, (t % 4) * P:(t % 4 + 1) * P], lambda c: wout_sb[n][:, :],
                          1, out_ready)

            each_batch(pe, 2, batch)


def project_scan(nc, x, x_wT, dt_wT, dt_b, bc_wT, conv_w, conv_b, xc_out, dt_out, dtx_out, b_out, c_parts):
    X, BC, DT = 0, DB, DB + 1
    JOBS = 2 * DB + 1
    PAIR_OF = [0, 1, 0, 1, 2, 3, 0, 1, 2]
    PAD = TAPS - 1

    with ExitStack() as ctx:
        st = Stage(nc, ctx, "prep")
        xt = [st.sb(f"x{u}", [P, TT, D]) for u in range(2)]
        norm = Norm(st)
        xnT = st.sb("xnT", [P, CB, T])
        xi = [st.sb(f"xi{i}", [P, PAD + T]) for i in range(2)]
        conv = [st.sb(f"conv{i}", [P, T]) for i in range(2)]
        xc = [st.sb(f"xc{d}", [P, T]) for d in range(DB)]
        soft = [st.sb(f"soft{i}", [P, T]) for i in range(2)]
        relu = [st.sb(f"relu{i}", [P, T]) for i in range(2)]
        dt = [st.sb(f"dt{i}", [P, T]) for i in range(2)]
        dtx = [st.sb(f"dtx{i}", [P, T]) for i in range(2)]
        bc = st.sb("bc", [2 * NS, T])
        bc_rest = st.sb("bc_rest", [2 * NS, T])
        bc_parts = st.sb("bc_parts", [2 * NS, 3, T], BF16)
        ident = st.sb("ident", [P, P])
        xw = st.sb("x_w", [P, CB, DI])
        dtw = st.sb("dt_w", [P, CB, DI])
        bcw = st.sb("bc_w", [P, CB, 2 * NS])
        dtb = st.sb("dt_b", [P, DB])
        cw = st.sb("conv_w", [P, DB, TAPS])
        cb = st.sb("conv_b", [P, DB])
        ps = [st.ps(f"p{i}", [P, PAIR]) for i in range(4)]

        weights = st.sem("weights")
        zeroed = st.sem("zeroed")
        ident_ready = st.sem("ident_ready")
        pads_ready = st.sem("pads_ready")
        x_loaded = [st.sem(f"x_loaded{u}") for u in range(2)]
        xnT_ready = st.sem("xnT_ready")
        product = st.sem("product")
        xi_ready = st.sem("xi_ready")
        tap0_ready = st.sem("tap0_ready")
        conv_steps = st.sem("conv_steps")
        xc_ready = st.sem("xc_ready")
        bc_hi = st.sem("bc_hi")
        bc_rested = st.sem("bc_rested")
        bc_steps = st.sem("bc_steps")
        relu_ready = st.sem("relu_ready")
        soft_steps = st.sem("soft_steps")
        dt_ready = st.sem("dt_ready")
        dtx_ready = st.sem("dtx_ready")
        xc_stored = [st.sem(f"xc_stored{d}") for d in range(DB)]
        dt_stored = [st.sem(f"dt_stored{i}") for i in range(2)]
        dtx_stored = [st.sem(f"dtx_stored{i}") for i in range(2)]
        b_stored = st.sem("b_stored")
        c_stored = st.sem("c_stored")
        block = ctx.enter_context(nc.Block())
        WEIGHTS = 16 * 6
        tokens = lambda a: a.rearrange("(t p) c -> p t c", p=P)

        @block.sync
        def _(sp):
            def load(b, u):
                sp.dma_start(xt[u][:, :, :], tokens(x[b])).then_inc(x_loaded[u], 16)

            load(0, 0)
            for tile, w in ((xw, x_wT), (dtw, dt_wT), (bcw, bc_wT)):
                sp.dma_start(tile[:, :, :], w.rearrange("(a p) c -> p a c", p=P)).then_inc(weights, 16)
            sp.dma_start(cw[:, :, :], conv_w.rearrange("(a p) c -> p a c", p=P)).then_inc(weights, 16)
            for tile, w in ((dtb, dt_b), (cb, conv_b)):
                sp.dma_start(tile[:, :], w).then_inc(weights, 16)
            load(1, 1)

            def batch(b, u, i):
                rows = lambda d: slice(d * P, (d + 1) * P)
                for d in range(DB):
                    sp.wait_ge(xc_ready, DB + DB * b + d + 1)
                    sp.dma_start(xc_out[b, rows(d), :], xc[d][:, :]).then_inc(xc_stored[d], 16)
                sp.wait_ge(bc_hi, 2 + 2 * (b + 1))
                sp.dma_start(b_out[b], bc[0:NS, :]).then_inc(b_stored, 16)
                sp.wait_ge(bc_steps, 2 * (b + 2))
                sp.dma_start(c_parts[b].rearrange("a s t -> s a t"), bc_parts[NS:2 * NS, :, :]).then_inc(c_stored, 16)
                for d in range(DB):
                    sp.wait_ge(dt_ready, DB + DB * b + d + 1)
                    sp.dma_start(dt_out[b, rows(d), :], dt[d % 2][:, :]).then_inc(dt_stored[d % 2], 16)
                    sp.wait_ge(dtx_ready, DB + DB * b + d + 1)
                    sp.dma_start(dtx_out[b, rows(d), :], dtx[d % 2][:, :]).then_inc(dtx_stored[d % 2], 16)

            def reload(b, u):
                sp.wait_ge(norm.xn_ready, b + 2)
                load(b + 2, u)

            with sp.Fori(0, NB // 2 - 1) as i:
                for u in range(2):
                    reload(2 * i + u, u)
                    batch(2 * i + u, u, i)
            for u in range(2):
                batch(NB - 2 + u, u, NB // 2 - 1)
            for d in range(DB):
                sp.wait_ge(xc_stored[d], 16 * (NB + 1))
            for n in range(2):
                sp.wait_ge(dt_stored[n], 16 * (DB // 2 * NB + 1))
                sp.wait_ge(dtx_stored[n], 16 * (DB // 2 * NB + 1))
            sp.wait_ge(b_stored, 16 * (NB + 1))
            sp.wait_ge(c_stored, 16 * (NB + 1))

        @block.gpsimd
        def _(pool):
            for n in range(2):
                last_m = nc.gpsimd.memset(xi[n][:, 0:PAD], 0.0)
            last_m.then_inc(pads_ready, 1)
            norm.setup(nc, pool)
            pool.sem_inc(dt_ready, DB)
            pool.sem_inc(dtx_ready, DB)
            pool.sem_inc(bc_steps, 2)
            make_identity(nc, pool, ident, zeroed, ident_ready)
            pool.wait_ge(weights, WEIGHTS)
            norm.gpsimd(nc, pool, 0, 0, xt[0])

            def batch(b, u, i, last):
                if not last:
                    norm.gpsimd(nc, pool, b + 1, 1 - u, xt[1 - u])
                for d in range(DB):
                    pool.wait_ge(xi_ready, DB + DB * b + d + 1)
                    pool.wait_ge(xc_ready, DB * b + d + 3)
                    stand(pool, norm.pool_passed)
                    nc.gpsimd.tensor_scalar(conv[d % 2][:, :], xi[d % 2][:, PAD:PAD + T], cw[:, d, PAD:PAD + 1],
                                            cb[:, d:d + 1], ALU.mult, ALU.add).then_inc(tap0_ready, 1)
                pool.wait_ge(bc_rested, 1 + b + 1)
                pool.wait_ge(c_stored, 16 * (b + 1))
                stand(pool, norm.pool_passed)
                nc.gpsimd.tensor_scalar(bc_parts[:, 1, :], bc_rest[:, :], 1.0, 0.0, ALU.mult, ALU.add)\
                    .then_inc(bc_steps, 1)
                pool.wait_ge(bc_steps, 2 + 2 * b + 1)
                nc.gpsimd.tensor_tensor(bc_parts[:, 2, :], bc_rest[:, :], bc_parts[:, 1, :], ALU.subtract)\
                    .then_inc(bc_steps, 1)
                for d in range(DB):
                    n = d % 2
                    pool.wait_ge(relu_ready, DB + DB * b + d + 1)
                    pool.wait_ge(soft_steps, 3 * DB + 3 * (DB * b + d + 1))
                    pool.wait_ge(dt_stored[n], 16 * (DB // 2 * b + d // 2 + 1))
                    nc.gpsimd.tensor_tensor(dt[n][:, :], relu[n][:, :], soft[n][:, :], ALU.add).then_inc(dt_ready, 1)
                    pool.wait_ge(dt_ready, DB + DB * b + d + 1)
                    pool.wait_ge(dtx_stored[n], 16 * (DB // 2 * b + d // 2 + 1))
                    nc.gpsimd.tensor_tensor(dtx[n][:, :], dt[n][:, :], xc[d][:, :], ALU.mult).then_inc(dtx_ready, 1)

            each_batch(pool, 2, batch)

        @block.vector
        def _(dve):
            dve.sem_inc(conv_steps, 3 * DB)
            dve.sem_inc(bc_rested, 1)
            dve.sem_inc(relu_ready, DB)
            dve.wait_ge(weights, WEIGHTS)
            dve.wait_ge(x_loaded[0], 16)
            norm.vector(nc, dve, 0, 0, xt[0])

            def batch(b, u, i, last):
                if not last:
                    dve.wait_ge(x_loaded[1 - u], 16 * (i + 1 + u))
                    norm.vector(nc, dve, b + 1, 1 - u, xt[1 - u])
                for d in range(DB):
                    n = d % 2
                    dve.wait_ge(tap0_ready, DB * b + d + 1)
                    for k in range(1, TAPS):
                        lag = PAD - k
                        if k > 1:
                            dve.wait_ge(conv_steps, 3 * (DB + DB * b + d) + k - 1)
                        nc.vector.scalar_tensor_tensor(conv[n][:, :], xi[n][:, lag:lag + T], cw[:, d, lag:lag + 1],
                                                       conv[n][:, :], ALU.mult, ALU.add).then_inc(conv_steps, 1)
                dve.wait_ge(bc_hi, 2 + 2 * (b + 1))
                dve.wait_ge(bc_steps, 2 * b + 2)
                nc.vector.tensor_tensor(bc_rest[:, :], ps[PAIR_OF[BC]][0:2 * NS, :], bc_parts[:, 0, :], ALU.subtract)\
                    .then_inc(bc_rested, 1)
                for d in range(DB):
                    dve.wait_ge(soft_steps, 3 * (DB + DB * b + d) + 1)
                    dve.wait_ge(dt_ready, DB * b + d + 3)
                    nc.vector.tensor_scalar(relu[d % 2][:, :], ps[PAIR_OF[DT + d]][:, :], dtb[:, d:d + 1], 0.0,
                                            ALU.add, ALU.max).then_inc(relu_ready, 1)

            each_batch(dve, 2, batch)

        @block.scalar
        def _(act):
            act.sem_inc(xnT_ready, CB)
            act.sem_inc(xi_ready, DB)
            act.sem_inc(xc_ready, DB)
            act.sem_inc(bc_hi, 2)
            act.sem_inc(soft_steps, 3 * DB)
            for s in (*xc_stored, *dt_stored, *dtx_stored, b_stored, c_stored):
                act.sem_inc(s, 16)
            act.wait_ge(pads_ready, 1)
            act.wait_ge(weights, WEIGHTS)

            def batch(b, u, i, last):
                for c in range(CB):
                    norm.wait_transposed(act, b, c)
                    nc.scalar.activation(xnT[:, c, :], ps[2 + c][:, :], ACT.Copy).then_inc(xnT_ready, 1)

                def silu(d):
                    act.wait_ge(conv_steps, 3 * (DB + DB * b + d + 1))
                    act.wait_ge(xc_stored[d], 16 * (b + 1))
                    act.wait_ge(dtx_ready, DB * (b + 1))
                    nc.scalar.activation(xc[d][:, :], conv[d % 2][:, :], ACT.Silu).then_inc(xc_ready, 1)

                for d in range(DB):
                    act.wait_ge(product, JOBS * b + X + d + 1)
                    act.wait_ge(conv_steps, 3 * (DB * b + d + 3))
                    nc.scalar.activation(xi[d % 2][:, PAD:PAD + T], ps[PAIR_OF[X + d]][:, :], ACT.Copy)\
                        .then_inc(xi_ready, 1)
                    if d > 0:
                        silu(d - 1)
                silu(DB - 1)
                act.wait_ge(product, JOBS * b + BC + 1)
                act.wait_ge(b_stored, 16 * (b + 1))
                nc.scalar.activation(bc[:, :], ps[PAIR_OF[BC]][0:2 * NS, :], ACT.Copy).then_inc(bc_hi, 1)
                act.wait_ge(c_stored, 16 * (b + 1))
                nc.scalar.activation(bc_parts[:, 0, :], ps[PAIR_OF[BC]][0:2 * NS, :], ACT.Copy).then_inc(bc_hi, 1)
                nc.scalar.preload_act_table_set("natural_log_exp_and_others")
                for d in range(DB):
                    t = soft[d % 2][:, :]
                    steps = 3 * (DB + DB * b + d)
                    act.wait_ge(product, JOBS * b + DT + d + 1)
                    act.wait_ge(dt_ready, DB * b + d + 3)
                    nc.scalar.activation(t, ps[PAIR_OF[DT + d]][:, :], ACT.Abs, bias=dtb[:, d:d + 1]).then_inc(soft_steps, 1)
                    act.wait_ge(soft_steps, steps + 1)
                    nc.scalar.activation(t, t, ACT.Exp, scale=-1.0).then_inc(soft_steps, 1)
                    act.wait_ge(soft_steps, steps + 2)
                    nc.scalar.activation(t, t, ACT.Ln, bias=1.0).then_inc(soft_steps, 1)

            each_batch(act, 2, batch)

        @block.tensor
        def _(pe):
            pe.wait_ge(weights, WEIGHTS)
            pe.wait_ge(ident_ready, 1)

            def read(job, b):
                if job < BC:
                    pe.wait_ge(xi_ready, DB + DB * b + job + 1)
                elif job == BC:
                    pe.wait_ge(bc_rested, 1 + b + 1)
                else:
                    pe.wait_ge(relu_ready, DB + DB * b + job - DT + 1)
                    pe.wait_ge(soft_steps, 3 * (DB + DB * b + job - DT) + 1)

            BEFORE = [(DT + 1, 1), (DT + 2, 1), (X, 0), (X + 1, 0), (None, 0), (None, 0), (X + 2, 0), (X + 3, 0), (BC, 0)]

            def batch(b, u, i, last):
                norm.tensor(nc, pe, b, u, ident, ps[2:4], lambda c: read((DT + 3, DT)[c], b - 1))
                for job in range(JOBS):
                    old, back = BEFORE[job]
                    if old is not None:
                        read(old, b - back)
                    if job == 0:
                        pe.wait_ge(xnT_ready, CB + CB * (b + 1))
                    rows = 2 * NS if job == BC else P
                    w, at = (xw, job * P) if job < BC else (bcw, 0) if job == BC else (dtw, (job - DT) * P)
                    for h in range(2):
                        for c in range(CB):
                            mm = nc.tensor.matmul(ps[PAIR_OF[job]][0:rows, h * HALF:(h + 1) * HALF],
                                                  w[:, c, at:at + rows], xnT[:, c, h * HALF:(h + 1) * HALF],
                                                  start=c == 0, stop=c == CB - 1)
                    mm.then_inc(product, 1)

            each_batch(pe, 2, batch)


def scan(nc, xc_in, dt_in, dtx_in, b_in, c_parts, a_log, d_skip, yT):
    CROWS = 96
    QS = 4
    STEPS = DB * NS
    NU, NGB = 4, 2

    with ExitStack() as ctx:
        st = Stage(nc, ctx, "scan")
        dt = [st.sb(f"dt{i}", [P, T]) for i in range(2)]
        dtx = [st.sb(f"dtx{i}", [P, T]) for i in range(2)]
        xc = [st.sb(f"xc{i}", [P, T]) for i in range(2)]
        bb = [st.sb(f"b{i}", [P, QS, T]) for i in range(NS // QS)]
        c = [st.sb(f"c{i}", [CROWS, T], BF16) for i in range(2)]
        pick = st.sb("pick", [CROWS, NS, P], BF16)
        pick_f = st.sb("pick_f", [CROWS, NS, P])
        ins = [st.sb(f"in{i}", [P, T]) for i in range(NU)]
        h = [st.sb(f"h{i}", [P, T]) for i in range(2)]
        hc = [st.sb(f"hc{i}", [P, T]) for i in range(NGB)]
        y = st.sb("y", [P, T])
        a = st.sb("a", [P, DB, NS])
        skip = st.sb("skip", [P, DB])
        ident = st.sb("ident", [P, P])
        psA = [st.ps(f"decay{i}", [P, PAIR]) for i in range(2)]
        psC = st.ps("c_wide", [P, PAIR])
        psY = st.ps("y_sum", [P, PAIR])

        weights = st.sem("weights")
        zeroed = st.sem("zeroed")
        ident_ready = st.sem("ident_ready")
        pick_steps = st.sem("pick_steps")
        c_zeroed = st.sem("c_zeroed")
        a_steps = st.sem("a_steps")
        block_loaded = [st.sem(f"block_loaded{i}") for i in range(2)]
        b_loaded = [st.sem(f"b_loaded{i}") for i in range(NS // QS)]
        c_loaded = [st.sem(f"c_loaded{i}") for i in range(2)]
        decay_ready = st.sem("decay_ready")
        in_ready = st.sem("in_ready")
        scanned = st.sem("scanned")
        c_wide = st.sem("c_wide")
        hc_ready = st.sem("hc_ready")
        summed = st.sem("summed")
        y_ready = st.sem("y_ready")
        y_stored = st.sem("y_stored")
        block = ctx.enter_context(nc.Block())
        WEIGHTS = 16 * 2

        @block.sync
        def _(sp):
            sp.dma_start(a[:, :, :], a_log.rearrange("(a p) s -> p a s", p=P)).then_inc(weights, 16)
            sp.dma_start(skip[:, :], d_skip).then_inc(weights, 16)
            rows = lambda d: slice(d * P, (d + 1) * P)

            def load_block(b, d):
                for tile, source in ((dt, dt_in), (dtx, dtx_in), (xc, xc_in)):
                    sp.dma_start(tile[d % 2][:, :], source[b, rows(d), :]).then_inc(block_loaded[d % 2], 16)

            def load_b(b, n):
                sp.dma_start(bb[n][:, :, :], b_in[b, n * QS:(n + 1) * QS, :].unsqueeze(0).to_broadcast([P, QS, T]))\
                    .then_inc(b_loaded[n], 16)

            def load_c(b, u):
                sp.dma_start(c[u][0:3 * NS, :], c_parts[b].rearrange("a s t -> (a s) t")).then_inc(c_loaded[u], 16)

            sp.wait_ge(c_zeroed, 1)
            load_c(0, 0)
            load_c(1, 1)
            load_block(0, 0)
            for n in range(NS // QS):
                load_b(0, n)
            load_block(0, 1)

            def batch(b, u, i, last):
                for d in range(DB):
                    if d == DB - 1 and not last:
                        for n in range(NS // QS):
                            sp.wait_ge(in_ready, STEPS * b + d * NS + (n + 1) * QS)
                            load_b(b + 1, n)
                    sp.wait_ge(y_ready, 1 + DB * b + d + 1)
                    sp.dma_start(yT[b, rows(d), :], y[:, :]).then_inc(y_stored, 16)
                    if not (last and d >= DB - 2):
                        load_block(b + (d + 2) // DB, (d + 2) % DB)

            def more_c(b, u):
                sp.wait_ge(c_wide, STEPS * (b + 1))
                load_c(b + 2, u)

            with sp.Fori(0, NB // 2 - 1) as i:
                for u in range(2):
                    batch(2 * i + u, u, i, False)
                    more_c(2 * i + u, u)
            for u in range(2):
                batch(NB - 2 + u, u, NB // 2 - 1, u == 1)
            sp.wait_ge(y_stored, 16 * (NB * DB + 1))

        @block.gpsimd
        def _(pool):
            for n in range(2):
                last_m = nc.gpsimd.memset(c[n][:, :], 0.0)
            last_m.then_inc(c_zeroed, 1)
            make_identity(nc, pool, ident, zeroed, ident_ready)
            nc.gpsimd.memset(pick_f[:, :, :], 0.0).then_inc(pick_steps, 1)
            for part in range(3):
                pool.wait_ge(pick_steps, part + 1)
                nc.gpsimd.affine_select(out=pick_f[:, :, :], in_=pick_f[:, :, :], compare_op=ALU.not_equal,
                                        fill=1.0, base=-part * NS, pattern=[[-1, NS], [0, P]],
                                        channel_multiplier=1).then_inc(pick_steps, 1)
            pool.wait_ge(pick_steps, 4)
            nc.gpsimd.tensor_copy(pick[:, :, :], pick_f[:, :, :]).then_inc(pick_steps, 1)

            def batch(b, u, i, last):
                for n in range(STEPS):
                    d, s = n // NS, n % NS
                    if s == 0:
                        pool.wait_ge(block_loaded[d % 2], 48 * (DB // 2 * b + d // 2 + 1))
                    if d == 0 and s % QS == 0:
                        pool.wait_ge(b_loaded[s // QS], 16 * (b + 1))
                    pool.wait_ge(scanned, STEPS * b + n + 1)
                    nc.gpsimd.tensor_tensor(ins[n % NU][:, :], dtx[d % 2][:, :], bb[s // QS][:, s % QS, :],
                                            ALU.mult).then_inc(in_ready, 1)

            each_batch(pool, 2, batch)

        @block.vector
        def _(dve):
            dve.sem_inc(scanned, NU)
            dve.sem_inc(hc_ready, 2)
            dve.sem_inc(y_ready, 1)
            dve.wait_ge(a_steps, 1)
            nc.vector.tensor_scalar(a[:, :, :], a[:, :, :], -1.0, None, ALU.mult).then_inc(a_steps, 1)

            def batch(b, u, i, last):
                def recur(n):
                    dve.wait_ge(decay_ready, STEPS * b + n + 1)
                    dve.wait_ge(in_ready, STEPS * b + n + 1)
                    dve.wait_ge(hc_ready, STEPS * b + n + 1)
                    nc.vector.tensor_tensor_scan(h[n % 2][:, :], psA[n % 2][:, :], ins[n % NU][:, :],
                                                 0.0, ALU.mult, ALU.add).then_inc(scanned, 1)

                def weigh(n):
                    dve.wait_ge(c_wide, STEPS * b + n + 1)
                    dve.wait_ge(scanned, NU + STEPS * b + n + 1)
                    dve.wait_ge(summed, STEPS * b + n + 1)
                    nc.vector.tensor_tensor(hc[n % NGB][:, :], h[n % 2][:, :], psC[:, :], ALU.mult)\
                        .then_inc(hc_ready, 1)

                def finish(d):
                    dve.wait_ge(summed, NGB + STEPS * b + (d + 1) * NS)
                    dve.wait_ge(block_loaded[d % 2], 48 * (DB // 2 * b + d // 2 + 1))
                    dve.wait_ge(y_stored, 16 * (DB * b + d + 1))
                    nc.vector.scalar_tensor_tensor(y[:, :], xc[d % 2][:, :], skip[:, d:d + 1], psY[:, :],
                                                   ALU.mult, ALU.add).then_inc(y_ready, 1)

                recur(0)
                for n in range(STEPS):
                    if n + 1 < STEPS:
                        recur(n + 1)
                    weigh(n)
                    if n % NS == 0 and n > 0:
                        finish(n // NS - 1)
                finish(DB - 1)

            each_batch(dve, 2, batch)

        @block.scalar
        def _(act):
            act.sem_inc(summed, NGB)
            act.sem_inc(y_stored, 16)
            act.wait_ge(weights, WEIGHTS)
            nc.scalar.activation(a[:, :, :], a[:, :, :], ACT.Exp).then_inc(a_steps, 1)
            act.wait_ge(a_steps, 2)

            def batch(b, u, i, last):
                for n in range(STEPS):
                    d, s = n // NS, n % NS
                    if s == 0:
                        act.wait_ge(block_loaded[d % 2], 48 * (DB // 2 * b + d // 2 + 1))
                    act.wait_ge(scanned, STEPS * b + n + NU - 1)
                    nc.scalar.activation(psA[n % 2][:, :], dt[d % 2][:, :], ACT.Exp, scale=a[:, d, s:s + 1])\
                        .then_inc(decay_ready, 1)

            each_batch(act, 2, batch)

        @block.tensor
        def _(pe):
            pe.wait_ge(ident_ready, 1)
            pe.wait_ge(pick_steps, 5)

            def batch(b, u, i, last):
                def widen(n):
                    if n == 0:
                        pe.wait_ge(c_loaded[u], 16 * (i + 1))
                    pe.wait_ge(hc_ready, 2 + STEPS * b + n)
                    for half in range(2):
                        mm = nc.tensor.matmul(psC[:, half * HALF:(half + 1) * HALF], pick[:, n % NS, :],
                                              c[u][:, half * HALF:(half + 1) * HALF], start=True, stop=True)
                    mm.then_inc(c_wide, 1)

                def add(n):
                    s = n % NS
                    pe.wait_ge(hc_ready, 2 + STEPS * b + n + 1)
                    if s == 0:
                        pe.wait_ge(y_ready, 1 + DB * b + n // NS)
                    for half in range(2):
                        cols = slice(half * HALF, (half + 1) * HALF)
                        mm = nc.tensor.matmul(psY[:, cols], ident[:, :], hc[n % NGB][:, cols], start=s == 0,
                                              stop=s == NS - 1)
                    mm.then_inc(summed, 1)

                for n in range(STEPS):
                    widen(n)
                    if n > 0:
                        add(n - 1)
                add(STEPS - 1)

            each_batch(pe, 2, batch)


def hybrid_block(nc, a):
    def dram(name, shape, dt=F32):
        return nc.dram_tensor(name, shape, dt).ap()

    qk_parts = dram("qk_parts", [NB, 2, 3, D, T], BF16)
    v_ones = dram("v_ones", [NB, P, TT * NH * VW])
    max_scratch = dram("max_scratch", [NG, P, 3 * 32], BF16)
    attnT = dram("attnT", [NB, D, T])
    x2 = dram("x2", [NB, T, D])
    xc, dt, dtx, yT = (dram(n, [NB, DI, T]) for n in ("xc", "dt", "dtx", "yT"))
    b_rows = dram("b_rows", [NB, NS, T])
    c_parts = dram("c_parts", [NB, 3, NS, T], BF16)
    ffn = [a[n] for n in ("win", "b_in", "w1", "b1", "w2", "b2", "wout", "bout")]

    project_qkv(nc, a["x"], a["wq"], a["wk_b"], a["wkv_aT"], a["wv_bT"], a["turnT"], qk_parts, v_ones)
    attention(nc, qk_parts, v_ones, max_scratch, attnT)
    residual_ffn(nc, "ffn1", a["x"], attnT, a["woT"], *ffn, x2)
    project_scan(nc, x2, a["x_wT"], a["dt_wT"], a["dt_b"], a["bc_wT"], a["conv_w"], a["conv_b"],
                 xc, dt, dtx, b_rows, c_parts)
    scan(nc, xc, dt, dtx, b_rows, c_parts, a["a_log"], a["d_skip"], yT)
    residual_ffn(nc, "ffn2", x2, yT, a["out_wT"], *ffn, a["out"])


def head_turns():
    inv = (np.float32(1.0) / np.float32(10000.0) ** (np.arange(0, HD, 2, dtype=np.float32) / np.float32(HD)))
    angle = np.arange(NH, dtype=np.float32)[:, None] * inv.astype(np.float32)[None, :]
    cos, sin = np.cos(angle), np.sin(angle)
    turn = np.zeros((D, D), np.float32)
    even = np.arange(0, D, 2)
    turn[even, even] = turn[even + 1, even + 1] = cos.reshape(-1)
    turn[even, even + 1] = -sin.reshape(-1)
    turn[even + 1, even] = sin.reshape(-1)
    return np.stack([turn[c * P:(c + 1) * P, c * P:(c + 1) * P].T for c in range(CB)])


def kernel(**inputs):
    import concourse.bacc as bacc
    from concourse.bass_utils import run_bass_kernel_spmd

    w = {k.split("_", 1)[1]: np.asarray(v) for k, v in inputs.items()}
    by_block = lambda v: v.reshape(-1, P).T
    arrays = {
        "x": w["attn_a_x"], "wq": w["attn_a_wq"], "wk_b": w["attn_a_wk_b"],
        "wkv_aT": np.concatenate([w["attn_a_wk_a"].T, w["attn_a_wv_a"].T], axis=1),
        "wv_bT": w["attn_a_wv_b"].T, "woT": w["attn_a_wo"].T, "turnT": head_turns(),
        "win": w["ffn_Win"], "b_in": w["ffn_bin_"], "w1": w["ffn_W1"], "b1": w["ffn_b1"],
        "w2": w["ffn_W2"], "b2": w["ffn_b2"], "wout": w["ffn_Wout"], "bout": w["ffn_bout"],
        "x_wT": w["attn_b_x_proj_w"].T, "dt_wT": w["attn_b_dt_proj_w"].T,
        "dt_b": by_block(w["attn_b_dt_proj_b"]),
        "bc_wT": np.concatenate([w["attn_b_B_proj_w"].T, w["attn_b_C_proj_w"].T], axis=1),
        "conv_w": w["attn_b_conv_w"].reshape(DI, TAPS), "conv_b": by_block(w["attn_b_conv_b"]),
        "a_log": w["attn_b_A_log"], "d_skip": by_block(w["attn_b_D"]),
        "out_wT": w["attn_b_out_proj_w"].T,
    }
    arrays = {k: np.ascontiguousarray(v) for k, v in arrays.items()}
    nc = bacc.Bacc("TRN2", target_bir_lowering=False, num_devices=1)
    args = {k: nc.dram_tensor(k, v.shape, mybir.dt.from_np(v.dtype), kind="ExternalInput").ap()
            for k, v in arrays.items()}
    args["out"] = nc.dram_tensor("out", (NB, T, D), F32, kind="ExternalOutput").ap()
    hybrid_block(nc, args)
    return run_bass_kernel_spmd(nc, [arrays], core_ids=[0]).results[0]["out"]
```

```python
import numpy as np
import concourse.bass as bass
from concourse import mybir
from contextlib import ExitStack

F32 = mybir.dt.float32
BF16 = mybir.dt.bfloat16
ALU = mybir.AluOpType
ACT = mybir.ActivationFunctionType
AX = mybir.AxisListType

P = 128
NB, T, D = 8, 1024, 256
NH, HD = 16, 16
LAT = 64
DI, NS, TAPS = 512, 16, 4
M, INNER = 64, 16
EPS = 1e-5

TT = T // P
CB = D // P
DB = DI // P
HALF = 512
PAIR = 2 * HALF
NG, GH = 4, 4
SLOTS = 6
ROWS = SLOTS * HD
VW = 32
Q_PARTS = (0, 0, 0, 1, 1, 2)
K_PARTS = (0, 1, 2, 0, 1, 0)


def each_batch(eng, unroll, body):
    turns = (NB - 1) // unroll
    with eng.Fori(0, turns) as i:
        for u in range(unroll):
            body(i * unroll + u, u, i, NB - turns * unroll)
    for b in range(turns * unroll, NB):
        body(b, b % unroll, b // unroll, NB - 1 - b)


class Stage:

    def __init__(self, nc, ctx, name):
        self.nc, self.ctx, self.name = nc, ctx, name
        self.sems = []
        ctx.callback(self.end)

    def end(self):
        self.nc.clear_and_free_semaphores(self.sems)
        self.nc.all_engine_barrier()

    def sb(self, name, shape, dt=F32):
        return self.ctx.enter_context(self.nc.sbuf_tensor(f"{self.name}_{name}", shape, dt))

    def ps(self, name, shape):
        return self.ctx.enter_context(self.nc.psum_tensor(f"{self.name}_{name}", shape, F32))

    def sem(self, name):
        self.sems.append(self.nc.alloc_semaphore(name=f"{self.name}_{name}"))
        return self.sems[-1]


def stand(eng, passed):
    eng.sem_inc(passed, 1)


def make_identity(nc, pool, ident, zeroed, ready):
    nc.gpsimd.memset(ident[:, :], 0.0).then_inc(zeroed, 1)
    pool.wait_ge(zeroed, 1)
    nc.gpsimd.affine_select(out=ident[:, :], in_=ident[:, :], compare_op=ALU.not_equal, fill=1.0,
                            base=0, pattern=[[-1, P]], channel_multiplier=1).then_inc(ready, 1)


class Norm:

    def __init__(self, st, buffers=2):
        self.buffers = buffers
        self.stats = st.sb("stats", [P, TT, 6])
        self.mv = [st.sb(f"mean_var{u}", [P, TT, 2]) for u in range(buffers)]
        self.var_eps = st.sb("var_eps", [P, TT])
        self.neg_mean = st.sb("neg_mean", [P, TT])
        self.rstd = st.sb("rstd", [P, TT])
        self.exponent = st.sb("exponent", [P, TT])
        self.xn = [st.sb(f"xn{u}", [P, TT, D]) for u in range(buffers)]
        self.stats_done = st.sem("stats_done")
        self.mv_ready = st.sem("mean_var_ready")
        self.rstd_steps = st.sem("rstd_steps")
        self.xn_ready = st.sem("xn_ready")
        self.transposed = st.sem("transposed")
        self.exponent_set = st.sem("exponent_set")
        self.pool_passed = st.sem("pool_passed")
        self.dve_passed = st.sem("dve_passed")

    def setup(self, nc, pool):
        pool.sem_inc(self.transposed, self.buffers * CB)
        pool.sem_inc(self.mv_ready, 1)
        pool.sem_inc(self.xn_ready, 1)
        nc.gpsimd.memset(self.exponent[:, :], -0.5).then_inc(self.exponent_set, 1)

    def vector(self, nc, dve, b, u, x):
        dve.wait_ge(self.mv_ready, b + 1)
        for t in range(TT):
            last = nc.vector.bn_stats(self.stats[:, t, :], x[:, t, :])
        last.then_inc(self.stats_done, 1)
        dve.wait_ge(self.stats_done, b + 1)
        dve.wait_ge(self.transposed, CB * (b + 1))
        stand(dve, self.dve_passed)
        for t in range(TT):
            last = nc.vector.bn_aggr(self.mv[u][:, t, :], self.stats[:, t, :])
        last.then_inc(self.mv_ready, 1)

    def gpsimd(self, nc, pool, b, u, x):
        mv = self.mv[u]
        pool.wait_ge(self.exponent_set, 1)
        pool.wait_ge(self.xn_ready, b + 1)
        pool.wait_ge(self.mv_ready, b + 2)
        stand(pool, self.pool_passed)
        nc.gpsimd.tensor_scalar(self.var_eps[:, :], mv[:, :, 1], 1.0, EPS, ALU.mult, ALU.add)\
            .then_inc(self.rstd_steps, 1)
        nc.gpsimd.tensor_scalar(self.neg_mean[:, :], mv[:, :, 0], -1.0, 0.0, ALU.mult, ALU.add)\
            .then_inc(self.rstd_steps, 1)
        pool.wait_ge(self.rstd_steps, 3 * b + 2)
        nc.gpsimd.tensor_tensor(self.rstd[:, :], self.var_eps[:, :], self.exponent[:, :], ALU.pow)\
            .then_inc(self.rstd_steps, 1)
        pool.wait_ge(self.rstd_steps, 3 * b + 3)
        pool.wait_ge(self.transposed, CB * (b + 1))
        stand(pool, self.pool_passed)
        for t in range(TT):
            last = nc.gpsimd.tensor_scalar(self.xn[u][:, t, :], x[:, t, :], self.neg_mean[:, t:t + 1],
                                           self.rstd[:, t:t + 1], ALU.add, ALU.mult)
        last.then_inc(self.xn_ready, 1)

    def tensor(self, nc, pe, b, u, ident, banks, free):
        pe.wait_ge(self.xn_ready, b + 2)
        for c in range(CB):
            free(c)
            for t in range(TT):
                last = nc.tensor.transpose(banks[c][:, t * P:(t + 1) * P],
                                           self.xn[u][:, t, c * P:(c + 1) * P], ident[:, :])
            last.then_inc(self.transposed, 1)

    def wait_transposed(self, eng, b, c):
        eng.wait_ge(self.transposed, CB * (self.buffers + b) + c + 1)


def project_qkv(nc, x, wq, wk_b, wkv_aT, wv_bT, turnT, qk_parts, v_ones):
    T0, T1, LATENT, Q0, Q1, K0, K1, V0, V1 = range(9)
    JOBS, PRODUCTS = 9, 7
    PAIR_OF = {T0: 0, T1: 1, LATENT: 2, Q0: 3, Q1: 0, K0: 1, K1: 2, V0: 3, V1: 1}
    BEFORE = {T0: Q1, T1: V1, LATENT: K1, Q0: V0, Q1: T0, K0: T1, K1: LATENT, V0: Q0, V1: K0}
    QK = (Q0, Q1, K0, K1)

    with ExitStack() as ctx:
        st = Stage(nc, ctx, "qkv")
        xt = [st.sb(f"x{u}", [P, TT, D]) for u in range(2)]
        norm = Norm(st)
        xnT = st.sb("xnT", [P, CB, T])
        latent = st.sb("latent", [P, T])
        parts = [st.sb(f"parts{u}", [P, len(QK), 3, T], BF16) for u in range(2)]
        rest = st.sb("rest", [P, len(QK), T])
        v = [st.sb(f"v{u}", [P, TT, NH, VW]) for u in range(2)]
        ident = st.sb("ident", [P, P])
        wq_n = st.sb("wq", [P, CB, D])
        wkb_n = st.sb("wk_b", [P, CB, LAT])
        turn = st.sb("turn", [P, CB, P])
        wqT = st.sb("wqT", [P, CB, D])
        wkbT = st.sb("wk_bT", [P, D])
        wvbT = st.sb("wv_bT", [P, D])
        wkvaT = st.sb("wkv_aT", [P, CB, P])
        ps = [st.ps(f"p{i}", [P, PAIR]) for i in range(4)]

        weights = st.sem("weights")
        x_loaded = [st.sem(f"x_loaded{u}") for u in range(2)]
        zeroed = st.sem("zeroed")
        ident_ready = st.sem("ident_ready")
        pads_ready = st.sem("pads_ready")
        ones_ready = st.sem("ones_ready")
        turned = st.sem("turned")
        turned_copied = st.sem("turned_copied")
        product = st.sem("product")
        act_read = st.sem("act_read")
        rest_ready = st.sem("rest_ready")
        mid_ready = st.sem("mid_ready")
        parts_ready = st.sem("parts_ready")
        parts_stored = [st.sem(f"parts_stored{u}") for u in range(2)]
        v_stored = [st.sem(f"v_stored{u}") for u in range(2)]
        pool_passed = norm.pool_passed
        block = ctx.enter_context(nc.Block())
        WEIGHTS = 16 * 5

        @block.sync
        def _(sp):
            sp.dma_start(xt[0][:, :, :], x[0].rearrange("(t p) c -> p t c", p=P)).then_inc(x_loaded[0], 16)
            sp.dma_start(wq_n[:, :, :], wq.rearrange("(a p) c -> p a c", p=P)).then_inc(weights, 16)
            sp.dma_start(wkb_n[:, :, :], wk_b.rearrange("(a p) c -> p a c", p=P)).then_inc(weights, 16)
            sp.dma_start(turn[:, :, :], turnT.rearrange("a p c -> p a c")).then_inc(weights, 16)
            sp.dma_start(wkvaT[:, :, :], wkv_aT.rearrange("(a p) c -> p a c", p=P)).then_inc(weights, 16)
            sp.wait_ge(pads_ready, 1)
            sp.dma_start(wvbT[LAT:P, :], wv_bT).then_inc(weights, 16)
            sp.dma_start(xt[1][:, :, :], x[1].rearrange("(t p) c -> p t c", p=P)).then_inc(x_loaded[1], 16)

            def batch(b, u, i, left):
                if left > 1:
                    sp.wait_ge(norm.xn_ready, b + 2)
                    sp.dma_start(xt[u][:, :, :], x[b + 2].rearrange("(t p) c -> p t c", p=P)).then_inc(x_loaded[u], 16)
                for k in range(len(QK)):
                    sp.wait_ge(parts_ready, 4 + 4 * b + k + 1)
                    sp.dma_start(qk_parts[b, k // 2, :, (k % 2) * P:(k % 2 + 1) * P, :].rearrange("a p t -> p a t"),
                                 parts[u][:, k, :, :]).then_inc(parts_stored[u], 16)
                sp.wait_ge(act_read, JOBS + JOBS * b + V1 + 1)
                sp.dma_start(v_ones[b], v[u][:, :, :, :].rearrange("p t h w -> p (t h w)")).then_inc(v_stored[u], 16)

            each_batch(sp, 2, batch)
            for u in range(2):
                sp.wait_ge(parts_stored[u], 64 * (NB // 2 + 1))
                sp.wait_ge(v_stored[u], 16 * (NB // 2 + 1))

        @block.gpsimd
        def _(pool):
            nc.gpsimd.memset(wvbT[:, :], 0.0)
            nc.gpsimd.memset(wkbT[:, :], 0.0).then_inc(pads_ready, 1)
            pool.sem_inc(parts_ready, 4)
            norm.setup(nc, pool)
            make_identity(nc, pool, ident, zeroed, ident_ready)
            pool.wait_ge(x_loaded[0], 16)
            norm.gpsimd(nc, pool, 0, 0, xt[0])

            def batch(b, u, i, left):
                if left:
                    pool.wait_ge(x_loaded[1 - u], 16 * (i + 1 + u))
                    norm.gpsimd(nc, pool, b + 1, 1 - u, xt[1 - u])
                for k in range(len(QK)):
                    pool.wait_ge(rest_ready, 4 + 4 * b + k + 1)
                    pool.wait_ge(parts_stored[u], 64 * (i + 1))
                    stand(pool, pool_passed)
                    nc.gpsimd.tensor_scalar(parts[u][:, k, 1, :], rest[:, k, :], 1.0, 0.0, ALU.mult, ALU.add)\
                        .then_inc(mid_ready, 1)
                    pool.wait_ge(mid_ready, 4 * b + k + 1)
                    nc.gpsimd.tensor_tensor(parts[u][:, k, 2, :], rest[:, k, :], parts[u][:, k, 1, :], ALU.subtract)\
                        .then_inc(parts_ready, 1)

            each_batch(pool, 2, batch)

        @block.vector
        def _(dve):
            dve.sem_inc(rest_ready, 4)
            for u in range(2):
                last = nc.vector.memset(v[u][:, :, :, HD:VW], 1.0)
            last.then_inc(ones_ready, 1)
            dve.wait_ge(x_loaded[0], 16)
            norm.vector(nc, dve, 0, 0, xt[0])

            def batch(b, u, i, left):
                if left:
                    dve.wait_ge(x_loaded[1 - u], 16 * (i + 1 + u))
                    norm.vector(nc, dve, b + 1, 1 - u, xt[1 - u])
                for k, job in enumerate(QK):
                    dve.wait_ge(act_read, JOBS + JOBS * b + job + 1)
                    dve.wait_ge(parts_ready, 4 * b + k + 1 + 0)
                    nc.vector.tensor_tensor(rest[:, k, :], ps[PAIR_OF[job]][:, :], parts[u][:, k, 0, :], ALU.subtract)\
                        .then_inc(rest_ready, 1)

            each_batch(dve, 2, batch)

        @block.scalar
        def _(act):
            act.sem_inc(act_read, JOBS)
            for u in range(2):
                act.sem_inc(parts_stored[u], 64)
                act.sem_inc(v_stored[u], 16)
            act.wait_ge(pads_ready, 1)
            for c in range(CB):
                act.wait_ge(turned, c + 1)
                nc.scalar.activation(wqT[:, c, :], ps[c][:, 0:D], ACT.Copy).then_inc(turned_copied, 1)
            act.wait_ge(turned, 3)
            nc.scalar.activation(wkbT[0:LAT, :], ps[2][0:LAT, 0:D], ACT.Copy).then_inc(turned_copied, 1)
            act.wait_ge(ones_ready, 1)

            def batch(b, u, i, left):
                def read(job, out, in_):
                    if job in (T0, T1):
                        norm.wait_transposed(act, b, job - T0)
                    else:
                        act.wait_ge(product, PRODUCTS * b + job - LATENT + 1)
                    nc.scalar.activation(out, in_, ACT.Copy).then_inc(act_read, 1)

                for job in (T0, T1):
                    read(job, xnT[:, job - T0, :], ps[PAIR_OF[job]][:, :])
                read(LATENT, latent[:, :], ps[PAIR_OF[LATENT]][:, :])
                act.wait_ge(parts_stored[u], 64 * (i + 1))
                for k, job in enumerate(QK):
                    read(job, parts[u][:, k, 0, :], ps[PAIR_OF[job]][:, :])
                act.wait_ge(v_stored[u], 16 * (i + 1))
                for n, job in enumerate((V0, V1)):
                    read(job, v[u][:, 4 * n:4 * n + 4, :, 0:HD],
                         ps[PAIR_OF[job]][:, :].rearrange("p (t h d) -> p t h d", t=4, h=NH))

            each_batch(act, 2, batch)

        @block.tensor
        def _(pe):
            pe.wait_ge(weights, WEIGHTS)
            for c in range(CB):
                for f in range(CB):
                    last = nc.tensor.matmul(ps[c][:, f * P:(f + 1) * P], wq_n[:, f, c * P:(c + 1) * P],
                                            turn[:, f, :], start=True, stop=True)
                last.then_inc(turned, 1)
            for f in range(CB):
                last = nc.tensor.matmul(ps[2][0:LAT, f * P:(f + 1) * P], wkb_n[:, f, :], turn[:, f, :],
                                        start=True, stop=True)
            last.then_inc(turned, 1)
            pe.wait_ge(turned_copied, 3)
            pe.wait_ge(ident_ready, 1)

            def batch(b, u, i, left):
                def free(job):
                    old = BEFORE[job]
                    turn_ = b if old < job else b - 1
                    pe.wait_ge(act_read, JOBS + JOBS * turn_ + old + 1)
                    if old in QK:
                        pe.wait_ge(rest_ready, 4 + 4 * turn_ + QK.index(old) + 1)

                norm.tensor(nc, pe, b, u, ident, (ps[PAIR_OF[T0]], ps[PAIR_OF[T1]]), lambda c: free(T0 + c))

                def project(job, weight, source, blocks):
                    free(job)
                    for h in range(2):
                        for c in range(blocks):
                            last_m = nc.tensor.matmul(ps[PAIR_OF[job]][:, h * HALF:(h + 1) * HALF], weight(c),
                                                      source(c, h), start=c == 0, stop=c == blocks - 1)
                    last_m.then_inc(product, 1)

                half = lambda c, h: xnT[:, c, h * HALF:(h + 1) * HALF]
                pe.wait_ge(act_read, JOBS + JOBS * b + T1 + 1)
                project(LATENT, lambda c: wkvaT[:, c, :], half, CB)
                for f in range(CB):
                    project(Q0 + f, lambda c: wqT[:, c, f * P:(f + 1) * P], half, CB)
                pe.wait_ge(act_read, JOBS + JOBS * b + LATENT + 1)
                for f in range(CB):
                    project(K0 + f, lambda c: wkbT[:, f * P:(f + 1) * P],
                            lambda c, h: latent[:, h * HALF:(h + 1) * HALF], 1)
                for n, job in enumerate((V0, V1)):
                    free(job)
                    for t in range(4):
                        last_m = nc.tensor.matmul(ps[PAIR_OF[job]][:, t * D:(t + 1) * D],
                                                  latent[:, (4 * n + t) * P:(4 * n + t + 1) * P], wvbT[:, :],
                                                  start=True, stop=True)
                    last_m.then_inc(product, 1)

            each_batch(pe, 2, batch)


def attention(nc, qk_parts, v_ones, max_scratch, valuesT, sums_out):
    LEAD = 3
    UNITS = GH * TT
    STEPS = 2 * TT
    BANK = (0, 1, 2, 0)
    SINCE = (1, 4, 4, 3)
    FULL = ROWS + 3
    SCALE = float(HD) ** -0.5

    with ExitStack() as ctx:
        st = Stage(nc, ctx, "attn")
        q = [st.sb(f"q{g}", [FULL, GH, T], BF16) for g in range(NG)]
        k = [st.sb(f"k{g}", [FULL, GH, T], BF16) for g in range(NG)]
        v = [st.sb(f"v{g}", [P, TT, GH * VW]) for g in range(NG)]
        probs = [st.sb(f"probs{i}", [P, GH, HALF]) for i in range(2)]
        maxima = [st.sb(f"maxima{i}", [P, UNITS]) for i in range(2)]
        maxT = [st.sb(f"maxT{i}", [P, 32]) for i in range(2)]
        max_rest = st.sb("max_rest", [P, 32])
        max_parts = [st.sb(f"max_parts{i}", [P, 3, 32], BF16) for i in range(2)]
        out = [st.sb(f"out{i}", [P, 2, HALF]) for i in range(2)]
        psT = [st.ps(f"scoresT{i}", [P, HALF]) for i in range(3)]
        psM = [st.ps(f"scores{i}", [P, PAIR]) for i in range(2)]
        psO = st.ps("out_sum", [P, HALF])

        qk_loaded = [st.sem(f"qk_loaded{g}") for g in range(NG)]
        v_loaded = [st.sem(f"v_loaded{g}") for g in range(NG)]
        ones_ready = st.sem("ones_ready")
        scores_ready = st.sem("scores_ready")
        maxima_read = st.sem("maxima_read")
        maxT_ready = st.sem("maxT_ready")
        max_steps = st.sem("max_steps")
        max_stored = st.sem("max_stored")
        max_loaded = [st.sem(f"max_loaded{g}") for g in range(NG)]
        scoresT_ready = st.sem("scoresT_ready")
        exps_done = st.sem("exps_done")
        pv_done = st.sem("pv_done")
        out_copied = st.sem("out_copied")
        out_stored = [st.sem(f"out_stored{i}") for i in range(2)]
        pool_passed = st.sem("pool_passed")
        block = ctx.enter_context(nc.Block())
        LOADS = 16 * 2 * SLOTS
        STORES = 16 * (GH + 1)

        @block.sync
        def _(sp):
            def load(b, g):
                for tile, which, slots in ((q, 0, Q_PARTS), (k, 1, K_PARTS)):
                    for s, part in enumerate(slots):
                        heads = qk_parts[b, which, part, g * GH * HD:(g + 1) * GH * HD, :]
                        sp.dma_start(tile[g][s * HD:(s + 1) * HD, :, :],
                                     heads.rearrange("(h d) t -> d h t", d=HD)).then_inc(qk_loaded[g], 16)
                sp.dma_start(v[g][:, :, :], v_ones[b].rearrange("p (t w) -> p t w", t=TT)
                             [:, :, g * GH * VW:(g + 1) * GH * VW]).then_inc(v_loaded[g], 16)

            def max_rows(b, g, n):
                sp.wait_ge(max_steps, 4 * (n + 1))
                sp.dma_start(max_scratch[g], max_parts[g % 2][:, :, :].rearrange("p a r -> p (a r)"))\
                    .then_inc(max_stored, 16)
                sp.wait_ge(max_stored, 16 * (n + 1))
                for a in range(3):
                    sp.dma_start(q[g][ROWS + a:ROWS + a + 1, :, :].rearrange("o h (t q r) -> o (h t) q r", q=4, r=32),
                                 max_scratch[g][:, a * 32:(a + 1) * 32].rearrange("(o q c) r -> o c q r", o=1, q=4))\
                        .then_inc(max_loaded[g], 16)

            for g in range(NG):
                load(0, g)
            max_rows(0, 0, 0)

            def batch(b, u, i, left):
                for g in range(NG):
                    n = NG * b + g
                    if left or g < NG - 1:
                        max_rows(b, (g + 1) % NG, n + 1)
                    if left:
                        sp.wait_ge(pv_done, 2 + STEPS * (n + 1))
                        load(b + 1, g)
                    sp.wait_ge(out_copied, 1 + 2 * (n + 1))
                    done = out[g % 2][:, :, :].rearrange("p a t -> p (a t)")
                    for h in range(GH):
                        row = g * GH * HD + h * HD
                        sp.dma_start(valuesT[b, row:row + HD, :], done[h * VW:h * VW + HD, :])\
                            .then_inc(out_stored[g % 2], 16)
                    sp.dma_start(sums_out[b, g * GH:(g + 1) * GH, :], done[HD:P:VW, :]).then_inc(out_stored[g % 2], 16)

            each_batch(sp, 1, batch)
            for i in range(2):
                sp.wait_ge(out_stored[i], STORES * (NB * NG // 2 + 1))

        @block.gpsimd
        def _(pool):
            for g in range(NG):
                last_m = nc.gpsimd.memset(k[g][ROWS:FULL, :, :], 1.0)
            last_m.then_inc(ones_ready, 1)

            def split(g, n):
                i = g % 2
                pool.wait_ge(maxT_ready, n + 1)
                pool.wait_ge(max_steps, 4 * n)
                stand(pool, pool_passed)
                nc.gpsimd.tensor_scalar(max_parts[i][:, 0, :], maxT[i][:, :], 1.0, 0.0, ALU.mult, ALU.add)\
                    .then_inc(max_steps, 1)
                pool.wait_ge(max_steps, 4 * n + 1)
                nc.gpsimd.tensor_tensor(max_rest[:, :], maxT[i][:, :], max_parts[i][:, 0, :], ALU.subtract)\
                    .then_inc(max_steps, 1)
                pool.wait_ge(max_steps, 4 * n + 2)
                stand(pool, pool_passed)
                nc.gpsimd.tensor_scalar(max_parts[i][:, 1, :], max_rest[:, :], 1.0, 0.0, ALU.mult, ALU.add)\
                    .then_inc(max_steps, 1)
                pool.wait_ge(max_steps, 4 * n + 3)
                nc.gpsimd.tensor_tensor(max_parts[i][:, 2, :], max_rest[:, :], max_parts[i][:, 1, :], ALU.subtract)\
                    .then_inc(max_steps, 1)

            split(0, 0)

            def batch(b, u, i, left):
                for g in range(NG):
                    if left or g < NG - 1:
                        split((g + 1) % NG, NG * b + g + 1)

            each_batch(pool, 1, batch)

        @block.vector
        def _(dve):
            dve.sem_inc(maxima_read, 2)

            def unit(b, m):
                g, c = m // UNITS, m % UNITS
                n, i = NG * b + g, g % 2
                dve.wait_ge(scores_ready, UNITS * n + c + 1)
                if c == 0:
                    dve.wait_ge(maxT_ready, n)
                nc.vector.tensor_reduce(maxima[i][:, c:c + 1], psM[c % 2][:, :], AX.X, ALU.max, negate=True)\
                    .then_inc(maxima_read, 1)
                if c == UNITS - 1:
                    dve.wait_ge(maxima_read, 2 + UNITS * (n + 1))
                    nc.vector.transpose(maxT[i][:, :], maxima[i][:, :]).then_inc(maxT_ready, 1)

            for m in range(UNITS + 2 * LEAD):
                unit(0, m)

            def batch(b, u, i, left):
                for s in range(NG * STEPS):
                    for w in range(2):
                        m = UNITS + 2 * LEAD + 2 * s + w
                        if left or m < NG * UNITS:
                            unit(b, m)

            each_batch(dve, 1, batch)

        @block.scalar
        def _(act):
            act.sem_inc(exps_done, GH)
            act.sem_inc(out_copied, 1)
            for n in range(2):
                act.sem_inc(out_stored[n], STORES)

            def copy_out(b, g, half):
                n = NG * b + g
                act.wait_ge(pv_done, 2 + STEPS * n + TT * (half + 1))
                if half == 0:
                    act.wait_ge(out_stored[g % 2], STORES * (NG // 2 * b + g // 2 + 1))
                nc.scalar.activation(out[g % 2][:, half, :], psO[:, :], ACT.Copy).then_inc(out_copied, 1)

            def batch(b, u, i, left):
                for s in range(NG * STEPS):
                    if s % TT == 1 and s > 1:
                        copy_out(b, (s - TT) // STEPS, (s - TT) % STEPS // TT)
                    for h in range(GH):
                        act.wait_ge(scoresT_ready, GH * (NG * STEPS * b + s) + h + 1)
                        if h == 0:
                            act.wait_ge(pv_done, NG * STEPS * b + s + 1)
                        nc.scalar.activation(probs[s % 2][:, h, :], psT[BANK[h]][:, :], ACT.Exp, scale=SCALE)\
                            .then_inc(exps_done, 1)
                copy_out(b, NG - 1, 1)

            each_batch(act, 1, batch)

        @block.tensor
        def _(pe):
            pe.sem_inc(pv_done, 2)
            pe.wait_ge(ones_ready, 1)

            def unit_half(b, m, half):
                g, c = m // UNITS, m % UNITS
                n, g = NG * b + g, g % NG
                h, t = c // TT, c % TT
                if half == 0:
                    if c == 0:
                        pe.wait_ge(qk_loaded[g], LOADS * (b + 1 + m // (NG * UNITS)))
                    pe.wait_ge(maxima_read, UNITS * n + c + 1)
                mm = nc.tensor.matmul(psM[c % 2][:, half * HALF:(half + 1) * HALF],
                                      q[g][0:ROWS, h, t * P:(t + 1) * P],
                                      k[g][0:ROWS, h, half * HALF:(half + 1) * HALF], start=True, stop=True)
                if half == 1:
                    mm.then_inc(scores_ready, 1)

            def values(b, s):
                g, half, kt = s // STEPS, s % STEPS // TT, s % TT
                pe.wait_ge(exps_done, GH + GH * (NG * STEPS * b + s + 1))
                if kt == 0:
                    pe.wait_ge(out_copied, 2 * (NG * b + g) + half + 1)
                    pe.wait_ge(v_loaded[g], 16 * (b + 1))
                for h in range(GH):
                    mm = nc.tensor.matmul(psO[h * VW:(h + 1) * VW, :], v[g][:, kt, h * VW:(h + 1) * VW],
                                          probs[s % 2][:, h, :], start=kt == 0, stop=kt == TT - 1)
                mm.then_inc(pv_done, 1)

            for m in range(UNITS + 2 * LEAD):
                for half in range(2):
                    unit_half(0, m, half)

            def batch(b, u, i, left):
                for s in range(NG * STEPS):
                    g, half, kt = s // STEPS, s % STEPS // TT, s % TT
                    if s % STEPS == 0:
                        pe.wait_ge(max_loaded[g], 48 * (b + 1))
                    for h in range(GH):
                        pe.wait_ge(exps_done, GH + GH * (NG * STEPS * b + s) + h - SINCE[h] + 1)
                        nc.tensor.matmul(psT[BANK[h]][:, :], k[g][0:FULL, h, kt * P:(kt + 1) * P],
                                         q[g][0:FULL, h, half * HALF:(half + 1) * HALF], start=True, stop=True)\
                            .then_inc(scoresT_ready, 1)
                        m = UNITS + 2 * LEAD + 2 * s + h // 2
                        if left or m < NG * UNITS:
                            unit_half(b, m, h % 2)
                    if s > 0:
                        values(b, s - 1)
                values(b, NG * STEPS - 1)

            each_batch(pe, 1, batch)


def residual_ffn(nc, name, x_in, branchT, branch_w, win, b_in, w1, b1, w2, b2, wout, bout, x_out,
                 sums=None, recips=None):
    KB = branchT.shape[1] // P
    MIX0, MIX1, T0, T1, UNITS, OUT0, OUT1 = range(7)
    PAIR_OF = {MIX0: 0, MIX1: 1, T0: 2, T1: 3, UNITS: 2, OUT0: 3, OUT1: 2}
    BUF = 3
    RELUS = 4
    COPY_S = 12

    with ExitStack() as ctx:
        st = Stage(nc, ctx, name)
        xt = [st.sb(f"x{u}", [P, TT, D]) for u in range(BUF)]
        branch = [st.sb(f"branch{u}", [P, KB, T]) for u in range(BUF)]
        norm = Norm(st, BUF)
        xnT = st.sb("xnT", [P, CB, T])
        s = [st.sb(f"s{u}", [P, HALF]) for u in range(BUF)]
        hidden = [st.sb(f"hidden{i}", [P, HALF]) for i in range(RELUS)]
        g = st.sb("g", [P, HALF])
        ident = st.sb("ident", [P, P])
        bw = st.sb("branch_w", [P, KB, D])
        win_sb = st.sb("win", [P, CB, M])
        cols = st.sb("cols", [P, 2, 1])
        w1_sb, b1_sb, w2_sb = (st.sb(n, [P, INNER]) for n in ("w1", "b1", "w2"))
        wout_sb = [st.sb(f"wout{h}", [P, D]) for h in range(2)]
        bout_sb = st.sb("bout", [P, D])
        ps = [st.ps(f"p{i}", [P, PAIR]) for i in range(4)]
        if sums is not None:
            all_sums = st.sb("all_sums", [P, T])
            all_recips = st.sb("all_recips", [P, T])
            recip = [st.sb(f"recip{u}", [P, KB, T]) for u in range(BUF)]
            sums_loaded = st.sem("sums_loaded")
            recips_ready = st.sem("recips_ready")
            recips_stored = st.sem("recips_stored")
            scaled = st.sem("scaled")

        weights = st.sem("weights")
        pads_ready = st.sem("pads_ready")
        zeroed = st.sem("zeroed")
        ident_ready = st.sem("ident_ready")
        x_loaded = [st.sem(f"x_loaded{u}") for u in range(BUF)]
        branch_loaded = [st.sem(f"branch_loaded{u}") for u in range(BUF)]
        x_stored = [st.sem(f"x_stored{u}") for u in range(BUF)]
        mixed = st.sem("mixed")
        added = st.sem("added")
        copied = st.sem("copied")
        units_ready = st.sem("units_ready")
        biased = st.sem("biased")
        relu_ready = st.sem("relu_ready")
        summed = st.sem("summed")
        out_ready = st.sem("out_ready")
        x_ready = st.sem("x_ready")
        block = ctx.enter_context(nc.Block())
        WEIGHTS = 16 * (3 + 10 + 2)
        HEADS = P // HD
        BRANCH_LOADS = 16 * (1 + (KB * HEADS if sums is not None else 0))
        tokens = lambda a: a.rearrange("(t p) c -> p t c", p=P)

        def ahead(u, i, n):
            return (u + n) % BUF, i + (u + n) // BUF

        @block.sync
        def _(sp):
            def load_x(b, u):
                sp.dma_start(xt[u][:, :, :], tokens(x_in[b])).then_inc(x_loaded[u], 16)

            def load_branch(b, u):
                sp.dma_start(branch[u][:, :, :], branchT[b].rearrange("(a p) t -> p a t", p=P))\
                    .then_inc(branch_loaded[u], 16)

            def load_recips(b, u):
                if sums is not None:
                    for c in range(KB):
                        for h in range(HEADS):
                            row = c * HEADS + h
                            sp.dma_start(recip[u][h * HD:(h + 1) * HD, c, :],
                                         recips[b, row:row + 1, :].to_broadcast([HD, T])).then_inc(branch_loaded[u], 16)

            if sums is not None:
                sp.dma_start(all_sums[:, :], sums.rearrange("b h t -> (b h) t")).then_inc(sums_loaded, 16)
            sp.dma_start(bw[:, :, :], branch_w.rearrange("(a p) c -> p a c", p=P)).then_inc(weights, 16)
            load_branch(0, 0)
            load_x(0, 0)
            sp.dma_start(win_sb[:, :, :], win.rearrange("(a p) c -> p a c", p=P)).then_inc(weights, 16)
            sp.dma_start(bout_sb[:, :], bout.rearrange("(o c) -> o c", o=1).to_broadcast([P, D])).then_inc(weights, 16)
            for h in range(2):
                rows = slice(h * M, (h + 1) * M)
                for tile, w in ((w1_sb, w1), (b1_sb, b1), (w2_sb, w2)):
                    sp.dma_start(tile[rows, :], w).then_inc(weights, 16)
                for n, w in enumerate((b_in, b2)):
                    sp.dma_start(cols[rows, n, :], w.rearrange("(m o) -> m o", o=1)).then_inc(weights, 16)
            sp.wait_ge(pads_ready, 1)
            for h in range(2):
                sp.dma_start(wout_sb[h][h * M:(h + 1) * M, :], wout).then_inc(weights, 16)
            load_branch(1, 1)
            load_x(1, 1)
            if sums is not None:
                sp.wait_ge(recips_ready, 1)
                sp.dma_start(recips.rearrange("b h t -> (b h) t"), all_recips[:, :]).then_inc(recips_stored, 16)
                sp.wait_ge(recips_stored, 16)
            load_recips(0, 0)
            load_recips(1, 1)

            def batch(b, u, i, left):
                if left > 1:
                    u2, i2 = ahead(u, i, 2)
                    sp.wait_ge(mixed, 2 + 2 * b)
                    load_branch(b + 2, u2)
                    load_recips(b + 2, u2)
                    sp.wait_ge(x_stored[u2], 16 * (i2 + 1))
                    load_x(b + 2, u2)

            each_batch(sp, BUF, batch)
            for u in range(BUF):
                sp.wait_ge(x_stored[u], 16 * (len(range(u, NB, BUF)) + 1))

        @block.gpsimd
        def _(pool):
            for h in range(2):
                last_m = nc.gpsimd.memset(wout_sb[h][:, :], 0.0)
            last_m.then_inc(pads_ready, 1)
            norm.setup(nc, pool)
            make_identity(nc, pool, ident, zeroed, ident_ready)

            def scale(b, u, i):
                if sums is not None:
                    pool.wait_ge(branch_loaded[u], BRANCH_LOADS * (i + 1))
                    for c in range(KB):
                        tile = branch[u][:, c, :]
                        nc.gpsimd.tensor_tensor(tile, tile, recip[u][:, c, :], ALU.mult).then_inc(scaled, 1)

            scale(0, 0, 0)
            norm.gpsimd(nc, pool, 0, 0, xt[0])
            scale(1, 1, 0)
            norm.gpsimd(nc, pool, 1, 1, xt[1])
            pool.wait_ge(weights, WEIGHTS)

            def batch(b, u, i, left):
                u2, i2 = ahead(u, i, 2)
                if left > 1:
                    scale(b + 2, u2, i2)
                pool.wait_ge(norm.xn_ready, b + 2)
                for n in range(4):
                    tiles = xt[u][:, 2 * n:2 * n + 2, :]
                    nc.gpsimd.tensor_tensor(tiles, tiles, bout_sb[:, :].unsqueeze(1).to_broadcast([P, 2, D]), ALU.add)\
                        .then_inc(biased, 1)
                if left > 1:
                    norm.gpsimd(nc, pool, b + 2, u2, xt[u2])

            each_batch(pool, BUF, batch)

        @block.vector
        def _(dve):
            dve.sem_inc(summed, RELUS)
            dve.sem_inc(out_ready, 2)
            if sums is not None:
                dve.wait_ge(sums_loaded, 16)
                nc.vector.reciprocal(all_recips[:, :], all_sums[:, :]).then_inc(recips_ready, 1)

            def front(b, u, i):
                dve.wait_ge(x_loaded[u], 16 * (i + 1))
                for n in range(4):
                    if n % 2 == 0:
                        dve.wait_ge(mixed, 2 + 2 * b + n // 2 + 1)
                    tiles = xt[u][:, 2 * n:2 * n + 2, :]
                    nc.vector.tensor_tensor(tiles, tiles, ps[PAIR_OF[MIX0 + n // 2]]
                                            [:, (n % 2) * HALF:(n % 2 + 1) * HALF]
                                            .rearrange("p (t c) -> p t c", t=2), ALU.add).then_inc(added, 1)
                dve.wait_ge(added, 4 * (b + 1))
                norm.vector(nc, dve, b, u, xt[u])

            front(0, 0, 0)
            front(1, 1, 0)
            dve.wait_ge(weights, WEIGHTS)

            def batch(b, u, i, left):
                for j in range(INNER):
                    dve.wait_ge(relu_ready, INNER * b + j + 1)
                    dve.wait_ge(summed, RELUS + INNER * b + j)
                    if j == 0:
                        dve.wait_ge(out_ready, 2 * b + 2)
                        ins = nc.vector.tensor_scalar(g[:, :], hidden[j % RELUS][:, :], w2_sb[:, j:j + 1],
                                                      cols[:, 1, :], ALU.mult, ALU.add)
                    else:
                        ins = nc.vector.scalar_tensor_tensor(g[:, :], hidden[j % RELUS][:, :], w2_sb[:, j:j + 1],
                                                             g[:, :], ALU.mult, ALU.add)
                    ins.then_inc(summed, 1)
                if left > 1:
                    u2, i2 = ahead(u, i, 2)
                    front(b + 2, u2, i2)
                dve.wait_ge(biased, 4 * (b + 1))
                for n in range(4):
                    if n % 2 == 0:
                        dve.wait_ge(out_ready, 2 + 2 * b + n // 2 + 1)
                    tiles = xt[u][:, 2 * n:2 * n + 2, :]
                    nc.vector.tensor_tensor(tiles, tiles, ps[PAIR_OF[OUT0 + n // 2]]
                                            [:, (n % 2) * HALF:(n % 2 + 1) * HALF]
                                            .rearrange("p (t c) -> p t c", t=2), ALU.add).then_inc(x_ready, 1)

            each_batch(dve, BUF, batch)

        @block.scalar
        def _(act):
            for u in range(BUF):
                act.sem_inc(x_stored[u], 16)
            act.wait_ge(weights, WEIGHTS)

            def copy_transposed(b):
                for c in range(CB):
                    norm.wait_transposed(act, b, c)
                    nc.scalar.activation(xnT[:, c, :], ps[PAIR_OF[T0 + c]][:, :], ACT.Copy).then_inc(copied, 1)

            def copy_units(b, u):
                act.wait_ge(units_ready, b + 1)
                nc.scalar.activation(s[u][:, :], ps[PAIR_OF[UNITS]][:, 0:HALF], ACT.Identity, bias=cols[:, 0, :])\
                    .then_inc(copied, 1)

            def relu(b, u, j):
                act.wait_ge(summed, INNER * b + j + 1)
                nc.scalar.activation(hidden[j % RELUS][:, :], s[u][:, :], ACT.Relu, bias=b1_sb[:, j:j + 1],
                                     scale=w1_sb[:, j:j + 1]).then_inc(relu_ready, 1)

            copy_transposed(0)
            copy_units(0, 0)
            act.wait_ge(copied, 3)
            for j in range(RELUS):
                relu(0, 0, j)

            def batch(b, u, i, left):
                u1 = ahead(u, i, 1)[0]
                if left:
                    copy_transposed(b + 1)
                for j in range(RELUS, INNER):
                    if left and j == COPY_S:
                        copy_units(b + 1, u1)
                    relu(b, u, j)
                if left:
                    act.wait_ge(copied, 3 * (b + 2))
                    for j in range(RELUS):
                        relu(b + 1, u1, j)
                act.wait_ge(x_ready, 4 * (b + 1))
                act.dma_start(tokens(x_out[b]), xt[u][:, :, :]).then_inc(x_stored[u], 16)

            each_batch(act, BUF, batch)

        @block.tensor
        def _(pe):
            pe.sem_inc(mixed, 2)
            pe.wait_ge(weights, WEIGHTS)
            pe.wait_ge(ident_ready, 1)

            def tiles(job, n, source, weight, blocks, done):
                for t in range(4):
                    for c in range(blocks):
                        mm = nc.tensor.matmul(ps[PAIR_OF[job]][:, t * D:(t + 1) * D], source(c, 4 * n + t), weight(c),
                                              start=c == 0, stop=c == blocks - 1)
                mm.then_inc(done, 1)

            def mix(b, u, i, free):
                if sums is not None:
                    pe.wait_ge(scaled, KB * (b + 1))
                else:
                    pe.wait_ge(branch_loaded[u], BRANCH_LOADS * (i + 1))
                for n in range(2):
                    free(n)
                    tiles(MIX0 + n, n, lambda c, t: branch[u][:, c, t * P:(t + 1) * P], lambda c: bw[:, c, :], KB, mixed)

            def units(b):
                pe.wait_ge(copied, 3 * b + 2)
                for h in range(2):
                    for c in range(CB):
                        mm = nc.tensor.matmul(ps[PAIR_OF[UNITS]][h * M:(h + 1) * M, 0:HALF], win_sb[:, c, :],
                                              xnT[:, c, h * HALF:(h + 1) * HALF], start=c == 0, stop=c == CB - 1)
                mm.then_inc(units_ready, 1)

            def transposes(b, u, free):
                norm.tensor(nc, pe, b, u, ident, (ps[PAIR_OF[T0]], ps[PAIR_OF[T1]]), free)

            mix(0, 0, 0, lambda n: None)
            transposes(0, 0, lambda c: None)
            mix(1, 1, 0, lambda n: pe.wait_ge(added, 2 * n + 2))
            units(0)
            transposes(1, 1, lambda c: pe.wait_ge(copied, 3))

            def batch(b, u, i, left):
                u2, i2 = ahead(u, i, 2)
                if left:
                    units(b + 1)
                if left > 1:
                    mix(b + 2, u2, i2, lambda n: pe.wait_ge(added, 4 * (b + 1) + 2 * n + 2))
                pe.wait_ge(summed, RELUS + INNER * (b + 1))
                for n in range(2):
                    if n == 1:
                        pe.wait_ge(copied, 3 * (b + 1 + min(left, 1)))
                    tiles(OUT0 + n, n, lambda c, t: g[:, (t % 4) * P:(t % 4 + 1) * P], lambda c: wout_sb[n][:, :],
                          1, out_ready)
                if left > 1:
                    transposes(b + 2, u2, lambda c: pe.wait_ge(x_ready, 4 * (b + 1) - 2 * c))

            each_batch(pe, BUF, batch)


def project_scan(nc, x, x_wT, dt_wT, dt_b, bc_wT, conv_w, conv_b, xc_out, dt_out, dtx_out, b_out, c_parts):
    X, BC, DT = 0, DB, DB + 1
    JOBS = 2 * DB + 1
    PAIR_OF = [0, 1, 2, 3, 0, 3, 0, 1, 2]
    T_PAIRS = (1, 2)
    PAD = TAPS - 1

    with ExitStack() as ctx:
        st = Stage(nc, ctx, "prep")
        xt = [st.sb(f"x{u}", [P, TT, D]) for u in range(2)]
        norm = Norm(st)
        xnT = [st.sb(f"xnT{u}", [P, CB, T]) for u in range(2)]
        xi = [st.sb(f"xi{i}", [P, PAD + T]) for i in range(2)]
        conv = [st.sb(f"conv{i}", [P, T]) for i in range(2)]
        xc = [st.sb(f"xc{d}", [P, T]) for d in range(DB)]
        soft = [st.sb(f"soft{i}", [P, T]) for i in range(2)]
        relu = [st.sb(f"relu{i}", [P, T]) for i in range(2)]
        dt = [st.sb(f"dt{i}", [P, T]) for i in range(2)]
        dtx = [st.sb(f"dtx{i}", [P, T]) for i in range(2)]
        bc = st.sb("bc", [2 * NS, T])
        bc_rest = st.sb("bc_rest", [2 * NS, T])
        bc_parts = st.sb("bc_parts", [2 * NS, 3, T], BF16)
        ident = st.sb("ident", [P, P])
        xw = st.sb("x_w", [P, CB, DI])
        dtw = st.sb("dt_w", [P, CB, DI])
        bcw = st.sb("bc_w", [P, CB, 2 * NS])
        dtb = st.sb("dt_b", [P, DB])
        cw = st.sb("conv_w", [P, DB, TAPS])
        cb = st.sb("conv_b", [P, DB])
        ps = [st.ps(f"p{i}", [P, PAIR]) for i in range(4)]

        weights = st.sem("weights")
        zeroed = st.sem("zeroed")
        ident_ready = st.sem("ident_ready")
        pads_ready = st.sem("pads_ready")
        x_loaded = [st.sem(f"x_loaded{u}") for u in range(2)]
        xnT_ready = st.sem("xnT_ready")
        product = st.sem("product")
        xi_ready = st.sem("xi_ready")
        tap0_ready = st.sem("tap0_ready")
        conv_steps = st.sem("conv_steps")
        xc_ready = st.sem("xc_ready")
        bc_hi = st.sem("bc_hi")
        bc_rested = st.sem("bc_rested")
        bc_steps = st.sem("bc_steps")
        relu_ready = st.sem("relu_ready")
        soft_steps = st.sem("soft_steps")
        dt_ready = st.sem("dt_ready")
        dtx_ready = st.sem("dtx_ready")
        xc_stored = [st.sem(f"xc_stored{d}") for d in range(DB)]
        dt_stored = [st.sem(f"dt_stored{i}") for i in range(2)]
        dtx_stored = [st.sem(f"dtx_stored{i}") for i in range(2)]
        b_stored = st.sem("b_stored")
        c_stored = st.sem("c_stored")
        block = ctx.enter_context(nc.Block())
        WEIGHTS = 16 * 6
        tokens = lambda a: a.rearrange("(t p) c -> p t c", p=P)

        @block.sync
        def _(sp):
            def load(b, u):
                sp.dma_start(xt[u][:, :, :], tokens(x[b])).then_inc(x_loaded[u], 16)

            load(0, 0)
            for tile, w in ((xw, x_wT), (dtw, dt_wT), (bcw, bc_wT)):
                sp.dma_start(tile[:, :, :], w.rearrange("(a p) c -> p a c", p=P)).then_inc(weights, 16)
            sp.dma_start(cw[:, :, :], conv_w.rearrange("(a p) c -> p a c", p=P)).then_inc(weights, 16)
            for tile, w in ((dtb, dt_b), (cb, conv_b)):
                sp.dma_start(tile[:, :], w).then_inc(weights, 16)
            load(1, 1)

            def batch(b, u, i, left):
                rows = lambda d: slice(d * P, (d + 1) * P)
                if left > 1:
                    sp.wait_ge(norm.xn_ready, b + 2)
                    load(b + 2, u)
                for d in range(DB):
                    sp.wait_ge(xc_ready, DB + DB * b + d + 1)
                    sp.dma_start(xc_out[b, rows(d), :], xc[d][:, :]).then_inc(xc_stored[d], 16)
                sp.wait_ge(bc_hi, 2 + 2 * (b + 1))
                sp.dma_start(b_out[b], bc[0:NS, :]).then_inc(b_stored, 16)
                sp.wait_ge(bc_steps, 2 * (b + 2))
                sp.dma_start(c_parts[b].rearrange("a s t -> s a t"), bc_parts[NS:2 * NS, :, :]).then_inc(c_stored, 16)
                for d in range(DB):
                    sp.wait_ge(dt_ready, DB + DB * b + d + 1)
                    sp.dma_start(dt_out[b, rows(d), :], dt[d % 2][:, :]).then_inc(dt_stored[d % 2], 16)
                    sp.wait_ge(dtx_ready, DB + DB * b + d + 1)
                    sp.dma_start(dtx_out[b, rows(d), :], dtx[d % 2][:, :]).then_inc(dtx_stored[d % 2], 16)

            each_batch(sp, 2, batch)
            for d in range(DB):
                sp.wait_ge(xc_stored[d], 16 * (NB + 1))
            for n in range(2):
                sp.wait_ge(dt_stored[n], 16 * (DB // 2 * NB + 1))
                sp.wait_ge(dtx_stored[n], 16 * (DB // 2 * NB + 1))
            sp.wait_ge(b_stored, 16 * (NB + 1))
            sp.wait_ge(c_stored, 16 * (NB + 1))

        @block.gpsimd
        def _(pool):
            for n in range(2):
                last_m = nc.gpsimd.memset(xi[n][:, 0:PAD], 0.0)
            last_m.then_inc(pads_ready, 1)
            norm.setup(nc, pool)
            pool.sem_inc(dt_ready, DB)
            pool.sem_inc(dtx_ready, DB)
            pool.sem_inc(bc_steps, 2)
            make_identity(nc, pool, ident, zeroed, ident_ready)
            pool.wait_ge(weights, WEIGHTS)
            norm.gpsimd(nc, pool, 0, 0, xt[0])

            def batch(b, u, i, left):
                if left:
                    norm.gpsimd(nc, pool, b + 1, 1 - u, xt[1 - u])
                for d in range(DB):
                    pool.wait_ge(xi_ready, DB + DB * b + d + 1)
                    pool.wait_ge(xc_ready, DB * b + d + 3)
                    stand(pool, norm.pool_passed)
                    nc.gpsimd.tensor_scalar(conv[d % 2][:, :], xi[d % 2][:, PAD:PAD + T], cw[:, d, PAD:PAD + 1],
                                            cb[:, d:d + 1], ALU.mult, ALU.add).then_inc(tap0_ready, 1)
                pool.wait_ge(bc_rested, 1 + b + 1)
                pool.wait_ge(c_stored, 16 * (b + 1))
                stand(pool, norm.pool_passed)
                nc.gpsimd.tensor_scalar(bc_parts[:, 1, :], bc_rest[:, :], 1.0, 0.0, ALU.mult, ALU.add)\
                    .then_inc(bc_steps, 1)
                pool.wait_ge(bc_steps, 2 + 2 * b + 1)
                nc.gpsimd.tensor_tensor(bc_parts[:, 2, :], bc_rest[:, :], bc_parts[:, 1, :], ALU.subtract)\
                    .then_inc(bc_steps, 1)
                for d in range(DB):
                    n = d % 2
                    pool.wait_ge(relu_ready, DB + DB * b + d + 1)
                    pool.wait_ge(soft_steps, 3 * DB + 3 * (DB * b + d + 1))
                    pool.wait_ge(dt_stored[n], 16 * (DB // 2 * b + d // 2 + 1))
                    nc.gpsimd.tensor_tensor(dt[n][:, :], relu[n][:, :], soft[n][:, :], ALU.add).then_inc(dt_ready, 1)
                    pool.wait_ge(dt_ready, DB + DB * b + d + 1)
                    pool.wait_ge(dtx_stored[n], 16 * (DB // 2 * b + d // 2 + 1))
                    nc.gpsimd.tensor_tensor(dtx[n][:, :], dt[n][:, :], xc[d][:, :], ALU.mult).then_inc(dtx_ready, 1)

            each_batch(pool, 2, batch)

        @block.vector
        def _(dve):
            dve.sem_inc(conv_steps, 3 * DB)
            dve.sem_inc(bc_rested, 1)
            dve.sem_inc(relu_ready, DB)
            dve.wait_ge(weights, WEIGHTS)
            dve.wait_ge(x_loaded[0], 16)
            norm.vector(nc, dve, 0, 0, xt[0])

            def batch(b, u, i, left):
                if left:
                    dve.wait_ge(x_loaded[1 - u], 16 * (i + 1 + u))
                    norm.vector(nc, dve, b + 1, 1 - u, xt[1 - u])
                for d in range(DB):
                    n = d % 2
                    dve.wait_ge(tap0_ready, DB * b + d + 1)
                    for k in range(1, TAPS):
                        lag = PAD - k
                        if k > 1:
                            dve.wait_ge(conv_steps, 3 * (DB + DB * b + d) + k - 1)
                        nc.vector.scalar_tensor_tensor(conv[n][:, :], xi[n][:, lag:lag + T], cw[:, d, lag:lag + 1],
                                                       conv[n][:, :], ALU.mult, ALU.add).then_inc(conv_steps, 1)
                dve.wait_ge(bc_hi, 2 + 2 * (b + 1))
                dve.wait_ge(bc_steps, 2 * b + 2)
                nc.vector.tensor_tensor(bc_rest[:, :], ps[PAIR_OF[BC]][0:2 * NS, :], bc_parts[:, 0, :], ALU.subtract)\
                    .then_inc(bc_rested, 1)
                for d in range(DB):
                    dve.wait_ge(soft_steps, 3 * (DB + DB * b + d) + 1)
                    dve.wait_ge(dt_ready, DB * b + d + 3)
                    nc.vector.tensor_scalar(relu[d % 2][:, :], ps[PAIR_OF[DT + d]][:, :], dtb[:, d:d + 1], 0.0,
                                            ALU.add, ALU.max).then_inc(relu_ready, 1)

            each_batch(dve, 2, batch)

        @block.scalar
        def _(act):
            act.sem_inc(xnT_ready, CB)
            act.sem_inc(xi_ready, DB)
            act.sem_inc(xc_ready, DB)
            act.sem_inc(bc_hi, 2)
            act.sem_inc(soft_steps, 3 * DB)
            for s in (*xc_stored, *dt_stored, *dtx_stored, b_stored, c_stored):
                act.sem_inc(s, 16)
            act.wait_ge(pads_ready, 1)
            act.wait_ge(weights, WEIGHTS)

            def transposed(b, u):
                for c in range(CB):
                    norm.wait_transposed(act, b, c)
                    nc.scalar.activation(xnT[u][:, c, :], ps[T_PAIRS[c]][:, :], ACT.Copy).then_inc(xnT_ready, 1)

            transposed(0, 0)

            def batch(b, u, i, left):

                def silu(d):
                    act.wait_ge(conv_steps, 3 * (DB + DB * b + d + 1))
                    act.wait_ge(xc_stored[d], 16 * (b + 1))
                    act.wait_ge(dtx_ready, DB * (b + 1))
                    nc.scalar.activation(xc[d][:, :], conv[d % 2][:, :], ACT.Silu).then_inc(xc_ready, 1)

                for d in range(DB):
                    act.wait_ge(product, JOBS * b + X + d + 1)
                    act.wait_ge(conv_steps, 3 * (DB * b + d + 3))
                    nc.scalar.activation(xi[d % 2][:, PAD:PAD + T], ps[PAIR_OF[X + d]][:, :], ACT.Copy)\
                        .then_inc(xi_ready, 1)
                    if d > 0:
                        silu(d - 1)
                silu(DB - 1)
                act.wait_ge(product, JOBS * b + BC + 1)
                act.wait_ge(b_stored, 16 * (b + 1))
                nc.scalar.activation(bc[:, :], ps[PAIR_OF[BC]][0:2 * NS, :], ACT.Copy).then_inc(bc_hi, 1)
                act.wait_ge(c_stored, 16 * (b + 1))
                nc.scalar.activation(bc_parts[:, 0, :], ps[PAIR_OF[BC]][0:2 * NS, :], ACT.Copy).then_inc(bc_hi, 1)
                if left:
                    transposed(b + 1, 1 - u)
                nc.scalar.preload_act_table_set("natural_log_exp_and_others")
                for d in range(DB):
                    t = soft[d % 2][:, :]
                    steps = 3 * (DB + DB * b + d)
                    act.wait_ge(product, JOBS * b + DT + d + 1)
                    act.wait_ge(dt_ready, DB * b + d + 3)
                    nc.scalar.activation(t, ps[PAIR_OF[DT + d]][:, :], ACT.Abs, bias=dtb[:, d:d + 1]).then_inc(soft_steps, 1)
                    act.wait_ge(soft_steps, steps + 1)
                    nc.scalar.activation(t, t, ACT.Exp, scale=-1.0).then_inc(soft_steps, 1)
                    act.wait_ge(soft_steps, steps + 2)
                    nc.scalar.activation(t, t, ACT.Ln, bias=1.0).then_inc(soft_steps, 1)

            each_batch(act, 2, batch)

        @block.tensor
        def _(pe):
            pe.wait_ge(weights, WEIGHTS)
            pe.wait_ge(ident_ready, 1)

            def read(job, b):
                if job < BC:
                    pe.wait_ge(xi_ready, DB + DB * b + job + 1)
                elif job == BC:
                    pe.wait_ge(bc_rested, 1 + b + 1)
                else:
                    pe.wait_ge(relu_ready, DB + DB * b + job - DT + 1)
                    pe.wait_ge(soft_steps, 3 * (DB + DB * b + job - DT) + 1)

            def transposes(b, u):
                norm.tensor(nc, pe, b, u, ident, [ps[n] for n in T_PAIRS], lambda c: read(X + 1 + c, b - 1))

            BEFORE = [(DT + 1, 1), (DT + 2, 1), (DT + 3, 1), (DT, 1), (X, 0), (X + 3, 0), (BC, 0), None, None]
            transposes(0, 0)

            def batch(b, u, i, left):
                for job in range(JOBS):
                    if job == DT and left:
                        transposes(b + 1, 1 - u)
                    if BEFORE[job]:
                        read(BEFORE[job][0], b - BEFORE[job][1])
                    elif left:
                        pe.wait_ge(xnT_ready, CB + CB * (b + 1) + (job - DT - 1))
                    else:
                        read(X + job - DT - 1, b)
                    if job == 0:
                        pe.wait_ge(xnT_ready, CB + CB * (b + 1))
                    rows = 2 * NS if job == BC else P
                    w, at = (xw, job * P) if job < BC else (bcw, 0) if job == BC else (dtw, (job - DT) * P)
                    for h in range(2):
                        for c in range(CB):
                            mm = nc.tensor.matmul(ps[PAIR_OF[job]][0:rows, h * HALF:(h + 1) * HALF],
                                                  w[:, c, at:at + rows], xnT[u][:, c, h * HALF:(h + 1) * HALF],
                                                  start=c == 0, stop=c == CB - 1)
                    mm.then_inc(product, 1)

            each_batch(pe, 2, batch)


def scan(nc, xc_in, dt_in, dtx_in, b_in, c_parts, a_log, d_skip, yT):
    CROWS = 96
    QS = 4
    STEPS = DB * NS
    NU, NGB = 4, 2

    with ExitStack() as ctx:
        st = Stage(nc, ctx, "scan")
        dt = [st.sb(f"dt{i}", [P, T]) for i in range(2)]
        dtx = [st.sb(f"dtx{i}", [P, T]) for i in range(2)]
        xc = [st.sb(f"xc{i}", [P, T]) for i in range(2)]
        bb = [st.sb(f"b{i}", [P, QS, T]) for i in range(NS // QS)]
        c = [st.sb(f"c{i}", [CROWS, T], BF16) for i in range(2)]
        pick = st.sb("pick", [CROWS, NS, P], BF16)
        pick_f = st.sb("pick_f", [CROWS, NS, P])
        ins = [st.sb(f"in{i}", [P, T]) for i in range(NU)]
        h = [st.sb(f"h{i}", [P, T]) for i in range(2)]
        hc = [st.sb(f"hc{i}", [P, T]) for i in range(NGB)]
        y = st.sb("y", [P, T])
        a = st.sb("a", [P, DB, NS])
        skip = st.sb("skip", [P, DB])
        ident = st.sb("ident", [P, P])
        psA = [st.ps(f"decay{i}", [P, PAIR]) for i in range(2)]
        psC = st.ps("c_wide", [P, PAIR])
        psY = st.ps("y_sum", [P, PAIR])

        weights = st.sem("weights")
        zeroed = st.sem("zeroed")
        ident_ready = st.sem("ident_ready")
        pick_steps = st.sem("pick_steps")
        c_zeroed = st.sem("c_zeroed")
        a_steps = st.sem("a_steps")
        block_loaded = [st.sem(f"block_loaded{i}") for i in range(2)]
        b_loaded = [st.sem(f"b_loaded{i}") for i in range(NS // QS)]
        c_loaded = [st.sem(f"c_loaded{i}") for i in range(2)]
        decay_ready = st.sem("decay_ready")
        in_ready = st.sem("in_ready")
        scanned = st.sem("scanned")
        c_wide = st.sem("c_wide")
        hc_ready = st.sem("hc_ready")
        summed = st.sem("summed")
        y_ready = st.sem("y_ready")
        y_stored = st.sem("y_stored")
        block = ctx.enter_context(nc.Block())
        WEIGHTS = 16 * 2

        @block.sync
        def _(sp):
            sp.dma_start(a[:, :, :], a_log.rearrange("(a p) s -> p a s", p=P)).then_inc(weights, 16)
            sp.dma_start(skip[:, :], d_skip).then_inc(weights, 16)
            rows = lambda d: slice(d * P, (d + 1) * P)

            def load_block(b, d):
                for tile, source in ((dt, dt_in), (dtx, dtx_in), (xc, xc_in)):
                    sp.dma_start(tile[d % 2][:, :], source[b, rows(d), :]).then_inc(block_loaded[d % 2], 16)

            def load_b(b, n):
                sp.dma_start(bb[n][:, :, :], b_in[b, n * QS:(n + 1) * QS, :].unsqueeze(0).to_broadcast([P, QS, T]))\
                    .then_inc(b_loaded[n], 16)

            def load_c(b, u):
                sp.dma_start(c[u][0:3 * NS, :], c_parts[b].rearrange("a s t -> (a s) t")).then_inc(c_loaded[u], 16)

            sp.wait_ge(c_zeroed, 1)
            load_c(0, 0)
            load_c(1, 1)
            load_block(0, 0)
            for n in range(NS // QS):
                load_b(0, n)
            load_block(0, 1)

            def batch(b, u, i, left):
                for d in range(DB):
                    if d == DB - 1 and left:
                        for n in range(NS // QS):
                            sp.wait_ge(in_ready, STEPS * b + d * NS + (n + 1) * QS)
                            load_b(b + 1, n)
                    sp.wait_ge(y_ready, 1 + DB * b + d + 1)
                    sp.dma_start(yT[b, rows(d), :], y[:, :]).then_inc(y_stored, 16)
                    if left or d < DB - 2:
                        load_block(b + (d + 2) // DB, (d + 2) % DB)
                if left > 1:
                    sp.wait_ge(c_wide, STEPS * (b + 1))
                    load_c(b + 2, u)

            each_batch(sp, 2, batch)
            sp.wait_ge(y_stored, 16 * (NB * DB + 1))

        @block.gpsimd
        def _(pool):
            for n in range(2):
                last_m = nc.gpsimd.memset(c[n][:, :], 0.0)
            last_m.then_inc(c_zeroed, 1)
            make_identity(nc, pool, ident, zeroed, ident_ready)
            nc.gpsimd.memset(pick_f[:, :, :], 0.0).then_inc(pick_steps, 1)
            for part in range(3):
                pool.wait_ge(pick_steps, part + 1)
                nc.gpsimd.affine_select(out=pick_f[:, :, :], in_=pick_f[:, :, :], compare_op=ALU.not_equal,
                                        fill=1.0, base=-part * NS, pattern=[[-1, NS], [0, P]],
                                        channel_multiplier=1).then_inc(pick_steps, 1)
            pool.wait_ge(pick_steps, 4)
            nc.gpsimd.tensor_copy(pick[:, :, :], pick_f[:, :, :]).then_inc(pick_steps, 1)

            def batch(b, u, i, left):
                for n in range(STEPS):
                    d, s = n // NS, n % NS
                    if s == 0:
                        pool.wait_ge(block_loaded[d % 2], 48 * (DB // 2 * b + d // 2 + 1))
                    if d == 0 and s % QS == 0:
                        pool.wait_ge(b_loaded[s // QS], 16 * (b + 1))
                    pool.wait_ge(scanned, STEPS * b + n + 1)
                    nc.gpsimd.tensor_tensor(ins[n % NU][:, :], dtx[d % 2][:, :], bb[s // QS][:, s % QS, :],
                                            ALU.mult).then_inc(in_ready, 1)

            each_batch(pool, 2, batch)

        @block.vector
        def _(dve):
            dve.sem_inc(scanned, NU)
            dve.sem_inc(hc_ready, 2)
            dve.sem_inc(y_ready, 1)
            dve.wait_ge(a_steps, 1)
            nc.vector.tensor_scalar(a[:, :, :], a[:, :, :], -1.0, None, ALU.mult).then_inc(a_steps, 1)

            def batch(b, u, i, left):
                def recur(n):
                    dve.wait_ge(decay_ready, STEPS * b + n + 1)
                    dve.wait_ge(in_ready, STEPS * b + n + 1)
                    dve.wait_ge(hc_ready, STEPS * b + n + 1)
                    nc.vector.tensor_tensor_scan(h[n % 2][:, :], psA[n % 2][:, :], ins[n % NU][:, :],
                                                 0.0, ALU.mult, ALU.add).then_inc(scanned, 1)

                def weigh(n):
                    dve.wait_ge(c_wide, STEPS * b + n + 1)
                    dve.wait_ge(scanned, NU + STEPS * b + n + 1)
                    dve.wait_ge(summed, STEPS * b + n + 1)
                    nc.vector.tensor_tensor(hc[n % NGB][:, :], h[n % 2][:, :], psC[:, :], ALU.mult)\
                        .then_inc(hc_ready, 1)

                def finish(d):
                    dve.wait_ge(summed, NGB + STEPS * b + (d + 1) * NS)
                    dve.wait_ge(block_loaded[d % 2], 48 * (DB // 2 * b + d // 2 + 1))
                    dve.wait_ge(y_stored, 16 * (DB * b + d + 1))
                    nc.vector.scalar_tensor_tensor(y[:, :], xc[d % 2][:, :], skip[:, d:d + 1], psY[:, :],
                                                   ALU.mult, ALU.add).then_inc(y_ready, 1)

                recur(0)
                for n in range(STEPS):
                    if n + 1 < STEPS:
                        recur(n + 1)
                    weigh(n)
                    if n % NS == 0 and n > 0:
                        finish(n // NS - 1)
                finish(DB - 1)

            each_batch(dve, 2, batch)

        @block.scalar
        def _(act):
            act.sem_inc(summed, NGB)
            act.sem_inc(y_stored, 16)
            act.wait_ge(weights, WEIGHTS)
            nc.scalar.activation(a[:, :, :], a[:, :, :], ACT.Exp).then_inc(a_steps, 1)
            act.wait_ge(a_steps, 2)

            def batch(b, u, i, left):
                for n in range(STEPS):
                    d, s = n // NS, n % NS
                    if s == 0:
                        act.wait_ge(block_loaded[d % 2], 48 * (DB // 2 * b + d // 2 + 1))
                    act.wait_ge(scanned, STEPS * b + n + NU - 1)
                    nc.scalar.activation(psA[n % 2][:, :], dt[d % 2][:, :], ACT.Exp, scale=a[:, d, s:s + 1])\
                        .then_inc(decay_ready, 1)

            each_batch(act, 2, batch)

        @block.tensor
        def _(pe):
            pe.wait_ge(ident_ready, 1)
            pe.wait_ge(pick_steps, 5)

            def batch(b, u, i, left):
                def widen(n):
                    if n == 0:
                        pe.wait_ge(c_loaded[u], 16 * (i + 1))
                    pe.wait_ge(hc_ready, 2 + STEPS * b + n)
                    for half in range(2):
                        mm = nc.tensor.matmul(psC[:, half * HALF:(half + 1) * HALF], pick[:, n % NS, :],
                                              c[u][:, half * HALF:(half + 1) * HALF], start=True, stop=True)
                    mm.then_inc(c_wide, 1)

                def add(n):
                    s = n % NS
                    pe.wait_ge(hc_ready, 2 + STEPS * b + n + 1)
                    if s == 0:
                        pe.wait_ge(y_ready, 1 + DB * b + n // NS)
                    for half in range(2):
                        cols = slice(half * HALF, (half + 1) * HALF)
                        mm = nc.tensor.matmul(psY[:, cols], ident[:, :], hc[n % NGB][:, cols], start=s == 0,
                                              stop=s == NS - 1)
                    mm.then_inc(summed, 1)

                for n in range(STEPS):
                    widen(n)
                    if n > 0:
                        add(n - 1)
                add(STEPS - 1)

            each_batch(pe, 2, batch)


def hybrid_block(nc, a):
    def dram(name, shape, dt=F32):
        return nc.dram_tensor(name, shape, dt).ap()

    qk_parts = dram("qk_parts", [NB, 2, 3, D, T], BF16)
    v_ones = dram("v_ones", [NB, P, TT * NH * VW])
    max_scratch = dram("max_scratch", [NG, P, 3 * 32], BF16)
    valuesT = dram("valuesT", [NB, D, T])
    sums, recips = (dram(n, [NB, NH, T]) for n in ("sums", "recips"))
    x2 = dram("x2", [NB, T, D])
    xc, dt, dtx, yT = (dram(n, [NB, DI, T]) for n in ("xc", "dt", "dtx", "yT"))
    b_rows = dram("b_rows", [NB, NS, T])
    c_parts = dram("c_parts", [NB, 3, NS, T], BF16)
    ffn = [a[n] for n in ("win", "b_in", "w1", "b1", "w2", "b2", "wout", "bout")]

    project_qkv(nc, a["x"], a["wq"], a["wk_b"], a["wkv_aT"], a["wv_bT"], a["turnT"], qk_parts, v_ones)
    attention(nc, qk_parts, v_ones, max_scratch, valuesT, sums)
    residual_ffn(nc, "ffn1", a["x"], valuesT, a["woT"], *ffn, x2, sums, recips)
    project_scan(nc, x2, a["x_wT"], a["dt_wT"], a["dt_b"], a["bc_wT"], a["conv_w"], a["conv_b"],
                 xc, dt, dtx, b_rows, c_parts)
    scan(nc, xc, dt, dtx, b_rows, c_parts, a["a_log"], a["d_skip"], yT)
    residual_ffn(nc, "ffn2", x2, yT, a["out_wT"], *ffn, a["out"])


def head_turns():
    inv = (np.float32(1.0) / np.float32(10000.0) ** (np.arange(0, HD, 2, dtype=np.float32) / np.float32(HD)))
    angle = np.arange(NH, dtype=np.float32)[:, None] * inv.astype(np.float32)[None, :]
    cos, sin = np.cos(angle), np.sin(angle)
    turn = np.zeros((D, D), np.float32)
    even = np.arange(0, D, 2)
    turn[even, even] = turn[even + 1, even + 1] = cos.reshape(-1)
    turn[even, even + 1] = -sin.reshape(-1)
    turn[even + 1, even] = sin.reshape(-1)
    return np.stack([turn[c * P:(c + 1) * P, c * P:(c + 1) * P].T for c in range(CB)])


def kernel(**inputs):
    import concourse.bacc as bacc
    from concourse.bass_utils import run_bass_kernel_spmd

    w = {k.split("_", 1)[1]: np.asarray(v) for k, v in inputs.items()}
    by_block = lambda v: v.reshape(-1, P).T
    arrays = {
        "x": w["attn_a_x"], "wq": w["attn_a_wq"], "wk_b": w["attn_a_wk_b"],
        "wkv_aT": np.concatenate([w["attn_a_wk_a"].T, w["attn_a_wv_a"].T], axis=1),
        "wv_bT": w["attn_a_wv_b"].T, "woT": w["attn_a_wo"].T, "turnT": head_turns(),
        "win": w["ffn_Win"], "b_in": w["ffn_bin_"], "w1": w["ffn_W1"], "b1": w["ffn_b1"],
        "w2": w["ffn_W2"], "b2": w["ffn_b2"], "wout": w["ffn_Wout"], "bout": w["ffn_bout"],
        "x_wT": w["attn_b_x_proj_w"].T, "dt_wT": w["attn_b_dt_proj_w"].T,
        "dt_b": by_block(w["attn_b_dt_proj_b"]),
        "bc_wT": np.concatenate([w["attn_b_B_proj_w"].T, w["attn_b_C_proj_w"].T], axis=1),
        "conv_w": w["attn_b_conv_w"].reshape(DI, TAPS), "conv_b": by_block(w["attn_b_conv_b"]),
        "a_log": w["attn_b_A_log"], "d_skip": by_block(w["attn_b_D"]),
        "out_wT": w["attn_b_out_proj_w"].T,
    }
    arrays = {k: np.ascontiguousarray(v) for k, v in arrays.items()}
    nc = bacc.Bacc("TRN2", target_bir_lowering=False, num_devices=1)
    args = {k: nc.dram_tensor(k, v.shape, mybir.dt.from_np(v.dtype), kind="ExternalInput").ap()
            for k, v in arrays.items()}
    args["out"] = nc.dram_tensor("out", (NB, T, D), F32, kind="ExternalOutput").ap()
    hybrid_block(nc, args)
    return run_bass_kernel_spmd(nc, [arrays], core_ids=[0]).results[0]["out"]
```

```python
import numpy as np
import concourse.bass as bass
from concourse import mybir
from contextlib import ExitStack

F32 = mybir.dt.float32
BF16 = mybir.dt.bfloat16
ALU = mybir.AluOpType
ACT = mybir.ActivationFunctionType
AX = mybir.AxisListType

P = 128
NB, T, D = 8, 1024, 256
NH, HD = 16, 16
LAT = 64
DI, NS, TAPS = 512, 16, 4
M, INNER = 64, 16
EPS = 1e-5

TT = T // P
CB = D // P
DB = DI // P
HALF = 512
PAIR = 2 * HALF
NG, GH = 4, 4
SLOTS = 6
ROWS = SLOTS * HD
CROWS = 96
VW = 32
Q_PARTS = (0, 0, 0, 1, 1, 2)
K_PARTS = (0, 1, 2, 0, 1, 0)


def each_batch(eng, unroll, body):
    turns = (NB - 1) // unroll
    with eng.Fori(0, turns) as i:
        for u in range(unroll):
            body(i * unroll + u, u, i, NB - turns * unroll)
    for b in range(turns * unroll, NB):
        body(b, b % unroll, b // unroll, NB - 1 - b)


class Stage:

    def __init__(self, nc, ctx, name):
        self.nc, self.ctx, self.name = nc, ctx, name
        self.sems = []
        ctx.callback(self.end)

    def end(self):
        self.nc.clear_and_free_semaphores(self.sems)
        self.nc.all_engine_barrier()

    def sb(self, name, shape, dt=F32):
        return self.ctx.enter_context(self.nc.sbuf_tensor(f"{self.name}_{name}", shape, dt))

    def ps(self, name, shape):
        return self.ctx.enter_context(self.nc.psum_tensor(f"{self.name}_{name}", shape, F32))

    def sem(self, name):
        self.sems.append(self.nc.alloc_semaphore(name=f"{self.name}_{name}"))
        return self.sems[-1]


def stand(eng, passed):
    eng.sem_inc(passed, 1)


def make_identity(nc, pool, ident, zeroed, ready):
    nc.gpsimd.memset(ident[:, :], 0.0).then_inc(zeroed, 1)
    pool.wait_ge(zeroed, 1)
    nc.gpsimd.affine_select(out=ident[:, :], in_=ident[:, :], compare_op=ALU.not_equal, fill=1.0,
                            base=0, pattern=[[-1, P]], channel_multiplier=1).then_inc(ready, 1)


class Norm:

    def __init__(self, st, buffers=2):
        self.buffers = buffers
        self.stats = st.sb("stats", [P, TT, 6])
        self.mv = [st.sb(f"mean_var{u}", [P, TT, 2]) for u in range(buffers)]
        self.var_eps = st.sb("var_eps", [P, TT])
        self.neg_mean = st.sb("neg_mean", [P, TT])
        self.rstd = st.sb("rstd", [P, TT])
        self.exponent = st.sb("exponent", [P, TT])
        self.xn = [st.sb(f"xn{u}", [P, TT, D]) for u in range(buffers)]
        self.stats_done = st.sem("stats_done")
        self.mv_ready = st.sem("mean_var_ready")
        self.rstd_steps = st.sem("rstd_steps")
        self.xn_ready = st.sem("xn_ready")
        self.transposed = st.sem("transposed")
        self.exponent_set = st.sem("exponent_set")
        self.pool_passed = st.sem("pool_passed")
        self.dve_passed = st.sem("dve_passed")

    def setup(self, nc, pool):
        pool.sem_inc(self.transposed, self.buffers * CB)
        pool.sem_inc(self.mv_ready, 1)
        pool.sem_inc(self.xn_ready, 1)
        nc.gpsimd.memset(self.exponent[:, :], -0.5).then_inc(self.exponent_set, 1)

    def vector(self, nc, dve, b, u, x):
        dve.wait_ge(self.mv_ready, b + 1)
        for t in range(TT):
            last = nc.vector.bn_stats(self.stats[:, t, :], x[:, t, :])
        last.then_inc(self.stats_done, 1)
        dve.wait_ge(self.stats_done, b + 1)
        dve.wait_ge(self.transposed, CB * (b + 1))
        stand(dve, self.dve_passed)
        for t in range(TT):
            last = nc.vector.bn_aggr(self.mv[u][:, t, :], self.stats[:, t, :])
        last.then_inc(self.mv_ready, 1)

    def gpsimd(self, nc, pool, b, u, x):
        mv = self.mv[u]
        pool.wait_ge(self.exponent_set, 1)
        pool.wait_ge(self.xn_ready, b + 1)
        pool.wait_ge(self.mv_ready, b + 2)
        stand(pool, self.pool_passed)
        nc.gpsimd.tensor_scalar(self.var_eps[:, :], mv[:, :, 1], 1.0, EPS, ALU.mult, ALU.add)\
            .then_inc(self.rstd_steps, 1)
        nc.gpsimd.tensor_scalar(self.neg_mean[:, :], mv[:, :, 0], -1.0, 0.0, ALU.mult, ALU.add)\
            .then_inc(self.rstd_steps, 1)
        pool.wait_ge(self.rstd_steps, 3 * b + 2)
        nc.gpsimd.tensor_tensor(self.rstd[:, :], self.var_eps[:, :], self.exponent[:, :], ALU.pow)\
            .then_inc(self.rstd_steps, 1)
        pool.wait_ge(self.rstd_steps, 3 * b + 3)
        pool.wait_ge(self.transposed, CB * (b + 1))
        stand(pool, self.pool_passed)
        for t in range(TT):
            last = nc.gpsimd.tensor_scalar(self.xn[u][:, t, :], x[:, t, :], self.neg_mean[:, t:t + 1],
                                           self.rstd[:, t:t + 1], ALU.add, ALU.mult)
        last.then_inc(self.xn_ready, 1)

    def tensor(self, nc, pe, b, u, ident, banks, free):
        pe.wait_ge(self.xn_ready, b + 2)
        for c in range(CB):
            free(c)
            for t in range(TT):
                last = nc.tensor.transpose(banks[c][:, t * P:(t + 1) * P],
                                           self.xn[u][:, t, c * P:(c + 1) * P], ident[:, :])
            last.then_inc(self.transposed, 1)

    def wait_transposed(self, eng, b, c):
        eng.wait_ge(self.transposed, CB * (self.buffers + b) + c + 1)


class Constants:

    def __init__(self, nc, ctx):
        def sb(name, shape, dt=F32):
            return ctx.enter_context(nc.sbuf_tensor(f"const_{name}", shape, dt))

        self.ident = sb("ident", [P, P])
        self.wo, self.out_w = sb("wo", [P, CB, D]), sb("out_w", [P, DB, D])
        self.win = sb("win", [P, CB, M])
        self.cols = sb("cols", [P, 2, 1])
        self.w1, self.b1, self.w2 = (sb(n, [P, INNER]) for n in ("w1", "b1", "w2"))
        self.wout = [sb(f"wout{h}", [P, D]) for h in range(2)]
        self.bout = sb("bout", [P, D])
        self.x_w, self.dt_w = sb("x_w", [P, CB, DI]), sb("dt_w", [P, CB, DI])
        self.bc_w = sb("bc_w", [P, CB, 2 * NS])
        self.dt_b = sb("dt_b", [P, DB])
        self.conv_w, self.conv_b = sb("conv_w", [P, DB, TAPS]), sb("conv_b", [P, DB])
        self.a = sb("a", [P, DB, NS])
        self.skip = sb("skip", [P, DB])
        self.skip_diag = sb("skip_diag", [P, DB, P])
        self.pick = sb("pick", [CROWS, NS, P], BF16)

    def load(self, sp, w, loaded):
        blocks = lambda t: t.rearrange("(a p) c -> p a c", p=P)
        pairs = [(t[:, :, :], blocks(w[n])) for t, n in (
            (self.wo, "woT"), (self.win, "win"), (self.x_w, "x_wT"), (self.dt_w, "dt_wT"), (self.bc_w, "bc_wT"),
            (self.conv_w, "conv_w"), (self.a, "a_log"), (self.out_w, "out_wT"))]
        pairs += [(t[:, :], w[n]) for t, n in ((self.dt_b, "dt_b"), (self.conv_b, "conv_b"), (self.skip, "d_skip"))]
        pairs.append((self.bout[:, :], w["bout"].rearrange("(o c) -> o c", o=1).to_broadcast([P, D])))
        for h in range(2):
            rows = slice(h * M, (h + 1) * M)
            pairs += [(t[rows, :], w[n]) for t, n in ((self.w1, "w1"), (self.b1, "b1"), (self.w2, "w2"),
                                                      (self.wout[h], "wout"))]
            pairs += [(self.cols[rows, k, :], w[n].rearrange("(m o) -> m o", o=1))
                      for k, n in enumerate(("b_in", "b2"))]
        for tile, source in pairs:
            sp.dma_start(tile, source).then_inc(loaded, 16)
        return 16 * len(pairs)


def project_qkv(nc, const, w, x, wq, wk_b, wkv_aT, wv_bT, turnT, qk_parts, v_ones):
    T0, T1, LATENT, Q0, Q1, K0, K1, V0, V1 = range(9)
    JOBS, PRODUCTS = 9, 7
    PAIR_OF = {T0: 0, T1: 1, LATENT: 2, Q0: 3, Q1: 0, K0: 1, K1: 2, V0: 3, V1: 1}
    BEFORE = {T0: Q1, T1: V1, LATENT: K1, Q0: V0, Q1: T0, K0: T1, K1: LATENT, V0: Q0, V1: K0}
    QK = (Q0, Q1, K0, K1)

    with ExitStack() as ctx:
        st = Stage(nc, ctx, "qkv")
        xt = [st.sb(f"x{u}", [P, TT, D]) for u in range(2)]
        norm = Norm(st)
        xnT = st.sb("xnT", [P, CB, T])
        latent = st.sb("latent", [P, T])
        parts = [st.sb(f"parts{u}", [P, len(QK), 3, T], BF16) for u in range(2)]
        rest = st.sb("rest", [P, len(QK), T])
        v = [st.sb(f"v{u}", [P, TT, NH, VW]) for u in range(2)]
        ident = const.ident
        wq_n = st.sb("wq", [P, CB, D])
        wkb_n = st.sb("wk_b", [P, CB, LAT])
        turn = st.sb("turn", [P, CB, P])
        wqT = st.sb("wqT", [P, CB, D])
        wkbT = st.sb("wk_bT", [P, D])
        wvbT = st.sb("wv_bT", [P, D])
        wkvaT = st.sb("wkv_aT", [P, CB, P])
        ps = [st.ps(f"p{i}", [P, PAIR]) for i in range(4)]

        weights = st.sem("weights")
        const_loaded = st.sem("const_loaded")
        x_loaded = [st.sem(f"x_loaded{u}") for u in range(2)]
        zeroed = st.sem("zeroed")
        ident_ready = st.sem("ident_ready")
        pads_ready = st.sem("pads_ready")
        ones_ready = st.sem("ones_ready")
        turned = st.sem("turned")
        turned_copied = st.sem("turned_copied")
        product = st.sem("product")
        act_read = st.sem("act_read")
        rest_ready = st.sem("rest_ready")
        mid_ready = st.sem("mid_ready")
        parts_ready = st.sem("parts_ready")
        parts_stored = [st.sem(f"parts_stored{u}") for u in range(2)]
        v_stored = [st.sem(f"v_stored{u}") for u in range(2)]
        block = ctx.enter_context(nc.Block())
        WEIGHTS = 16 * 5

        @block.sync
        def _(sp):
            sp.dma_start(xt[0][:, :, :], x[0].rearrange("(t p) c -> p t c", p=P)).then_inc(x_loaded[0], 16)
            sp.dma_start(wq_n[:, :, :], wq.rearrange("(a p) c -> p a c", p=P)).then_inc(weights, 16)
            sp.dma_start(wkb_n[:, :, :], wk_b.rearrange("(a p) c -> p a c", p=P)).then_inc(weights, 16)
            sp.dma_start(turn[:, :, :], turnT.rearrange("a p c -> p a c")).then_inc(weights, 16)
            sp.dma_start(wkvaT[:, :, :], wkv_aT.rearrange("(a p) c -> p a c", p=P)).then_inc(weights, 16)
            sp.wait_ge(pads_ready, 1)
            sp.dma_start(wvbT[LAT:P, :], wv_bT).then_inc(weights, 16)
            sp.dma_start(xt[1][:, :, :], x[1].rearrange("(t p) c -> p t c", p=P)).then_inc(x_loaded[1], 16)
            const_loads = const.load(sp, w, const_loaded)

            def batch(b, u, i, left):
                if left > 1:
                    sp.wait_ge(norm.xn_ready, b + 2)
                    sp.dma_start(xt[u][:, :, :], x[b + 2].rearrange("(t p) c -> p t c", p=P)).then_inc(x_loaded[u], 16)
                for k in range(len(QK)):
                    sp.wait_ge(parts_ready, 4 + 4 * b + k + 1)
                    sp.dma_start(qk_parts[b, k // 2, :, (k % 2) * P:(k % 2 + 1) * P, :].rearrange("a p t -> p a t"),
                                 parts[u][:, k, :, :]).then_inc(parts_stored[u], 16)
                sp.wait_ge(act_read, JOBS + JOBS * b + V1 + 1)
                sp.dma_start(v_ones[b], v[u][:, :, :, :].rearrange("p t h w -> p (t h w)")).then_inc(v_stored[u], 16)

            each_batch(sp, 2, batch)
            sp.wait_ge(const_loaded, const_loads)
            for u in range(2):
                sp.wait_ge(parts_stored[u], 64 * (NB // 2 + 1))
                sp.wait_ge(v_stored[u], 16 * (NB // 2 + 1))

        @block.gpsimd
        def _(pool):
            for h in range(2):
                nc.gpsimd.memset(const.wout[h][:, :], 0.0)
            nc.gpsimd.memset(wvbT[:, :], 0.0)
            nc.gpsimd.memset(wkbT[:, :], 0.0).then_inc(pads_ready, 1)
            pool.sem_inc(parts_ready, 4)
            norm.setup(nc, pool)
            make_identity(nc, pool, ident, zeroed, ident_ready)
            pool.wait_ge(x_loaded[0], 16)
            norm.gpsimd(nc, pool, 0, 0, xt[0])

            def batch(b, u, i, left):
                if left:
                    pool.wait_ge(x_loaded[1 - u], 16 * (i + 1 + u))
                    norm.gpsimd(nc, pool, b + 1, 1 - u, xt[1 - u])
                for k in range(len(QK)):
                    pool.wait_ge(mid_ready, 4 * b + k + 1)
                    pool.wait_ge(parts_stored[u], 64 * (i + 1))
                    nc.gpsimd.tensor_tensor(parts[u][:, k, 2, :], rest[:, k, :], parts[u][:, k, 1, :], ALU.subtract)\
                        .then_inc(parts_ready, 1)

            each_batch(pool, 2, batch)

        @block.vector
        def _(dve):
            dve.sem_inc(rest_ready, 4)
            for u in range(2):
                last = nc.vector.memset(v[u][:, :, :, HD:VW], 1.0)
            last.then_inc(ones_ready, 1)
            dve.wait_ge(x_loaded[0], 16)
            norm.vector(nc, dve, 0, 0, xt[0])

            def batch(b, u, i, left):
                if left:
                    dve.wait_ge(x_loaded[1 - u], 16 * (i + 1 + u))
                    norm.vector(nc, dve, b + 1, 1 - u, xt[1 - u])
                for k, job in enumerate(QK):
                    dve.wait_ge(act_read, JOBS + JOBS * b + job + 1)
                    dve.wait_ge(parts_ready, 4 * b + k + 1)
                    nc.vector.tensor_tensor(rest[:, k, :], ps[PAIR_OF[job]][:, :], parts[u][:, k, 0, :], ALU.subtract)\
                        .then_inc(rest_ready, 1)
                    dve.wait_ge(rest_ready, 4 + 4 * b + k + 1)
                    dve.wait_ge(parts_stored[u], 64 * (i + 1))
                    nc.vector.tensor_copy(parts[u][:, k, 1, :], rest[:, k, :]).then_inc(mid_ready, 1)

            each_batch(dve, 2, batch)

        @block.scalar
        def _(act):
            act.sem_inc(act_read, JOBS)
            for u in range(2):
                act.sem_inc(parts_stored[u], 64)
                act.sem_inc(v_stored[u], 16)
            act.wait_ge(pads_ready, 1)
            for c in range(CB):
                act.wait_ge(turned, c + 1)
                nc.scalar.activation(wqT[:, c, :], ps[c][:, 0:D], ACT.Copy).then_inc(turned_copied, 1)
            act.wait_ge(turned, 3)
            nc.scalar.activation(wkbT[0:LAT, :], ps[2][0:LAT, 0:D], ACT.Copy).then_inc(turned_copied, 1)
            act.wait_ge(ones_ready, 1)

            def batch(b, u, i, left):
                def read(job, out, in_):
                    if job in (T0, T1):
                        norm.wait_transposed(act, b, job - T0)
                    else:
                        act.wait_ge(product, PRODUCTS * b + job - LATENT + 1)
                    nc.scalar.activation(out, in_, ACT.Copy).then_inc(act_read, 1)

                for job in (T0, T1):
                    read(job, xnT[:, job - T0, :], ps[PAIR_OF[job]][:, :])
                read(LATENT, latent[:, :], ps[PAIR_OF[LATENT]][:, :])
                act.wait_ge(parts_stored[u], 64 * (i + 1))
                for k, job in enumerate(QK):
                    read(job, parts[u][:, k, 0, :], ps[PAIR_OF[job]][:, :])
                act.wait_ge(v_stored[u], 16 * (i + 1))
                for n, job in enumerate((V0, V1)):
                    read(job, v[u][:, 4 * n:4 * n + 4, :, 0:HD],
                         ps[PAIR_OF[job]][:, :].rearrange("p (t h d) -> p t h d", t=4, h=NH))

            each_batch(act, 2, batch)

        @block.tensor
        def _(pe):
            pe.wait_ge(weights, WEIGHTS)
            for c in range(CB):
                for f in range(CB):
                    last = nc.tensor.matmul(ps[c][:, f * P:(f + 1) * P], wq_n[:, f, c * P:(c + 1) * P],
                                            turn[:, f, :], start=True, stop=True)
                last.then_inc(turned, 1)
            for f in range(CB):
                last = nc.tensor.matmul(ps[2][0:LAT, f * P:(f + 1) * P], wkb_n[:, f, :], turn[:, f, :],
                                        start=True, stop=True)
            last.then_inc(turned, 1)
            pe.wait_ge(turned_copied, 3)
            pe.wait_ge(ident_ready, 1)

            def batch(b, u, i, left):
                def free(job):
                    old = BEFORE[job]
                    turn_ = b if old < job else b - 1
                    pe.wait_ge(act_read, JOBS + JOBS * turn_ + old + 1)
                    if old in QK:
                        pe.wait_ge(rest_ready, 4 + 4 * turn_ + QK.index(old) + 1)

                norm.tensor(nc, pe, b, u, ident, (ps[PAIR_OF[T0]], ps[PAIR_OF[T1]]), lambda c: free(T0 + c))

                def project(job, weight, source, blocks):
                    free(job)
                    for h in range(2):
                        for c in range(blocks):
                            last_m = nc.tensor.matmul(ps[PAIR_OF[job]][:, h * HALF:(h + 1) * HALF], weight(c),
                                                      source(c, h), start=c == 0, stop=c == blocks - 1)
                    last_m.then_inc(product, 1)

                half = lambda c, h: xnT[:, c, h * HALF:(h + 1) * HALF]
                pe.wait_ge(act_read, JOBS + JOBS * b + T1 + 1)
                project(LATENT, lambda c: wkvaT[:, c, :], half, CB)
                for f in range(CB):
                    project(Q0 + f, lambda c: wqT[:, c, f * P:(f + 1) * P], half, CB)
                pe.wait_ge(act_read, JOBS + JOBS * b + LATENT + 1)
                for f in range(CB):
                    project(K0 + f, lambda c: wkbT[:, f * P:(f + 1) * P],
                            lambda c, h: latent[:, h * HALF:(h + 1) * HALF], 1)
                for n, job in enumerate((V0, V1)):
                    free(job)
                    for t in range(4):
                        last_m = nc.tensor.matmul(ps[PAIR_OF[job]][:, t * D:(t + 1) * D],
                                                  latent[:, (4 * n + t) * P:(4 * n + t + 1) * P], wvbT[:, :],
                                                  start=True, stop=True)
                    last_m.then_inc(product, 1)

            each_batch(pe, 2, batch)


def attention(nc, const, qk_parts, v_ones, max_scratch, valuesT, sums_out):
    LEAD = 3
    SPANS = 2 * NG
    QT = HALF // P
    UNITS = GH * QT
    STEPS = TT
    BANK = (0, 1, 2, 0)
    SINCE = (1, 4, 4, 3)
    FULL = ROWS + 3
    SCALE = float(HD) ** -0.5

    with ExitStack() as ctx:
        st = Stage(nc, ctx, "attn")
        q = [st.sb(f"q{g}", [FULL, GH, T], BF16) for g in range(NG)]
        k = [st.sb(f"k{g}", [FULL, GH, T], BF16) for g in range(NG)]
        v = [st.sb(f"v{g}", [P, TT, GH * VW]) for g in range(NG)]
        probs = [st.sb(f"probs{i}", [P, GH, HALF]) for i in range(2)]
        maxima = [st.sb(f"maxima{i}", [P, 32]) for i in range(2)]
        maxT = [st.sb(f"maxT{i}", [P, 32]) for i in range(2)]
        max_rest = st.sb("max_rest", [P, 32])
        max_parts = [st.sb(f"max_parts{i}", [P, 3, 32], BF16) for i in range(2)]
        out = [st.sb(f"out{i}", [P, 2, HALF]) for i in range(2)]
        pick_f = st.sb("pick_f", [CROWS, NS, P])
        psT = [st.ps(f"scoresT{i}", [P, HALF]) for i in range(3)]
        psM = [st.ps(f"scores{i}", [P, PAIR]) for i in range(2)]
        psO = st.ps("out_sum", [P, HALF])

        qk_loaded = [st.sem(f"qk_loaded{g}") for g in range(NG)]
        v_loaded = [st.sem(f"v_loaded{g}") for g in range(NG)]
        ones_ready = st.sem("ones_ready")
        scores_ready = st.sem("scores_ready")
        maxima_read = st.sem("maxima_read")
        maxima_zeroed = st.sem("maxima_zeroed")
        maxT_ready = st.sem("maxT_ready")
        max_steps = st.sem("max_steps")
        max_stored = st.sem("max_stored")
        max_loaded = [st.sem(f"max_loaded{j}") for j in range(SPANS)]
        scoresT_ready = st.sem("scoresT_ready")
        exps_done = st.sem("exps_done")
        pv_done = st.sem("pv_done")
        out_copied = st.sem("out_copied")
        out_stored = [st.sem(f"out_stored{i}") for i in range(2)]
        pool_passed = st.sem("pool_passed")
        a_steps = st.sem("a_steps")
        pick_steps = st.sem("pick_steps")
        diag_ready = st.sem("diag_ready")
        block = ctx.enter_context(nc.Block())
        LOADS = 16 * 2 * SLOTS
        STORES = 16 * (GH + 1)

        @block.sync
        def _(sp):
            def load(b, g):
                for tile, which, slots in ((q, 0, Q_PARTS), (k, 1, K_PARTS)):
                    for s, part in enumerate(slots):
                        heads = qk_parts[b, which, part, g * GH * HD:(g + 1) * GH * HD, :]
                        sp.dma_start(tile[g][s * HD:(s + 1) * HD, :, :],
                                     heads.rearrange("(h d) t -> d h t", d=HD)).then_inc(qk_loaded[g], 16)
                sp.dma_start(v[g][:, :, :], v_ones[b].rearrange("p (t w) -> p t w", t=TT)
                             [:, :, g * GH * VW:(g + 1) * GH * VW]).then_inc(v_loaded[g], 16)

            def max_rows(b, j):
                n, j = SPANS * b + j, j % SPANS
                sp.wait_ge(max_steps, 4 * (n + 1))
                for r in range(4):
                    sp.dma_start(max_scratch[j, :, :, r, :].rearrange("a c r -> c a r"),
                                 max_parts[j % 2][r * 32:r * 32 + UNITS, :, :]).then_inc(max_stored, 16)
                sp.wait_ge(max_stored, 64 * (n + 1))
                sp.dma_start(q[j // 2][ROWS:FULL, :, (j % 2) * HALF:(j % 2 + 1) * HALF],
                             max_scratch[j].rearrange("a (h t) q r -> a h (t q r)", h=GH)).then_inc(max_loaded[j], 16)

            for g in range(NG):
                load(0, g)
                if g == NG - 2:
                    max_rows(0, 0)

            def batch(b, u, i, left):
                for g in range(NG):
                    n = NG * b + g
                    for j in (2 * g + 1, 2 * g + 2):
                        if left or j < SPANS:
                            max_rows(b, j)
                    if left:
                        sp.wait_ge(pv_done, 2 + 2 * STEPS * (n + 1))
                        load(b + 1, g)
                    sp.wait_ge(out_copied, 1 + 2 * (n + 1))
                    done = out[g % 2][:, :, :].rearrange("p a t -> p (a t)")
                    for h in range(GH):
                        row = g * GH * HD + h * HD
                        sp.dma_start(valuesT[b, row:row + HD, :], done[h * VW:h * VW + HD, :])\
                            .then_inc(out_stored[g % 2], 16)
                    sp.dma_start(sums_out[b, g * GH:(g + 1) * GH, :], done[HD:P:VW, :]).then_inc(out_stored[g % 2], 16)

            each_batch(sp, 1, batch)
            for i in range(2):
                sp.wait_ge(out_stored[i], STORES * (NB * NG // 2 + 1))

        @block.gpsimd
        def _(pool):
            for g in range(NG):
                last_m = nc.gpsimd.memset(k[g][ROWS:FULL, :, :], 1.0)
            last_m.then_inc(ones_ready, 1)
            pool.wait_ge(ones_ready, 1)

            def scan_constants():
                nc.gpsimd.memset(pick_f[:, :, :], 0.0).then_inc(pick_steps, 1)
                for part in range(3):
                    pool.wait_ge(pick_steps, part + 1)
                    nc.gpsimd.affine_select(out=pick_f[:, :, :], in_=pick_f[:, :, :], compare_op=ALU.not_equal,
                                            fill=1.0, base=-part * NS, pattern=[[-1, NS], [0, P]],
                                            channel_multiplier=1).then_inc(pick_steps, 1)
                pool.wait_ge(pick_steps, 4)
                nc.gpsimd.tensor_copy(const.pick[:, :, :], pick_f[:, :, :]).then_inc(pick_steps, 1)
                for d in range(DB):
                    nc.gpsimd.tensor_scalar(const.skip_diag[:, d, :], const.ident[:, :], const.skip[:, d:d + 1], 0.0,
                                            ALU.mult, ALU.add).then_inc(diag_ready, 1)
                pool.wait_ge(a_steps, 1)
                nc.gpsimd.tensor_scalar(const.a[:, :, :], const.a[:, :, :], -1.0, 0.0, ALU.mult, ALU.add)\
                    .then_inc(a_steps, 1)
                pool.wait_ge(pick_steps, 5)
                pool.wait_ge(diag_ready, DB)
                pool.wait_ge(a_steps, 2)

            def split(b, j):
                n, i = SPANS * b + j, j % 2
                pool.wait_ge(maxT_ready, n + 1)
                pool.wait_ge(max_steps, 4 * n)
                stand(pool, pool_passed)
                nc.gpsimd.tensor_scalar(max_parts[i][:, 0, :], maxT[i][:, :], 1.0, 0.0, ALU.mult, ALU.add)\
                    .then_inc(max_steps, 1)
                pool.wait_ge(max_steps, 4 * n + 1)
                nc.gpsimd.tensor_tensor(max_rest[:, :], maxT[i][:, :], max_parts[i][:, 0, :], ALU.subtract)\
                    .then_inc(max_steps, 1)
                pool.wait_ge(max_steps, 4 * n + 2)
                stand(pool, pool_passed)
                nc.gpsimd.tensor_scalar(max_parts[i][:, 1, :], max_rest[:, :], 1.0, 0.0, ALU.mult, ALU.add)\
                    .then_inc(max_steps, 1)
                pool.wait_ge(max_steps, 4 * n + 3)
                nc.gpsimd.tensor_tensor(max_parts[i][:, 2, :], max_rest[:, :], max_parts[i][:, 1, :], ALU.subtract)\
                    .then_inc(max_steps, 1)

            split(0, 0)
            scan_constants()

            def batch(b, u, i, left):
                for j in range(1, SPANS + 1):
                    if left or j < SPANS:
                        split(b, j)

            each_batch(pool, 1, batch)

        @block.vector
        def _(dve):
            dve.sem_inc(maxima_read, 2)

            for i in range(2):
                last_m = nc.vector.memset(maxima[i][:, :], 0.0)
            last_m.then_inc(maxima_zeroed, 1)
            dve.wait_ge(maxima_zeroed, 1)

            def unit(b, m):
                j, c = m // UNITS, m % UNITS
                n, i = SPANS * b + j, j % 2
                dve.wait_ge(scores_ready, UNITS * n + c + 1)
                if c == 0 and j > 0:
                    dve.wait_ge(maxT_ready, n)
                nc.vector.tensor_reduce(maxima[i][:, c:c + 1], psM[c % 2][:, :], AX.X, ALU.max, negate=True)\
                    .then_inc(maxima_read, 1)
                if c == UNITS - 1:
                    dve.wait_ge(maxima_read, 2 + UNITS * (n + 1))
                    nc.vector.transpose(maxT[i][:, :], maxima[i][:, :]).then_inc(maxT_ready, 1)

            for m in range(UNITS + 2 * LEAD):
                unit(0, m)

            def batch(b, u, i, left):
                for s in range(SPANS * STEPS):
                    for w in range(2):
                        m = UNITS + 2 * LEAD + 2 * s + w
                        if left or m < SPANS * UNITS:
                            unit(b, m)

            each_batch(dve, 1, batch)

        @block.scalar
        def _(act):
            nc.scalar.activation(const.a[:, :, :], const.a[:, :, :], ACT.Exp).then_inc(a_steps, 1)
            act.sem_inc(exps_done, GH)
            act.sem_inc(out_copied, 1)
            for n in range(2):
                act.sem_inc(out_stored[n], STORES)

            def copy_out(b, j):
                g = j // 2
                act.wait_ge(pv_done, 2 + STEPS * (SPANS * b + j + 1))
                if j % 2 == 0:
                    act.wait_ge(out_stored[g % 2], STORES * (NG // 2 * b + g // 2 + 1))
                nc.scalar.activation(out[g % 2][:, j % 2, :], psO[:, :], ACT.Copy).then_inc(out_copied, 1)

            def batch(b, u, i, left):
                for s in range(SPANS * STEPS):
                    if s % STEPS == 1 and s > 1:
                        copy_out(b, s // STEPS - 1)
                    for h in range(GH):
                        act.wait_ge(scoresT_ready, GH * (SPANS * STEPS * b + s) + h + 1)
                        if h == 0:
                            act.wait_ge(pv_done, SPANS * STEPS * b + s + 1)
                        nc.scalar.activation(probs[s % 2][:, h, :], psT[BANK[h]][:, :], ACT.Exp, scale=SCALE)\
                            .then_inc(exps_done, 1)
                copy_out(b, SPANS - 1)

            each_batch(act, 1, batch)

        @block.tensor
        def _(pe):
            pe.sem_inc(pv_done, 2)

            def unit_half(b, m, half):
                j, c = m // UNITS, m % UNITS
                n, g = SPANS * b + j, j // 2 % NG
                h, t = c // QT, c % QT
                if half == 0:
                    if c == 0 and j % 2 == 0:
                        pe.wait_ge(qk_loaded[g], LOADS * (b + 1 + j // SPANS))
                    pe.wait_ge(maxima_read, UNITS * n + c + 1)
                mm = nc.tensor.matmul(psM[c % 2][:, half * HALF:(half + 1) * HALF],
                                      q[g][0:ROWS, h, (j % 2) * HALF + t * P:(j % 2) * HALF + (t + 1) * P],
                                      k[g][0:ROWS, h, half * HALF:(half + 1) * HALF], start=True, stop=True)
                if half == 1:
                    mm.then_inc(scores_ready, 1)

            def values(b, s):
                j, kt = s // STEPS, s % STEPS
                g = j // 2
                pe.wait_ge(exps_done, GH + GH * (SPANS * STEPS * b + s + 1))
                if kt == 0:
                    pe.wait_ge(out_copied, SPANS * b + j + 1)
                    pe.wait_ge(v_loaded[g], 16 * (b + 1))
                for h in range(GH):
                    mm = nc.tensor.matmul(psO[h * VW:(h + 1) * VW, :], v[g][:, kt, h * VW:(h + 1) * VW],
                                          probs[s % 2][:, h, :], start=kt == 0, stop=kt == TT - 1)
                mm.then_inc(pv_done, 1)

            for m in range(UNITS + 2 * LEAD):
                for half in range(2):
                    unit_half(0, m, half)
            pe.wait_ge(ones_ready, 1)

            def batch(b, u, i, left):
                for s in range(SPANS * STEPS):
                    j, kt = s // STEPS, s % STEPS
                    g = j // 2
                    if kt == 0:
                        pe.wait_ge(max_loaded[j], 16 * (b + 1))
                    for h in range(GH):
                        pe.wait_ge(exps_done, GH + GH * (SPANS * STEPS * b + s) + h - SINCE[h] + 1)
                        nc.tensor.matmul(psT[BANK[h]][:, :], k[g][0:FULL, h, kt * P:(kt + 1) * P],
                                         q[g][0:FULL, h, (j % 2) * HALF:(j % 2 + 1) * HALF], start=True, stop=True)\
                            .then_inc(scoresT_ready, 1)
                        m = UNITS + 2 * LEAD + 2 * s + h // 2
                        if left or m < SPANS * UNITS:
                            unit_half(b, m, h % 2)
                    if s > 0:
                        values(b, s - 1)
                values(b, SPANS * STEPS - 1)

            each_batch(pe, 1, batch)


def residual_ffn(nc, const, name, x_in, branchT, branch_w, x_out, sums=None, recips=None):
    KB = branchT.shape[1] // P
    MIX0, MIX1, T0, T1, UNITS, OUT0, OUT1 = range(7)
    PAIR_OF = {MIX0: 0, MIX1: 1, T0: 2, T1: 3, UNITS: 0, OUT0: 3, OUT1: 2}
    BUF = 3
    RELUS = 4
    SUMS = INNER + 1

    with ExitStack() as ctx:
        st = Stage(nc, ctx, name)
        xt = [st.sb(f"x{u}", [P, TT, D]) for u in range(BUF)]
        branch = [st.sb(f"branch{u}", [P, KB, T]) for u in range(BUF)]
        norm = Norm(st, BUF)
        xnT = st.sb("xnT", [P, CB, T])
        s = [st.sb(f"s{u}", [P, HALF]) for u in range(BUF)]
        hidden = [st.sb(f"hidden{i}", [P, HALF]) for i in range(RELUS)]
        g = [st.sb(f"g{i}", [P, HALF]) for i in range(2)]
        ps = [st.ps(f"p{i}", [P, PAIR]) for i in range(4)]
        if sums is not None:
            all_sums = st.sb("all_sums", [P, NB, NH * T // P])
            all_recips = st.sb("all_recips", [P, NB, NH * T // P])
            recip = [st.sb(f"recip{u}", [P, KB, T]) for u in range(BUF)]
            sums_loaded = st.sem("sums_loaded")
            recips_ready = st.sem("recips_ready")
            recips_stored = st.sem("recips_stored")
            scaled = st.sem("scaled")

        x_loaded = [st.sem(f"x_loaded{u}") for u in range(BUF)]
        branch_loaded = [st.sem(f"branch_loaded{u}") for u in range(BUF)]
        x_stored = [st.sem(f"x_stored{u}") for u in range(BUF)]
        mixed = st.sem("mixed")
        added = st.sem("added")
        copied = st.sem("copied")
        units_ready = st.sem("units_ready")
        biased = st.sem("biased")
        relu_ready = st.sem("relu_ready")
        summed = st.sem("summed")
        out_ready = st.sem("out_ready")
        x_ready = st.sem("x_ready")
        block = ctx.enter_context(nc.Block())
        HEADS = P // HD
        BRANCH_LOADS = 16 * (1 + (KB if sums is not None else 0))
        SOME = (slice(0, 1), slice(1, 2), slice(2, NB))
        by_part = lambda a: a.rearrange("b h (q t) -> (h q) b t", q=P // NH)
        tokens = lambda a: a.rearrange("(t p) c -> p t c", p=P)

        def ahead(u, i, n):
            return (u + n) % BUF, i + (u + n) // BUF

        @block.sync
        def _(sp):
            def load_x(b, u):
                sp.dma_start(xt[u][:, :, :], tokens(x_in[b])).then_inc(x_loaded[u], 16)

            def load_branch(b, u):
                sp.dma_start(branch[u][:, :, :], branchT[b].rearrange("(a p) t -> p a t", p=P))\
                    .then_inc(branch_loaded[u], 16)

            def load_recips(b, u):
                if sums is not None:
                    for c in range(KB):
                        sp.dma_start(recip[u][:, c, :], recips[b, c * HEADS:(c + 1) * HEADS, :].unsqueeze(1)
                                     .to_broadcast([HEADS, HD, T])).then_inc(branch_loaded[u], 16)

            if sums is not None:
                sp.dma_start(all_sums[:, :, :], by_part(sums)).then_inc(sums_loaded, 16)
            load_branch(0, 0)
            for n in range(2):
                if sums is not None:
                    sp.wait_ge(recips_ready, n + 1)
                    sp.dma_start(by_part(recips)[:, SOME[n], :], all_recips[:, SOME[n], :]).then_inc(recips_stored, 16)
                    sp.wait_ge(recips_stored, 16 * (n + 1))
                    load_recips(n, n)
                load_x(n, n)
                if n == 0:
                    load_branch(1, 1)
            if sums is not None:
                sp.wait_ge(recips_ready, 3)
                sp.dma_start(by_part(recips)[:, SOME[2], :], all_recips[:, SOME[2], :]).then_inc(recips_stored, 16)
                sp.wait_ge(recips_stored, 16 * 3)

            def batch(b, u, i, left):
                if left > 1:
                    u2, i2 = ahead(u, i, 2)
                    sp.wait_ge(mixed, 2 + 2 * b)
                    load_branch(b + 2, u2)
                    load_recips(b + 2, u2)
                    sp.wait_ge(x_stored[u2], 16 * (i2 + 1))
                    load_x(b + 2, u2)

            each_batch(sp, BUF, batch)
            for u in range(BUF):
                sp.wait_ge(x_stored[u], 16 * (len(range(u, NB, BUF)) + 1))

        @block.gpsimd
        def _(pool):
            norm.setup(nc, pool)

            def scale(b, u, i):
                if sums is not None:
                    pool.wait_ge(branch_loaded[u], BRANCH_LOADS * (i + 1))
                    for c in range(KB):
                        tile = branch[u][:, c, :]
                        nc.gpsimd.tensor_tensor(tile, tile, recip[u][:, c, :], ALU.mult).then_inc(scaled, 1)

            scale(0, 0, 0)
            scale(1, 1, 0)
            norm.gpsimd(nc, pool, 0, 0, xt[0])

            def batch(b, u, i, left):
                if left > 1:
                    scale(b + 2, *ahead(u, i, 2))
                if left:
                    u1 = ahead(u, i, 1)[0]
                    norm.gpsimd(nc, pool, b + 1, u1, xt[u1])
                else:
                    pool.wait_ge(norm.xn_ready, b + 2)
                for n in range(4):
                    tiles = xt[u][:, 2 * n:2 * n + 2, :]
                    nc.gpsimd.tensor_tensor(tiles, tiles, const.bout[:, :].unsqueeze(1).to_broadcast([P, 2, D]),
                                            ALU.add)\
                        .then_inc(biased, 1)

            each_batch(pool, BUF, batch)

        @block.vector
        def _(dve):
            dve.sem_inc(summed, RELUS)
            dve.sem_inc(out_ready, 2)
            dve.sem_inc(x_ready, 4)
            if sums is not None:
                dve.wait_ge(sums_loaded, 16)
                for some in SOME:
                    nc.vector.reciprocal(all_recips[:, some, :], all_sums[:, some, :]).then_inc(recips_ready, 1)

            def front(b, u, i):
                dve.wait_ge(x_loaded[u], 16 * (i + 1))
                for n in range(4):
                    if n % 2 == 0:
                        dve.wait_ge(mixed, 2 + 2 * b + n // 2 + 1)
                    tiles = xt[u][:, 2 * n:2 * n + 2, :]
                    nc.vector.tensor_tensor(tiles, tiles, ps[PAIR_OF[MIX0 + n // 2]]
                                            [:, (n % 2) * HALF:(n % 2 + 1) * HALF]
                                            .rearrange("p (t c) -> p t c", t=2), ALU.add).then_inc(added, 1)
                dve.wait_ge(added, 4 * (b + 1))
                norm.vector(nc, dve, b, u, xt[u])

            front(0, 0, 0)
            front(1, 1, 0)

            def batch(b, u, i, left):
                for j in range(INNER):
                    dve.wait_ge(relu_ready, INNER * b + j + 1)
                    if j > 0:
                        dve.wait_ge(summed, RELUS + SUMS * b + max(j - 1, 0))
                    terms = hidden[j % RELUS][:, :]
                    if j == 0:
                        dve.wait_ge(out_ready, 2 * b + 2)
                        ins = nc.vector.tensor_scalar(g[0][:, :], terms, const.w2[:, j:j + 1], const.cols[:, 1, :],
                                                      ALU.mult, ALU.add)
                    elif j == 1:
                        ins = nc.vector.tensor_scalar(g[1][:, :], terms, const.w2[:, j:j + 1], None, ALU.mult)
                    else:
                        ins = nc.vector.scalar_tensor_tensor(g[j % 2][:, :], terms, const.w2[:, j:j + 1],
                                                             g[j % 2][:, :], ALU.mult, ALU.add)
                    ins.then_inc(summed, 1)
                dve.wait_ge(summed, RELUS + SUMS * b + INNER)
                nc.vector.tensor_tensor(g[0][:, :], g[0][:, :], g[1][:, :], ALU.add).then_inc(summed, 1)
                if left > 1:
                    u2, i2 = ahead(u, i, 2)
                    front(b + 2, u2, i2)
                dve.wait_ge(biased, 4 * (b + 1))
                for n in range(4):
                    if n % 2 == 0:
                        dve.wait_ge(out_ready, 2 + 2 * b + n // 2 + 1)
                    tiles = xt[u][:, 2 * n:2 * n + 2, :]
                    nc.vector.tensor_tensor(tiles, tiles, ps[PAIR_OF[OUT0 + n // 2]]
                                            [:, (n % 2) * HALF:(n % 2 + 1) * HALF]
                                            .rearrange("p (t c) -> p t c", t=2), ALU.add).then_inc(x_ready, 1)

            each_batch(dve, BUF, batch)

        @block.scalar
        def _(act):
            for u in range(BUF):
                act.sem_inc(x_stored[u], 16)

            def copy_transposed(b):
                for c in range(CB):
                    norm.wait_transposed(act, b, c)
                    nc.scalar.activation(xnT[:, c, :], ps[PAIR_OF[T0 + c]][:, :], ACT.Copy).then_inc(copied, 1)

            def copy_units(b, u):
                act.wait_ge(units_ready, b + 1)
                nc.scalar.activation(s[u][:, :], ps[PAIR_OF[UNITS]][:, 0:HALF], ACT.Identity, bias=const.cols[:, 0, :])\
                    .then_inc(copied, 1)

            def relu(b, u, j):
                act.wait_ge(summed, SUMS * b + j + 1)
                nc.scalar.activation(hidden[j % RELUS][:, :], s[u][:, :], ACT.Relu, bias=const.b1[:, j:j + 1],
                                     scale=const.w1[:, j:j + 1]).then_inc(relu_ready, 1)

            copy_transposed(0)
            copy_units(0, 0)
            act.wait_ge(copied, 3)
            for j in range(RELUS):
                relu(0, 0, j)

            def batch(b, u, i, left):
                for j in range(RELUS, INNER):
                    relu(b, u, j)
                if left:
                    u1 = ahead(u, i, 1)[0]
                    copy_transposed(b + 1)
                    copy_units(b + 1, u1)
                    act.wait_ge(copied, 3 * (b + 2))
                    for j in range(RELUS):
                        relu(b + 1, u1, j)
                act.wait_ge(x_ready, 4 + 4 * (b + 1))
                act.dma_start(tokens(x_out[b]), xt[u][:, :, :]).then_inc(x_stored[u], 16)

            each_batch(act, BUF, batch)

        @block.tensor
        def _(pe):
            pe.sem_inc(mixed, 2)

            def tiles(job, n, source, weight, blocks, done):
                for t in range(4):
                    for c in range(blocks):
                        mm = nc.tensor.matmul(ps[PAIR_OF[job]][:, t * D:(t + 1) * D], source(c, 4 * n + t), weight(c),
                                              start=c == 0, stop=c == blocks - 1)
                mm.then_inc(done, 1)

            def mix(b, u, i, n):
                if n == 0:
                    if sums is not None:
                        pe.wait_ge(scaled, KB * (b + 1))
                    else:
                        pe.wait_ge(branch_loaded[u], BRANCH_LOADS * (i + 1))
                tiles(MIX0 + n, n, lambda c, t: branch[u][:, c, t * P:(t + 1) * P], lambda c: branch_w[:, c, :], KB, mixed)

            def transposes(b, u, free):
                norm.tensor(nc, pe, b, u, const.ident, (ps[PAIR_OF[T0]], ps[PAIR_OF[T1]]), free)

            def units(b):
                pe.wait_ge(copied, 3 * b + 2)
                for h in range(2):
                    for c in range(CB):
                        mm = nc.tensor.matmul(ps[PAIR_OF[UNITS]][h * M:(h + 1) * M, 0:HALF], const.win[:, c, :],
                                              xnT[:, c, h * HALF:(h + 1) * HALF], start=c == 0, stop=c == CB - 1)
                mm.then_inc(units_ready, 1)

            for b in range(2):
                for n in range(2):
                    if b > 0:
                        pe.wait_ge(added, 2 * n + 2)
                    mix(b, b, 0, n)
            transposes(0, 0, lambda c: None)
            pe.wait_ge(added, 4 + 2)
            units(0)

            def batch(b, u, i, left):
                u1, u2, i2 = ahead(u, i, 1)[0], *ahead(u, i, 2)
                if left > 1:
                    pe.wait_ge(copied, 3 * (b + 1))
                    mix(b + 2, u2, i2, 0)
                if left:
                    transposes(b + 1, u1, lambda c: pe.wait_ge(x_ready, 4 + 4 * b - 2 * c))
                if left > 1:
                    pe.wait_ge(added, 4 * (b + 2))
                    mix(b + 2, u2, i2, 1)
                pe.wait_ge(summed, RELUS + SUMS * (b + 1))
                if left:
                    pe.wait_ge(copied, 3 * (b + 1) + 2)
                else:
                    pe.wait_ge(x_ready, 4 + 4 * b)
                for n in range(2):
                    tiles(OUT0 + n, n, lambda c, t: g[0][:, (t % 4) * P:(t % 4 + 1) * P], lambda c: const.wout[n][:, :],
                          1, out_ready)
                if left:
                    if left > 1:
                        pe.wait_ge(added, 4 * (b + 2) + 2)
                    units(b + 1)

            each_batch(pe, BUF, batch)


def project_scan(nc, const, x, xc_out, dt_out, dtx_out, b_out, c_parts):
    PRODUCTS = 2 * DB + 1
    T_PAIRS = (0, 1)
    BC_PAIR = 2
    X_PAIR, DT_PAIR = (0, 2, 0, 2), (3, 1, 3, 1)
    PAD = TAPS - 1

    with ExitStack() as ctx:
        st = Stage(nc, ctx, "prep")
        xt = [st.sb(f"x{u}", [P, TT, D]) for u in range(2)]
        norm = Norm(st)
        xnT = [st.sb(f"xnT{u}", [P, CB, T]) for u in range(2)]
        xi = [st.sb(f"xi{i}", [P, PAD + T]) for i in range(2)]
        conv = [st.sb(f"conv{d}", [P, T]) for d in range(DB)]
        xc = [st.sb(f"xc{d}", [P, T]) for d in range(DB)]
        soft = [st.sb(f"soft{i}", [P, T]) for i in range(2)]
        relu = [st.sb(f"relu{i}", [P, T]) for i in range(2)]
        dt = [st.sb(f"dt{i}", [P, T]) for i in range(2)]
        dtx = [st.sb(f"dtx{i}", [P, T]) for i in range(2)]
        bc = st.sb("bc", [2 * NS, T])
        bc_rest = st.sb("bc_rest", [2 * NS, T])
        bc_parts = st.sb("bc_parts", [2 * NS, 3, T], BF16)
        xw, dtw, bcw, dtb, cw, cb = const.x_w, const.dt_w, const.bc_w, const.dt_b, const.conv_w, const.conv_b
        ps = [st.ps(f"p{i}", [P, PAIR]) for i in range(4)]

        pads_ready = st.sem("pads_ready")
        x_loaded = [st.sem(f"x_loaded{u}") for u in range(2)]
        xnT_ready = st.sem("xnT_ready")
        product = st.sem("product")
        xi_ready = st.sem("xi_ready")
        tap0_ready = st.sem("tap0_ready")
        conv_steps = st.sem("conv_steps")
        xc_ready = st.sem("xc_ready")
        bc_hi = st.sem("bc_hi")
        bc_rested = st.sem("bc_rested")
        bc_steps = st.sem("bc_steps")
        relu_ready = st.sem("relu_ready")
        soft_steps = st.sem("soft_steps")
        dt_ready = st.sem("dt_ready")
        dtx_ready = st.sem("dtx_ready")
        xc_stored = [st.sem(f"xc_stored{d}") for d in range(DB)]
        dt_stored = [st.sem(f"dt_stored{i}") for i in range(2)]
        dtx_stored = [st.sem(f"dtx_stored{i}") for i in range(2)]
        b_stored = st.sem("b_stored")
        c_stored = st.sem("c_stored")
        block = ctx.enter_context(nc.Block())
        tokens = lambda a: a.rearrange("(t p) c -> p t c", p=P)

        @block.sync
        def _(sp):
            def load(b, u):
                sp.dma_start(xt[u][:, :, :], tokens(x[b])).then_inc(x_loaded[u], 16)

            load(0, 0)
            load(1, 1)

            rows = lambda d: slice(d * P, (d + 1) * P)

            def batch(b, u, i, left):
                sp.wait_ge(bc_hi, 2 + 2 * (b + 1))
                sp.dma_start(b_out[b], bc[0:NS, :]).then_inc(b_stored, 16)
                for d in range(DB):
                    sp.wait_ge(xc_ready, DB + DB * b + d + 1)
                    sp.dma_start(xc_out[b, rows(d), :], xc[d][:, :]).then_inc(xc_stored[d], 16)
                sp.wait_ge(bc_steps, 2 * (b + 2))
                sp.dma_start(c_parts[b].rearrange("a s t -> s a t"), bc_parts[NS:2 * NS, :, :]).then_inc(c_stored, 16)
                for d in range(DB):
                    sp.wait_ge(dt_ready, DB + DB * b + d + 1)
                    sp.dma_start(dt_out[b, rows(d), :], dt[d % 2][:, :]).then_inc(dt_stored[d % 2], 16)
                    sp.wait_ge(dtx_ready, DB + DB * b + d + 1)
                    sp.dma_start(dtx_out[b, rows(d), :], dtx[d % 2][:, :]).then_inc(dtx_stored[d % 2], 16)

            each_batch(sp, 2, batch)
            for d in range(DB):
                sp.wait_ge(xc_stored[d], 16 * (NB + 1))
            for n in range(2):
                sp.wait_ge(dt_stored[n], 16 * (DB // 2 * NB + 1))
                sp.wait_ge(dtx_stored[n], 16 * (DB // 2 * NB + 1))
            sp.wait_ge(b_stored, 16 * (NB + 1))
            sp.wait_ge(c_stored, 16 * (NB + 1))

        @block.gpsimd
        def _(pool):
            for n in range(2):
                last_m = nc.gpsimd.memset(xi[n][:, 0:PAD], 0.0)
            last_m.then_inc(pads_ready, 1)
            norm.setup(nc, pool)
            pool.sem_inc(dt_ready, DB)
            pool.sem_inc(dtx_ready, DB)
            for b in range(2):
                norm.gpsimd(nc, pool, b, b, xt[b])

            def batch(b, u, i, left):
                for d in range(DB):
                    n = d % 2
                    pool.wait_ge(relu_ready, DB + DB * b + d + 1)
                    pool.wait_ge(soft_steps, 3 * DB + 3 * (DB * b + d + 1))
                    pool.wait_ge(dt_stored[n], 16 * (DB // 2 * b + d // 2 + 1))
                    nc.gpsimd.tensor_tensor(dt[n][:, :], relu[n][:, :], soft[n][:, :], ALU.add).then_inc(dt_ready, 1)
                    pool.wait_ge(dt_ready, DB + DB * b + d + 1)
                    pool.wait_ge(xc_ready, DB + DB * b + d + 1)
                    pool.wait_ge(dtx_stored[n], 16 * (DB // 2 * b + d // 2 + 1))
                    nc.gpsimd.tensor_tensor(dtx[n][:, :], dt[n][:, :], xc[d][:, :], ALU.mult).then_inc(dtx_ready, 1)
                    if d == 0 and left > 1:
                        norm.gpsimd(nc, pool, b + 2, u, xt[u])

            each_batch(pool, 2, batch)

        @block.vector
        def _(dve):
            dve.sem_inc(conv_steps, 6)
            dve.sem_inc(bc_steps, 2)
            dve.sem_inc(bc_rested, 1)
            dve.sem_inc(relu_ready, DB)
            for b in range(2):
                dve.wait_ge(x_loaded[b], 16)
                norm.vector(nc, dve, b, b, xt[b])

            def taps(b, d):
                n = d % 2
                dve.wait_ge(xi_ready, DB * b + d + 1)
                dve.wait_ge(tap0_ready, DB * b + d + 1)
                for k in range(1, TAPS):
                    lag = PAD - k
                    if k > 1:
                        dve.wait_ge(conv_steps, 6 + 3 * (DB * b + d) + k - 1)
                    nc.vector.scalar_tensor_tensor(conv[d][:, :], xi[n][:, lag:lag + T], cw[:, d, lag:lag + 1],
                                                   conv[d][:, :], ALU.mult, ALU.add).then_inc(conv_steps, 1)

            for d in range(DB):
                taps(0, d)

            def batch(b, u, i, left):
                dve.wait_ge(bc_hi, 2 + 2 * (b + 1))
                dve.wait_ge(bc_steps, 2 * b + 2)
                nc.vector.tensor_tensor(bc_rest[:, :], ps[BC_PAIR][0:2 * NS, :], bc_parts[:, 0, :], ALU.subtract)\
                    .then_inc(bc_rested, 1)
                dve.wait_ge(bc_rested, 1 + b + 1)
                dve.wait_ge(c_stored, 16 * (b + 1))
                nc.vector.tensor_copy(bc_parts[:, 1, :], bc_rest[:, :]).then_inc(bc_steps, 1)
                dve.wait_ge(bc_steps, 2 + 2 * b + 1)
                nc.vector.tensor_tensor(bc_parts[:, 2, :], bc_rest[:, :], bc_parts[:, 1, :], ALU.subtract)\
                    .then_inc(bc_steps, 1)
                if left > 1:
                    dve.wait_ge(x_loaded[u], 16 * (i + 2))
                    norm.vector(nc, dve, b + 2, u, xt[u])
                for d in range(DB):
                    dve.wait_ge(soft_steps, 3 * (DB + DB * b + d) + 1)
                    dve.wait_ge(dt_ready, DB * b + d + 3)
                    nc.vector.tensor_scalar(relu[d % 2][:, :], ps[DT_PAIR[d]][:, :], dtb[:, d:d + 1], 0.0,
                                            ALU.add, ALU.max).then_inc(relu_ready, 1)
                    if left:
                        taps(b + 1, d)

            each_batch(dve, 2, batch)

        @block.scalar
        def _(act):
            act.sem_inc(xc_ready, DB)
            act.sem_inc(bc_hi, 2)
            act.sem_inc(soft_steps, 3 * DB)
            for s in (*xc_stored, *dt_stored, *dtx_stored, b_stored, c_stored):
                act.sem_inc(s, 16)
            act.wait_ge(pads_ready, 1)

            def transposed(b, u):
                for c in range(CB):
                    norm.wait_transposed(act, b, c)
                    nc.scalar.activation(xnT[u][:, c, :], ps[T_PAIRS[c]][:, :], ACT.Copy).then_inc(xnT_ready, 1)

            def conv_input(b, d, products):
                act.wait_ge(product, products)
                act.wait_ge(conv_steps, 3 * (DB * b + d + 1))
                nc.scalar.activation(xi[d % 2][:, PAD:PAD + T], ps[X_PAIR[d]][:, :], ACT.Copy).then_inc(xi_ready, 1)
                act.wait_ge(xc_ready, DB * b + d + 1)
                nc.scalar.activation(conv[d][:, :], ps[X_PAIR[d]][:, :], ACT.Identity, scale=cw[:, d, PAD:PAD + 1],
                                     bias=cb[:, d:d + 1]).then_inc(tap0_ready, 1)

            transposed(0, 0)
            for d in range(DB):
                conv_input(0, d, d + 1)

            def batch(b, u, i, left):
                nc.scalar.preload_act_table_set("silu_and_others")
                if left > 1:
                    act.wait_ge(norm.xn_ready, b + 2)
                    act.dma_start(xt[u][:, :, :], tokens(x[b + 2])).then_inc(x_loaded[u], 16)
                if left:
                    act.wait_ge(product, DB + PRODUCTS * b - 1)
                    transposed(b + 1, 1 - u)
                act.wait_ge(product, DB + PRODUCTS * b + 1)
                act.wait_ge(b_stored, 16 * (b + 1))
                nc.scalar.activation(bc[:, :], ps[BC_PAIR][0:2 * NS, :], ACT.Copy).then_inc(bc_hi, 1)
                act.wait_ge(c_stored, 16 * (b + 1))
                nc.scalar.activation(bc_parts[:, 0, :], ps[BC_PAIR][0:2 * NS, :], ACT.Copy).then_inc(bc_hi, 1)
                for d in range(DB):
                    act.wait_ge(conv_steps, 6 + 3 * (DB * b + d + 1))
                    act.wait_ge(xc_stored[d], 16 * (b + 1))
                    act.wait_ge(dtx_ready, DB * b + d + 1)
                    nc.scalar.activation(xc[d][:, :], conv[d][:, :], ACT.Silu).then_inc(xc_ready, 1)
                nc.scalar.preload_act_table_set("natural_log_exp_and_others")
                for d in range(DB):
                    t = soft[d % 2][:, :]
                    steps = 3 * (DB + DB * b + d)
                    act.wait_ge(product, DB + PRODUCTS * b + (2 * d if left else d) + 2)
                    act.wait_ge(dt_ready, DB * b + d + 3)
                    nc.scalar.activation(t, ps[DT_PAIR[d]][:, :], ACT.Abs, bias=dtb[:, d:d + 1]).then_inc(soft_steps, 1)
                    if left:
                        conv_input(b + 1, d, DB + PRODUCTS * b + 2 * d + 3)
                    act.wait_ge(soft_steps, steps + 1)
                    nc.scalar.activation(t, t, ACT.Exp, scale=-1.0).then_inc(soft_steps, 1)
                    act.wait_ge(soft_steps, steps + 2)
                    nc.scalar.activation(t, t, ACT.Ln, bias=1.0).then_inc(soft_steps, 1)

            each_batch(act, 2, batch)

        @block.tensor
        def _(pe):

            def project(pair, u, w, at, rows=P):
                for h in range(2):
                    for c in range(CB):
                        mm = nc.tensor.matmul(ps[pair][0:rows, h * HALF:(h + 1) * HALF],
                                              w[:, c, at:at + rows], xnT[u][:, c, h * HALF:(h + 1) * HALF],
                                              start=c == 0, stop=c == CB - 1)
                mm.then_inc(product, 1)

            def project_x(b, u, d):
                if d == 0:
                    pe.wait_ge(xnT_ready, CB * (b + 1))
                elif d > 1:
                    pe.wait_ge(tap0_ready, DB * b + d - 1)
                project(X_PAIR[d], u, xw, d * P)

            norm.tensor(nc, pe, 0, 0, const.ident, [ps[n] for n in T_PAIRS], lambda c: None)
            for d in range(DB):
                project_x(0, 0, d)

            def batch(b, u, i, left):
                def free(c):
                    if c == 0:
                        pe.wait_ge(tap0_ready, DB * b + 3)
                    else:
                        pe.wait_ge(relu_ready, DB + DB * b)

                if left:
                    norm.tensor(nc, pe, b + 1, 1 - u, const.ident, [ps[n] for n in T_PAIRS], free)
                pe.wait_ge(tap0_ready, DB * (b + 1))
                project(BC_PAIR, u, bcw, 0, 2 * NS)
                for d in range(DB):
                    if d == 1:
                        if left:
                            pe.wait_ge(xnT_ready, CB * (b + 2))
                        else:
                            pe.wait_ge(relu_ready, DB + DB * b)
                    else:
                        pe.wait_ge(relu_ready, DB + DB * b + d - 1)
                    project(DT_PAIR[d], u, dtw, d * P)
                    if left:
                        if d == 1:
                            pe.wait_ge(bc_rested, 1 + b + 1)
                        project_x(b + 1, 1 - u, d)

            each_batch(pe, 2, batch)


def scan(nc, const, xc_in, dt_in, dtx_in, b_in, c_parts, yT):
    QS = 4
    PIECES = 4
    AHEAD = 3
    STEPS = DB * NS
    NU, NST, NGB = 8, 4, 4

    with ExitStack() as ctx:
        st = Stage(nc, ctx, "scan")
        dt = [st.sb(f"dt{i}", [P, T]) for i in range(2)]
        dtx = [st.sb(f"dtx{i}", [P, T]) for i in range(2)]
        xc = [st.sb(f"xc{i}", [P, T]) for i in range(2)]
        bb = [st.sb(f"b{i}", [P, QS, T]) for i in range(NS // QS)]
        c = [st.sb(f"c{i}", [CROWS, T], BF16) for i in range(2)]
        ins = [st.sb(f"in{i}", [P, T]) for i in range(NU)]
        h = [st.sb(f"h{i}", [P, T]) for i in range(NST)]
        hc = [st.sb(f"hc{i}", [P, T]) for i in range(NGB)]
        y = [st.sb(f"y{i}", [P, T]) for i in range(2)]
        psA = [st.ps(f"decay{i}", [P, PAIR]) for i in range(2)]
        psC = st.ps("c_wide", [P, PAIR])
        psY = st.ps("y_sum", [P, PAIR])

        c_zeroed = st.sem("c_zeroed")
        block_loaded = [st.sem(f"block_loaded{i}") for i in range(2)]
        b_loaded = [st.sem(f"b_loaded{i}") for i in range(NS // QS)]
        b_first = [st.sem(f"b_first{s}") for s in range(QS)]
        c_loaded = [st.sem(f"c_loaded{i}") for i in range(2)]
        decay_ready = st.sem("decay_ready")
        in_ready = st.sem("in_ready")
        scanned = st.sem("scanned")
        c_wide = st.sem("c_wide")
        hc_ready = st.sem("hc_ready")
        summed = st.sem("summed")
        y_ready = st.sem("y_ready")
        y_stored = [st.sem(f"y_stored{i}") for i in range(2)]
        block = ctx.enter_context(nc.Block())

        @block.sync
        def _(sp):
            rows = lambda d: slice(d * P, (d + 1) * P)

            def load_block(b, d):
                for tile, source in ((dtx, dtx_in), (dt, dt_in), (xc, xc_in)):
                    sp.dma_start(tile[d % 2][:, :], source[b, rows(d), :]).then_inc(block_loaded[d % 2], 16)

            def load_b(b, n):
                sp.dma_start(bb[n][:, :, :], b_in[b, n * QS:(n + 1) * QS, :].unsqueeze(0).to_broadcast([P, QS, T]))\
                    .then_inc(b_loaded[n], 16)

            def load_c(b, u):
                sp.dma_start(c[u][0:3 * NS, :], c_parts[b].rearrange("a s t -> (a s) t")).then_inc(c_loaded[u], 16)

            load_block(0, 0)
            sp.wait_ge(c_zeroed, 1)
            load_c(0, 0)
            for n in range(NS // QS):
                if n == 0:
                    for s in range(QS):
                        sp.dma_start(bb[0][:, s, :], b_in[0, s:s + 1, :].to_broadcast([P, T])).then_inc(b_first[s], 16)
                else:
                    load_b(0, n)
            load_c(1, 1)
            load_block(0, 1)

            def batch(b, u, i, left):
                for d in range(DB):
                    if d == DB - 1 and left:
                        for n in range(NS // QS):
                            sp.wait_ge(in_ready, STEPS * b + d * NS + (n + 1) * QS)
                            load_b(b + 1, n)
                    sp.wait_ge(y_ready, 2 + 2 * (DB * b + d + 1))
                    sp.dma_start(yT[b, rows(d), :], y[d % 2][:, :]).then_inc(y_stored[d % 2], 16)
                    if left or d < DB - 2:
                        load_block(b + (d + 2) // DB, (d + 2) % DB)
                if left > 1:
                    sp.wait_ge(c_wide, STEPS * (b + 1))
                    load_c(b + 2, u)

            each_batch(sp, 2, batch)
            for n in range(2):
                sp.wait_ge(y_stored[n], 16 * (NB * DB // 2 + 1))

        @block.gpsimd
        def _(pool):
            for n in range(2):
                last_m = nc.gpsimd.memset(c[n][:, :], 0.0)
            last_m.then_inc(c_zeroed, 1)
            def step(b, n, loaded=None):
                d, s = n // NS, n % NS
                if s == 0:
                    pool.wait_ge(block_loaded[d % 2], 48 * (DB // 2 * b + d // 2 + 1))
                if loaded is not None:
                    pool.wait_ge(loaded, 16)
                elif d == 0 and s % QS == 0:
                    pool.wait_ge(b_loaded[s // QS], 16 * (b + 1))
                pool.wait_ge(scanned, STEPS * b + n + 1)
                nc.gpsimd.tensor_tensor(ins[n % NU][:, :], dtx[d % 2][:, :], bb[s // QS][:, s % QS, :],
                                        ALU.mult).then_inc(in_ready, 1)

            pool.sem_inc(b_loaded[0], 16)
            for n in range(QS):
                step(0, n, b_first[n])

            def batch(b, u, i, left):
                for n in range(QS, STEPS + QS):
                    if left or n < STEPS:
                        step(b + n // STEPS, n % STEPS)

            each_batch(pool, 2, batch)

        @block.vector
        def _(dve):
            dve.sem_inc(scanned, NU)
            dve.sem_inc(hc_ready, NST)
            def recur(b, n):
                dve.wait_ge(decay_ready, STEPS * b + n + 1)
                dve.wait_ge(in_ready, STEPS * b + n + 1)
                dve.wait_ge(hc_ready, STEPS * b + n + 1)
                nc.vector.tensor_tensor_scan(h[n % NST][:, :], psA[n % 2][:, :], ins[n % NU][:, :],
                                             0.0, ALU.mult, ALU.add).then_inc(scanned, 1)

            def weigh(b, n):
                dve.wait_ge(c_wide, STEPS * b + n + 1)
                dve.wait_ge(scanned, NU + STEPS * b + n + 1)
                dve.wait_ge(summed, 2 * (STEPS * b + n + 1))
                nc.vector.tensor_tensor(hc[n % NGB][:, :], h[n % NST][:, :], psC[:, :], ALU.mult)\
                    .then_inc(hc_ready, 1)

            for n in range(2):
                recur(0, n)
            weigh(0, 0)

            def batch(b, u, i, left):
                for n in range(STEPS):
                    if left or n + 2 < STEPS:
                        recur(b, n + 2)
                    if left or n + 1 < STEPS:
                        weigh(b, n + 1)

            each_batch(dve, 2, batch)

        @block.scalar
        def _(act):
            act.sem_inc(summed, 2 * NGB)
            act.sem_inc(y_ready, 2)
            for n in range(2):
                act.sem_inc(y_stored[n], 16)
            def decay(b, n):
                d, step = n // NS, n % NS
                if step == 0:
                    act.wait_ge(block_loaded[d % 2], 48 * (DB // 2 * b + d // 2 + 1))
                act.wait_ge(scanned, STEPS * b + n + NU - 1)
                nc.scalar.activation(psA[n % 2][:, :], dt[d % 2][:, :], ACT.Exp, scale=const.a[:, d % DB, step:step + 1])\
                    .then_inc(decay_ready, 1)

            def finish(b, d):
                act.wait_ge(y_stored[d % 2], 16 * (DB // 2 * b + d // 2 + 1))
                for half in range(2):
                    act.wait_ge(summed, 2 * NGB + 2 * (STEPS * b + (d + 1) * NS) - 1 + half)
                    cols = slice(half * HALF, (half + 1) * HALF)
                    nc.scalar.activation(y[d % 2][:, cols], psY[:, cols], ACT.Copy).then_inc(y_ready, 1)

            for n in range(AHEAD):
                decay(0, n)

            def batch(b, u, i, left):
                for n in range(STEPS):
                    if left or n + AHEAD < STEPS:
                        decay(b, n + AHEAD)
                    if n % NS == NS - 1:
                        finish(b, n // NS)

            each_batch(act, 2, batch)

        @block.tensor
        def _(pe):
            def widen(b, u, i, n):
                if n % STEPS == 0:
                    u, i = (u + n // STEPS) % 2, i + (u + n // STEPS) // 2
                    pe.wait_ge(c_loaded[u], 16 * (i + 1))
                pe.wait_ge(hc_ready, NST + STEPS * b + n)
                for half in range(2):
                    mm = nc.tensor.matmul(psC[:, half * HALF:(half + 1) * HALF], const.pick[:, n % NS, :],
                                          c[u][:, half * HALF:(half + 1) * HALF], start=True, stop=True)
                mm.then_inc(c_wide, 1)

            widen(0, 0, 0, 0)

            def batch(b, u, i, left):
                def add(n):
                    d, s = n // NS, n % NS
                    if s == 0:
                        pe.wait_ge(block_loaded[d % 2], 48 * (DB // 2 * b + d // 2 + 1))
                    pe.wait_ge(hc_ready, NST + STEPS * b + n + 1)
                    for half in range(2):
                        if s == 0:
                            pe.wait_ge(y_ready, 2 * (DB * b + d) + half + 1)
                        cols = slice(half * HALF, (half + 1) * HALF)
                        mm = nc.tensor.matmul(psY[:, cols], const.ident[:, :], hc[n % NGB][:, cols], start=s == 0,
                                              stop=s == NS - 1)
                        mm.then_inc(summed, 1)
                    if s % PIECES == 1:
                        cols = slice(s // PIECES * (T // PIECES), (s // PIECES + 1) * (T // PIECES))
                        nc.tensor.matmul(psY[:, cols], const.skip_diag[:, d, :], xc[d % 2][:, cols], start=False, stop=False)

                for n in range(STEPS):
                    if left or n + 1 < STEPS:
                        widen(b, u, i, n + 1)
                    add(n)

            each_batch(pe, 2, batch)


def hybrid_block(nc, a):
    def dram(name, shape, dt=F32):
        return nc.dram_tensor(name, shape, dt).ap()

    qk_parts = dram("qk_parts", [NB, 2, 3, D, T], BF16)
    v_ones = dram("v_ones", [NB, P, TT * NH * VW])
    max_scratch = dram("max_scratch", [2 * NG, 3, GH * HALF // P, 4, 32], BF16)
    valuesT = dram("valuesT", [NB, D, T])
    sums, recips = (dram(n, [NB, NH, T]) for n in ("sums", "recips"))
    x2 = dram("x2", [NB, T, D])
    xc, dt, dtx, yT = (dram(n, [NB, DI, T]) for n in ("xc", "dt", "dtx", "yT"))
    b_rows = dram("b_rows", [NB, NS, T])
    c_parts = dram("c_parts", [NB, 3, NS, T], BF16)

    with ExitStack() as ctx:
        const = Constants(nc, ctx)
        project_qkv(nc, const, a, a["x"], a["wq"], a["wk_b"], a["wkv_aT"], a["wv_bT"], a["turnT"], qk_parts, v_ones)
        attention(nc, const, qk_parts, v_ones, max_scratch, valuesT, sums)
        residual_ffn(nc, const, "ffn1", a["x"], valuesT, const.wo, x2, sums, recips)
        project_scan(nc, const, x2, xc, dt, dtx, b_rows, c_parts)
        scan(nc, const, xc, dt, dtx, b_rows, c_parts, yT)
        residual_ffn(nc, const, "ffn2", x2, yT, const.out_w, a["out"])


def head_turns():
    inv = (np.float32(1.0) / np.float32(10000.0) ** (np.arange(0, HD, 2, dtype=np.float32) / np.float32(HD)))
    angle = np.arange(NH, dtype=np.float32)[:, None] * inv.astype(np.float32)[None, :]
    cos, sin = np.cos(angle), np.sin(angle)
    turn = np.zeros((D, D), np.float32)
    even = np.arange(0, D, 2)
    turn[even, even] = turn[even + 1, even + 1] = cos.reshape(-1)
    turn[even, even + 1] = -sin.reshape(-1)
    turn[even + 1, even] = sin.reshape(-1)
    return np.stack([turn[c * P:(c + 1) * P, c * P:(c + 1) * P].T for c in range(CB)])


def kernel(**inputs):
    import concourse.bacc as bacc
    from concourse.bass_utils import run_bass_kernel_spmd

    w = {k.split("_", 1)[1]: np.asarray(v) for k, v in inputs.items()}
    by_block = lambda v: v.reshape(-1, P).T
    arrays = {
        "x": w["attn_a_x"], "wq": w["attn_a_wq"], "wk_b": w["attn_a_wk_b"],
        "wkv_aT": np.concatenate([w["attn_a_wk_a"].T, w["attn_a_wv_a"].T], axis=1),
        "wv_bT": w["attn_a_wv_b"].T, "woT": w["attn_a_wo"].T, "turnT": head_turns(),
        "win": w["ffn_Win"], "b_in": w["ffn_bin_"], "w1": w["ffn_W1"], "b1": w["ffn_b1"],
        "w2": w["ffn_W2"], "b2": w["ffn_b2"], "wout": w["ffn_Wout"], "bout": w["ffn_bout"],
        "x_wT": w["attn_b_x_proj_w"].T, "dt_wT": w["attn_b_dt_proj_w"].T,
        "dt_b": by_block(w["attn_b_dt_proj_b"]),
        "bc_wT": np.concatenate([w["attn_b_B_proj_w"].T, w["attn_b_C_proj_w"].T], axis=1),
        "conv_w": w["attn_b_conv_w"].reshape(DI, TAPS), "conv_b": by_block(w["attn_b_conv_b"]),
        "a_log": w["attn_b_A_log"], "d_skip": by_block(w["attn_b_D"]),
        "out_wT": w["attn_b_out_proj_w"].T,
    }
    arrays = {k: np.ascontiguousarray(v) for k, v in arrays.items()}
    nc = bacc.Bacc("TRN2", target_bir_lowering=False, num_devices=1)
    args = {k: nc.dram_tensor(k, v.shape, mybir.dt.from_np(v.dtype), kind="ExternalInput").ap()
            for k, v in arrays.items()}
    args["out"] = nc.dram_tensor("out", (NB, T, D), F32, kind="ExternalOutput").ap()
    hybrid_block(nc, args)
    return run_bass_kernel_spmd(nc, [arrays], core_ids=[0]).results[0]["out"]
```
